# Optimizing a Trainium2 kernel written in Bass

```python
import numpy as np
import jax
import jax.numpy as jnp

def _softmax(x, axis=-1):
    return jax.nn.softmax(x, axis=axis)

def _gelu(x):
    return jax.nn.gelu(x, approximate=True)

def _silu(x):
    return jax.nn.silu(x)

def _sigmoid(x):
    return jax.nn.sigmoid(x)

def _layernorm(x, axis=-1, eps=1e-05):
    m = jnp.mean(x, axis=axis, keepdims=True)
    v = jnp.var(x, axis=axis, keepdims=True)
    return (x - m) / jnp.sqrt(v + eps)

def _scatter_add(tgt, idx, src, axis=0):
    return tgt.at[idx].add(src)

def _segment_sum(src, seg, n):
    return jax.ops.segment_sum(src, seg, n)
kernel_name = 'mk_gnn_preln_d2_gnn_r32_e11369'

def setup_inputs(seed: int=0):
    np.random.seed(seed)
    _w = jnp.asarray

    def _rec_inputs():
        import jax
        import jax.numpy as jnp
        _gk = jax.random.key(seed)
        x = -6.415e-05 + 1 * jax.random.normal(jax.random.fold_in(_gk, 1), (3125, 256), jnp.float32)
        src = jax.random.randint(jax.random.fold_in(_gk, 2), (50000,), 0, 3125, jnp.int32)
        dst = jax.random.randint(jax.random.fold_in(_gk, 3), (50000,), 0, 3125, jnp.int32)
        _o = jnp.argsort(dst, stable=True)
        src = src[_o]
        dst = dst[_o]
        edge_type_8 = jax.random.randint(jax.random.fold_in(_gk, 12), (50000,), 0, 8, jnp.int32)
        return (x, src, dst, edge_type_8)
    x, src, dst, edge_type_8 = _rec_inputs()

    def _L0_gnn_setup():
        import jax, jax.numpy as jnp
        import numpy as np
        N = 1250
        E = 20000
        D = 256
        H = 8
        DH = D // H
        DFF = 4 * D
        SCALE = D ** (-0.5)
        EPS = 1e-05

        def layernorm(x, g, b):
            mu = jnp.mean(x, axis=-1, keepdims=True)
            var = jnp.mean(jnp.square(x - mu), axis=-1, keepdims=True)
            return (x - mu) * jax.lax.rsqrt(var + EPS) * g + b
        key = jax.random.key(seed)
        ks = jax.random.split(key, 12)
        inv = 1.0 / np.sqrt(D)
        invf = 1.0 / np.sqrt(DFF)
        return {'triplet_h': jax.random.normal(ks[0], (N, D), dtype=jnp.float32), 'src': jax.random.randint(ks[1], (E,), 0, N, dtype=jnp.int32), 'dst': jax.random.randint(ks[2], (E,), 0, N, dtype=jnp.int32), 'Wqkv': jax.random.uniform(ks[3], (D, 3 * D), jnp.float32, -inv, inv), 'bqkv': jax.random.uniform(ks[4], (3 * D,), jnp.float32, -inv, inv), 'ln_attn_g': jnp.ones((D,), jnp.float32), 'ln_attn_b': jnp.zeros((D,), jnp.float32), 'ln_res_g': jnp.ones((D,), jnp.float32), 'ln_res_b': jnp.zeros((D,), jnp.float32), 'W_in': jax.random.uniform(ks[5], (D, DFF), jnp.float32, -inv, inv), 'b_in': jax.random.uniform(ks[6], (DFF,), jnp.float32, -inv, inv), 'W_out': jax.random.uniform(ks[7], (DFF, D), jnp.float32, -invf, invf), 'b_out': jax.random.uniform(ks[8], (D,), jnp.float32, -invf, invf)}
    _L0_gnn_all = _L0_gnn_setup()
    _L0_gnn_in = {k: v for k, v in _L0_gnn_all.items() if k in ('Wqkv', 'bqkv', 'ln_attn_g', 'ln_attn_b', 'ln_res_g', 'ln_res_b', 'W_in', 'b_in', 'W_out', 'b_out')}
    del _L0_gnn_all

    def _L1_gnn_setup():
        import jax, jax.numpy as jnp
        import numpy as np
        N_NODES = 625
        N_EDGES = 20000
        D = 256
        N_RELS = 8
        N_BASES = 4
        LN_EPS = 1e-05
        key = jax.random.key(seed)
        ks = jax.random.split(key, 8)
        node_feats = jax.random.normal(ks[0], (N_NODES, D), dtype=jnp.float32)
        src = jax.random.randint(ks[1], (N_EDGES,), 0, N_NODES, dtype=jnp.int32)
        dst = jax.random.randint(ks[2], (N_EDGES,), 0, N_NODES, dtype=jnp.int32)
        edge_types = jax.random.randint(ks[3], (N_EDGES,), 0, N_RELS, dtype=jnp.int32)
        basis = jax.random.normal(ks[4], (N_BASES, D, D), dtype=jnp.float32) * (1.0 / np.sqrt(D))
        comp = jax.random.normal(ks[5], (N_RELS, N_BASES), dtype=jnp.float32) * (1.0 / np.sqrt(N_BASES))
        loop_w = jax.random.normal(ks[6], (D, D), dtype=jnp.float32) * (1.0 / np.sqrt(D))
        h_bias = jnp.zeros((D,), dtype=jnp.float32)
        ln_gamma = jnp.ones((D,), dtype=jnp.float32)
        ln_beta = jnp.zeros((D,), dtype=jnp.float32)
        return {'node_feats': node_feats, 'src': src, 'dst': dst, 'edge_types': edge_types, 'basis': basis, 'comp': comp, 'loop_w': loop_w, 'h_bias': h_bias, 'ln_gamma': ln_gamma, 'ln_beta': ln_beta}
    _L1_gnn_all = _L1_gnn_setup()
    _L1_gnn_in = {k: v for k, v in _L1_gnn_all.items() if k in ('basis', 'comp', 'loop_w', 'h_bias', 'ln_gamma', 'ln_beta')}
    del _L1_gnn_all
    return {'x': x, 'src': src, 'dst': dst, 'edge_type_8': edge_type_8, 'L0_gnn_Wqkv': _L0_gnn_in['Wqkv'], 'L0_gnn_bqkv': _L0_gnn_in['bqkv'], 'L0_gnn_ln_attn_g': _L0_gnn_in['ln_attn_g'], 'L0_gnn_ln_attn_b': _L0_gnn_in['ln_attn_b'], 'L0_gnn_ln_res_g': _L0_gnn_in['ln_res_g'], 'L0_gnn_ln_res_b': _L0_gnn_in['ln_res_b'], 'L0_gnn_W_in': _L0_gnn_in['W_in'], 'L0_gnn_b_in': _L0_gnn_in['b_in'], 'L0_gnn_W_out': _L0_gnn_in['W_out'], 'L0_gnn_b_out': _L0_gnn_in['b_out'], 'L1_gnn_basis': _L1_gnn_in['basis'], 'L1_gnn_comp': _L1_gnn_in['comp'], 'L1_gnn_loop_w': _L1_gnn_in['loop_w'], 'L1_gnn_h_bias': _L1_gnn_in['h_bias'], 'L1_gnn_ln_gamma': _L1_gnn_in['ln_gamma'], 'L1_gnn_ln_beta': _L1_gnn_in['ln_beta']}

def reference(x, src, dst, edge_type_8, L0_gnn_Wqkv, L0_gnn_bqkv, L0_gnn_ln_attn_g, L0_gnn_ln_attn_b, L0_gnn_ln_res_g, L0_gnn_ln_res_b, L0_gnn_W_in, L0_gnn_b_in, L0_gnn_W_out, L0_gnn_b_out, L1_gnn_basis, L1_gnn_comp, L1_gnn_loop_w, L1_gnn_h_bias, L1_gnn_ln_gamma, L1_gnn_ln_beta):
    import jax
    import jax.numpy as jnp

    def _L0_gnn_ref(triplet_h, src, dst, Wqkv, bqkv, ln_attn_g, ln_attn_b, ln_res_g, ln_res_b, W_in, b_in, W_out, b_out):
        import jax, jax.numpy as jnp
        import numpy as np
        N = 1250
        E = 20000
        D = 256
        H = 8
        DH = D // H
        DFF = 4 * D
        SCALE = D ** (-0.5)
        EPS = 1e-05

        def layernorm(x, g, b):
            mu = jnp.mean(x, axis=-1, keepdims=True)
            var = jnp.mean(jnp.square(x - mu), axis=-1, keepdims=True)
            return (x - mu) * jax.lax.rsqrt(var + EPS) * g + b
        n = triplet_h.shape[0]
        h = layernorm(triplet_h, ln_attn_g, ln_attn_b)
        qkv = (h @ Wqkv + bqkv).reshape(n, 3, H, DH)
        q = qkv[:, 0] * SCALE
        k = qkv[:, 1]
        v = qkv[:, 2]
        scores = jnp.einsum('ehd,ehd->eh', q[src], k[dst])
        m = jax.ops.segment_max(scores, dst, num_segments=n)
        e = jnp.exp(scores - m[dst])
        s = jax.ops.segment_sum(e, dst, num_segments=n)
        sa = e / s[dst]
        he = (v[src] * sa[:, :, None]).reshape(-1, D)
        agg = jax.ops.segment_sum(he, dst, num_segments=n)
        x = triplet_h + agg
        y = layernorm(x, ln_res_g, ln_res_b)
        y = jax.nn.gelu(y @ W_in + b_in, approximate=False) @ W_out + b_out
        return x + y

    def _L1_gnn_ref(node_feats, src, dst, edge_types, basis, comp, loop_w, h_bias, ln_gamma, ln_beta):
        import jax, jax.numpy as jnp
        import numpy as np
        N_NODES = 625
        N_EDGES = 20000
        D = 256
        N_RELS = 8
        N_BASES = 4
        LN_EPS = 1e-05
        W = jnp.einsum('rb,bio->rio', comp, basis)
        h_all = jnp.einsum('ni,rio->nro', node_feats, W)
        msgs = h_all[src, edge_types]
        agg = jax.ops.segment_sum(msgs, dst, num_segments=node_feats.shape[0])
        rgcn_out = agg + node_feats @ loop_w + h_bias
        h = jax.nn.gelu(rgcn_out + node_feats, approximate=False)
        mu = jnp.mean(h, axis=-1, keepdims=True)
        var = jnp.mean(jnp.square(h - mu), axis=-1, keepdims=True)
        return (h - mu) * jax.lax.rsqrt(var + LN_EPS) * ln_gamma + ln_beta
    h = jnp.maximum(_layernorm(x, axis=-1), 0.0)
    x = x + _L0_gnn_ref(h, src, dst, L0_gnn_Wqkv, L0_gnn_bqkv, L0_gnn_ln_attn_g, L0_gnn_ln_attn_b, L0_gnn_ln_res_g, L0_gnn_ln_res_b, L0_gnn_W_in, L0_gnn_b_in, L0_gnn_W_out, L0_gnn_b_out)
    h = jnp.maximum(_layernorm(x, axis=-1), 0.0)
    x = x + _L1_gnn_ref(h, src, dst, edge_type_8, L1_gnn_basis, L1_gnn_comp, L1_gnn_loop_w, L1_gnn_h_bias, L1_gnn_ln_gamma, L1_gnn_ln_beta)
    return x

_drawn_inputs = setup_inputs


def setup_inputs(seed=0):
    import zlib

    import numpy as np

    out = dict(_drawn_inputs(seed))
    spreads = {'L0_gnn_ln_attn_g': (1.0, 0.6),
     'L0_gnn_ln_attn_b': (0.0, 0.1),
     'L0_gnn_ln_res_g': (1.0, 0.6),
     'L0_gnn_ln_res_b': (0.0, 0.629),
     'L1_gnn_h_bias': (0.0, 0.495),
     'L1_gnn_ln_gamma': (1.0, 0.2),
     'L1_gnn_ln_beta': (0.0, 0.1)}
    factors = {'L0_gnn_b_in': 7.111, 'L0_gnn_b_out': 5.163}
    for name, (base, spread) in spreads.items():
        noise = np.random.default_rng([zlib.crc32(name.encode()), seed]).standard_normal(out[name].shape)
        drawn = base * np.exp(spread * noise) if base else spread * noise
        out[name] = jnp.asarray(drawn.astype(out[name].dtype))
    for name, factor in factors.items():
        out[name] = (out[name] * factor).astype(out[name].dtype)
    return out
```

```python
import concourse.bass as bass
from concourse import mybir
from contextlib import ExitStack

FP32 = mybir.dt.float32
BF16 = mybir.dt.bfloat16
I32 = mybir.dt.int32
I16 = mybir.dt.int16
ALU = mybir.AluOpType
ACT = mybir.ActivationFunctionType
AX = mybir.AxisListType
RMAX = bass.bass_isa.ReduceOp.max

N, D = 3125, 256
E = 50000
H = 8
DH = D // H
FF = 4 * D
R, NB = 8, 4
EPS = 1e-5
SCALE = float(D) ** -0.5
P = 125
NBLK = N // P
CH = 5
NCH = NBLK // CH
T = 8
PAIRS = T // 2
GE = P * T
G = E // GE
WIN = 128
NWIN = -(-N // WIN)
VMAX = G * NWIN
VTAB = G * (NWIN + 1)
AWORDS = 21380
KW = D + H
AW = D + H
NPAD = N + 3 * P
TINY = 1e-37


class Steps:

    def __init__(self, eng, sem):
        self.eng, self.sem, self.n, self.base = eng, sem, 0, 0

    def did(self, ins):
        self.n += 1
        return ins.then_inc(self.sem, 1)

    def loop(self, i, per):
        self.per, self.first, self.i = per, self.n, i
        self.base = i * per

    def end(self, trips):
        assert self.n - self.first == self.per, (self.n - self.first, self.per)
        self.base = 0
        self.n = self.first + self.per * trips

    def wait(self):
        self.eng.wait_ge(self.sem, self.base + self.n)


def program(nc, x, src, dst, edge_type, Wqkv, bqkv, ga, ba, gr, br, W_in, b_in, W_out, b_out,
            basis, comp, loop_w, h_bias, gamma, beta, out):
    qv_tab = nc.dram_tensor("qv_tab", (N, 2 * D), FP32).ap()
    k_tab = nc.dram_tensor("k_tab", (NPAD, 3 * KW), BF16).ap()
    dst16 = nc.dram_tensor("dst16", (G, GE), I16).ap()
    bounds = nc.dram_tensor("bounds", (G, 2), FP32).ap()
    att = nc.dram_tensor("att", (NPAD, AW), FP32).ap()
    rel = nc.dram_tensor("rel", (NPAD, D), FP32).ap()
    h_all = nc.dram_tensor("h_all", (N * R, D), FP32).ap()

    x_v = x.rearrange("(b p) d -> p b d", p=P)
    out_v = out.rearrange("(b p) d -> p b d", p=P)
    ctx = ExitStack()
    with ctx:
        def sb(name, shape, dt=FP32):
            return ctx.enter_context(nc.sbuf_tensor(name, shape, dt))

        def sem(name):
            return ctx.enter_context(nc.semaphore(name))

        ps = ctx.enter_context(nc.psum_tensor("ps", [128, 8, 512], FP32))
        xs = sb("xs", [P, NBLK * D])
        hs = sb("hs", [P, NBLK * D])
        srcs = sb("srcs", [P, G * T], I32)
        dsti = sb("dsti", [P, G * T], I32)
        typs = sb("typs", [P, G * T], I32)
        dstf = sb("dstf", [P, G * T])
        gof = sb("gof", [1, VTAB], I32)
        wof = sb("wof", [128, VTAB + 1], I32)
        wnode = sb("wnode", [128, VTAB])
        wcar = sb("wcar", [128, VTAB])
        wst = sb("wst", [128, VTAB])
        bnd = sb("bnd", [128, G, 2])
        flg = sb("flg", [128, 8])
        trips = sb("trips", [128, 1], I32)
        iotap = sb("iotap", [128, 1])
        iotai = sb("iotai", [128, 128], I32)
        iotaj = sb("iotaj", [128, 128])
        ident = sb("ident", [128, 128])
        identb = sb("identb", [128, 128], BF16)
        win = sb("win", [128, 2, FF])
        wout = sb("wout", [128, FF // 128, D])
        wrel = sb("wrel", [128, 2, R * D])
        wloop = sb("wloop", [128, 2, D])
        cmpb = sb("cmpb", [128, R * NB])
        cols = sb("cols", [128, 4, 2])
        bin_ = sb("bin_", [128, FF // 128])
        rowb = sb("rowb", [P, 4, D])
        st6 = sb("st6", [P, CH, 6])
        mv = sb("mv", [P, CH, 2])
        rs = sb("rs", [P, CH])
        nm = sb("nm", [P, CH])
        st6b = sb("st6b", [P, CH, 6])
        mvb = sb("mvb", [P, CH, 2])
        rsb = sb("rsb", [P, CH])
        nmb = sb("nmb", [P, CH])
        nrm = sb("nrm", [P, NBLK, 2 * H])
        nmx = sb("nmx", [128, 2])
        nmr = sb("nmr", [128, 2])
        nbias = sb("nbias", [128, 1])
        A = sb("arena", [128, AWORDS])

        def carve():
            at = [0]

            def cut(shape, dt=FP32, parts=128):
                n = 1
                for s in shape:
                    n *= s
                words = n if dt in (FP32, I32) else (n + 1) // 2
                v = A[0:parts, at[0]:at[0] + words]
                at[0] += words
                assert at[0] <= AWORDS, at[0]
                if dt != FP32:
                    v = v.bitcast(dt)
                if len(shape) == 1:
                    return v
                names = "abcd"[:len(shape)]
                pat = "p (%s) -> p %s" % (" ".join(names), " ".join(names))
                return v.rearrange(pat, **{c: s for c, s in zip(names[1:], shape[1:])})
            return cut

        s_x, s_w, s_e, s_b = sem("x_loaded"), sem("weights_loaded"), sem("edges_loaded"), sem("bounds_back")
        s_w2, s_const = sem("later_weights_loaded"), sem("constants_ready")

        with nc.Block() as block:
            cut = carve()
            hn = cut([CH, D], parts=P)
            hT = cut([CH, 2, P])
            qvst = cut([CH, 2 * D], parts=P)
            kf = cut([CH, D], parts=P)
            r1 = cut([CH, D], parts=P)
            sq = cut([CH, 2 * D], parts=P)
            kst = cut([CH, 3, KW], BF16, parts=P)
            zero = cut([2 * AW], parts=P)
            wtmp = cut([4, 2, D])
            wq = cut([2, 3 * D])
            bq = cut([3 * D], parts=P)
            base = cut([NB, 2, D])
            rows = cut([GE], I32, parts=G)
            rows16 = cut([GE], I16, parts=G)
            st_ready, h_ready = sem("st_ready"), sem("h_ready")
            var_ready, dev_ready = sem("var_ready"), sem("dev_ready")
            hn_ready, hT_in_psum, hT_ready = sem("hn_ready"), sem("hT_in_psum"), sem("hT_ready")
            qkv_ready, qkv_taken = sem("qkv_ready"), sem("qkv_taken")
            kh_ready, r1_ready, km_ready, kl_ready = (sem(n) for n in ("kh_ready", "r1_ready", "km_ready", "kl_ready"))
            sq_ready, sq_used = sem("sq_ready"), sem("sq_used")
            qv_out, k_out, stored, zeroed, z_out = (sem(n) for n in ("qv_out", "k_out", "stored", "zeroed", "z_out"))
            d16, bout = sem("dst16_stored"), sem("bounds_stored")
            cast, mm, ident_ready = sem("rows_cast"), sem("bounds_found"), sem("ident_ready")
            nmax_in, nmax_back = sem("nmax_in"), sem("nmax_back")

            @block.sync
            def _(sp):
                sp.dma_start(rows, dst.rearrange("(g e) -> g e", g=G)).then_inc(s_b, 16)
                sp.dma_start(xs[:, :].rearrange("p (b d) -> p b d", d=D), x_v).then_inc(s_x, 16)
                for tab, a in ((srcs, src), (dsti, dst), (typs, edge_type)):
                    sp.dma_start(tab[:, :].rearrange("p (g t) -> p g t", t=T),
                                 a.rearrange("(g p t) -> p g t", p=P, t=T)).then_inc(s_e, 16)
                for o, c in ((0, 0), (1, 2), (2, 1)):
                    sp.dma_start(wq[:, :, o * D:(o + 1) * D],
                                 Wqkv[:, c * D:(c + 1) * D].rearrange("(k p) n -> p k n", p=128)).then_inc(s_w, 16)
                    sp.dma_start(bq[:, o * D:(o + 1) * D],
                                 bqkv[c * D:(c + 1) * D].partition_broadcast(P)).then_inc(s_w, 16)
                for n, a in enumerate((ga, ba, gr, br)):
                    sp.dma_start(cols[:, n, :], a.rearrange("(k p) -> p k", p=128),
                                 allow_slow_non_contiguous=True).then_inc(s_w, 16)
                sp.dma_start(bin_[:, :], b_in.rearrange("(k p) -> p k", p=128),
                             allow_slow_non_contiguous=True).then_inc(s_w2, 16)
                for n, a in enumerate((b_out, h_bias, gamma, beta)):
                    sp.dma_start(rowb[:, n, :], a.partition_broadcast(P)).then_inc(s_w2, 16)
                sp.dma_start(cmpb[:, :], comp.rearrange("r b -> (r b)").partition_broadcast(128)).then_inc(s_w2, 16)
                sp.dma_start(base, basis.rearrange("b (k p) o -> p b k o", p=128)).then_inc(s_w2, 16)
                sp.dma_start(wloop[:, :, :], loop_w.rearrange("(k p) n -> p k n", p=128)).then_inc(s_w2, 16)
                sp.dma_start(win[:, :, :], W_in.rearrange("(k p) n -> p k n", p=128)).then_inc(s_w2, 16)
                sp.dma_start(wout[:, :, :], W_out.rearrange("(k p) n -> p k n", p=128)).then_inc(s_w2, 16)
                sp.wait_ge(cast, 1)
                sp.dma_start(dst16, rows16).then_inc(d16, 16)
                sp.wait_ge(mm, 2)
                sp.dma_start(bounds, flg[0:G, 0:2]).then_inc(bout, 16)
                sp.wait_ge(bout, 16)
                sp.dma_start(bnd[:, :, :], bounds.partition_broadcast(128)).then_inc(s_b, 16)
                sp.wait_ge(zeroed, 2)
                for c in range(NPAD // P // 2):
                    sp.dma_start(att[c * 2 * P:(c + 1) * 2 * P, :].rearrange("(b p) d -> p b d", p=P),
                                 zero[:, 0:2 * AW].rearrange("p (b d) -> p b d", d=AW)).then_inc(z_out, 16)
                    sp.dma_start(rel[c * 2 * P:(c + 1) * 2 * P, :].rearrange("(b p) d -> p b d", p=P),
                                 zero[:, 0:2 * D].rearrange("p (b d) -> p b d", d=D)).then_inc(z_out, 16)
                for c in range(N, NPAD, P):
                    sp.dma_start(k_tab[c:c + P, :], zero.bitcast(BF16)[:, 0:3 * KW]).then_inc(z_out, 16)
                with sp.Fori(0, NCH) as i:
                    for j in range(CH):
                        b = i * CH + j
                        sp.wait_ge(qkv_taken, 2 * b + 12)
                        sp.dma_start(qv_tab[bass.ds(b * P, P), :], qvst[:, j, :]).then_inc(qv_out, 16)
                        sp.wait_ge(kl_ready, b + 1)
                        sp.dma_start(k_tab[bass.ds(b * P, P), :], kst[:, j, :, :].rearrange("p c d -> p (c d)")).then_inc(k_out, 16)
                        sp.wait_ge(qv_out, 16 * b + 16)
                        sp.wait_ge(k_out, 16 * b + 16)
                        sp.sem_inc(stored, 1)
                sp.wait_ge(d16, 16)
                sp.wait_ge(s_b, 32)
                sp.wait_ge(z_out, 16 * (NPAD // P + (NPAD - N) // P))

            @block.gpsimd
            def _(pool):
                own = Steps(pool, sem("pre_pool"))
                nc.gpsimd.iota(wof[:, 1:VTAB + 1].rearrange("p (w g) -> p w g", g=G), pattern=[[WIN, NWIN + 1], [0, G]],
                               base=0, channel_multiplier=0).then_inc(s_const, 1)
                nc.gpsimd.iota(gof[:, :].rearrange("p (w g) -> p w g", g=G), pattern=[[0, NWIN + 1], [1, G]],
                               base=0, channel_multiplier=0).then_inc(s_const, 1)
                nc.gpsimd.iota(iotai[:, :], pattern=[[1, 128]], base=0, channel_multiplier=0).then_inc(s_const, 1)
                nc.gpsimd.iota(trips[:, :], pattern=[[0, 1]], base=0, channel_multiplier=1).then_inc(s_const, 1)
                nc.gpsimd.memset(wof[:, 0:1], 0).then_inc(s_const, 1)
                nc.gpsimd.memset(nmx[:, :], 0.0).then_inc(s_const, 1)
                nc.gpsimd.memset(zero, 0.0).then_inc(zeroed, 1)
                nc.gpsimd.memset(kst[:, :, :, D:KW], 0.0).then_inc(zeroed, 1)
                pool.wait_ge(s_w2, 16 * 10)
                for r in range(R):
                    w = wrel[:, :, r * D:(r + 1) * D]
                    own.did(nc.gpsimd.tensor_scalar(w, base[:, 0, :, :], cmpb[:, r * NB:r * NB + 1], None, ALU.mult))
                for n in range(1, NB):
                    for half in range(2):
                        relations = range(half * R // 2, (half + 1) * R // 2)
                        for r in relations:
                            own.did(nc.gpsimd.tensor_scalar(wtmp[:, r % 4, :, :], base[:, n, :, :],
                                                            cmpb[:, r * NB + n:r * NB + n + 1], None, ALU.mult))
                        own.wait()
                        for r in relations:
                            w = wrel[:, :, r * D:(r + 1) * D]
                            own.did(nc.gpsimd.tensor_tensor(w, w, wtmp[:, r % 4, :, :], ALU.add))
                        own.wait()
                own.wait()
                pool.wait_ge(nmax_in, 1)
                nc.gpsimd.partition_all_reduce(nmr[:, :], nmx[:, :], 128, RMAX).then_inc(nmax_back, 1)

            @block.scalar
            def _(act):
                act.wait_ge(s_x, 16)
                act.wait_ge(s_w, 16 * 10)
                with act.Fori(0, NCH) as i:
                    act.wait_ge(var_ready, 2 * i + 1)
                    nc.scalar.activation(rs[:, :], rs[:, :], ACT.Sqrt).then_inc(dev_ready, 1)
                    act.wait_ge(st_ready, i + 1)
                    for j in range(CH):
                        o = (i * CH + j) * D
                        nc.scalar.activation(hs[:, bass.ds(o, D)], xs[:, bass.ds(o, D)], ACT.Relu,
                                             bias=nm[:, j:j + 1], scale=rs[:, j:j + 1]).then_inc(h_ready, 1)
                    act.wait_ge(var_ready, 2 * i + 2)
                    nc.scalar.activation(rsb[:, :], rsb[:, :], ACT.Sqrt).then_inc(dev_ready, 1)
                    for j in range(CH + 2):
                        b = i * CH + j
                        if j < CH:
                            act.wait_ge(hT_in_psum, 2 * b + 2)
                            for k in range(2):
                                nc.scalar.activation(hT[:, j, k, :], ps[:, j % 2, k * P:k * P + P], ACT.Identity,
                                                     bias=cols[:, 1, k:k + 1], scale=cols[:, 0, k:k + 1]).then_inc(hT_ready, 1)
                        if 1 <= j <= CH:
                            act.wait_ge(qkv_taken, 2 * b + 10)
                            nc.scalar.activation(kst[:, j - 1, 0, 0:D], kf[:, j - 1, :], ACT.Copy).then_inc(kh_ready, 1)
                            nc.scalar.activation(sq[:, j - 1, 0:D], qvst[:, j - 1, 0:D], ACT.Square).then_inc(sq_ready, 1)
                            nc.scalar.activation(sq[:, j - 1, D:2 * D], kf[:, j - 1, :], ACT.Square).then_inc(sq_ready, 1)
                        if j >= 2:
                            act.wait_ge(r1_ready, b - 1)
                            nc.scalar.activation(kst[:, j - 2, 1, 0:D], r1[:, j - 2, :], ACT.Copy).then_inc(km_ready, 1)
                act.wait_ge(var_ready, 2 * NCH + 1)
                nc.scalar.activation(nbias[:, :], nbias[:, :], ACT.Sqrt, scale=SCALE * SCALE).then_inc(dev_ready, 1)

            @block.tensor
            def _(pe):
                pe.wait_ge(s_w, 16 * 10)
                pe.wait_ge(ident_ready, 1)

                def turn(b, j):
                    pe.wait_ge(hn_ready, b + 1)
                    for k in range(2):
                        nc.tensor.transpose(ps[:, j % 2, k * P:k * P + P], hn[:, j, k * 128:k * 128 + 128],
                                            ident[0:P, 0:P]).then_inc(hT_in_psum, 1)

                def project(b, j):
                    pe.wait_ge(hT_ready, 2 * b + 2)
                    pe.wait_ge(qkv_taken, 2 * b + (10 if j == 0 else 6 if j == 1 else 8))
                    for c, bank, n in ((0, 2 + j % 2, 2 * D), (2 * D, 4 + j % 2, D)):
                        for k in range(2):
                            last = nc.tensor.matmul(ps[0:P, bank, 0:n], hT[:, j, k, :], wq[:, k, c:c + n],
                                                    start=(k == 0), stop=(k == 1))
                    last.then_inc(qkv_ready, 1)

                with pe.Fori(0, NCH) as i:
                    for j in range(CH + 1):
                        if j < CH:
                            turn(i * CH + j, j)
                        if j >= 1:
                            project(i * CH + j - 1, j - 1)

            @block.vector
            def _(dve):
                own = Steps(dve, sem("pre_dve"))
                dve.wait_ge(s_b, 16)
                nc.vector.tensor_copy(rows16, rows).then_inc(cast, 1)
                nc.vector.tensor_reduce(flg[0:G, 0:1], rows, AX.X, ALU.min).then_inc(mm, 1)
                nc.vector.tensor_reduce(flg[0:G, 1:2], rows, AX.X, ALU.max).then_inc(mm, 1)
                dve.sem_inc(qkv_taken, 10)
                dve.sem_inc(stored, CH)
                dve.wait_ge(s_const, 6)
                own.did(nc.vector.tensor_copy(iotaj[:, :], iotai[:, :]))
                own.did(nc.vector.tensor_copy(iotap[:, :], trips[:, :]))
                own.wait()
                own.did(nc.vector.tensor_scalar(ident[:, :], iotaj[:, :], iotap[:, :], None, ALU.is_equal))
                own.did(nc.vector.tensor_scalar(identb[:, :], iotaj[:, :], iotap[:, :], None, ALU.is_equal))
                own.wait()
                dve.sem_inc(ident_ready, 1)
                dve.wait_ge(s_x, 16)
                dve.wait_ge(s_w, 16 * 10)
                dve.wait_ge(zeroed, 2)
                with dve.Fori(0, NCH) as i:
                    own.loop(i, 4 * CH + 2)

                    def stats(tile, st, m, r, n, done):
                        for j in range(CH):
                            if done is not None:
                                dve.wait_ge(done, i * CH + j + 1)
                            own.did(nc.vector.bn_stats(st[:, j, :], tile(j)))
                        own.wait()
                        dve.nop(nofuse=True)
                        for j in range(CH):
                            own.did(nc.vector.bn_aggr(m[:, j, :], st[:, j, :]))
                        own.wait()
                        nc.vector.tensor_scalar(r[:, :], m[:, :, 1], EPS, None, ALU.add).then_inc(var_ready, 1)
                        dve.wait_ge(dev_ready, 2 * i + n + 1)
                        own.did(nc.vector.reciprocal(r[:, :], r[:, :]))
                        own.wait()

                    def x_(j):
                        return xs[:, bass.ds((i * CH + j) * D, D)]

                    def h_(j):
                        return hs[:, bass.ds((i * CH + j) * D, D)]

                    stats(x_, st6, mv, rs, 0, None)
                    nc.vector.scalar_tensor_tensor(out=nm[:, :], in0=mv[:, :, 0], scalar=-1.0, in1=rs[:, :],
                                                   op0=ALU.mult, op1=ALU.mult).then_inc(st_ready, 1)
                    stats(h_, st6b, mvb, rsb, 1, h_ready)
                    for j in range(CH):
                        nc.vector.tensor_scalar(hn[:, j, :], h_(j), mvb[:, j, 0:1], rsb[:, j:j + 1],
                                                ALU.subtract, ALU.mult).then_inc(hn_ready, 1)
                    for j in range(CH + 3):
                        b = i * CH + j
                        if j < CH:
                            dve.wait_ge(qkv_ready, b + 1)
                            dve.wait_ge(stored, b + 1)
                            nc.vector.tensor_tensor(qvst[:, j, :], ps[0:P, 2 + j % 2, :], bq[:, 0:2 * D],
                                                    ALU.add).then_inc(qkv_taken, 1)
                            nc.vector.tensor_tensor(kf[:, j, :], ps[0:P, 4 + j % 2, 0:D], bq[:, 2 * D:3 * D],
                                                    ALU.add).then_inc(qkv_taken, 1)
                        if 1 <= j <= CH:
                            dve.wait_ge(kh_ready, b)
                            nc.vector.tensor_tensor(r1[:, j - 1, :], kf[:, j - 1, :], kst[:, j - 1, 0, 0:D],
                                                    ALU.subtract).then_inc(r1_ready, 1)
                            dve.wait_ge(sq_ready, 2 * b)
                            nc.vector.tensor_reduce(nrm[:, bass.ds(b - 1, 1), :].rearrange("p o h -> p (o h)"),
                                                    sq[:, j - 1, :].rearrange("p (h d) -> p h d", d=DH),
                                                    AX.X, ALU.add).then_inc(sq_used, 1)
                        if 3 <= j:
                            dve.wait_ge(km_ready, b - 2)
                            nc.vector.tensor_tensor(kst[:, j - 3, 2, 0:D], r1[:, j - 3, :], kst[:, j - 3, 1, 0:D],
                                                    ALU.subtract).then_inc(kl_ready, 1)
                own.end(NCH)
                dve.wait_ge(s_e, 48)
                own.did(nc.vector.tensor_copy(dstf[:, :], dsti[:, :]))
                own.did(nc.vector.scalar_tensor_tensor(out=typs[:, :], in0=srcs[:, :], scalar=float(R), in1=typs[:, :],
                                                       op0=ALU.mult, op1=ALU.add))
                dve.wait_ge(s_b, 32)
                own.did(nc.vector.tensor_tensor(wst[:, 0:G], bnd[:, :, 1], bnd[:, :, 0], ALU.subtract))
                own.did(nc.vector.tensor_tensor(wst[:, G:2 * G - 1], bnd[:, 1:G, 0], bnd[:, 0:G - 1, 0], ALU.subtract))
                own.wait()
                own.did(nc.vector.tensor_reduce(flg[:, 2:3], wst[:, 0:G], AX.X, ALU.max))
                own.did(nc.vector.tensor_reduce(flg[:, 3:4], wst[:, G:2 * G - 1], AX.X, ALU.min))
                own.wait()
                own.did(nc.vector.tensor_scalar(flg[:, 4:5], flg[:, 2:3], float(WIN - 1), None, ALU.is_le))
                own.did(nc.vector.tensor_scalar(flg[:, 5:6], flg[:, 3:4], 0.0, None, ALU.is_ge))
                own.wait()
                own.did(nc.vector.tensor_tensor(flg[:, 6:7], flg[:, 4:5], flg[:, 5:6], ALU.mult))
                own.wait()
                own.did(nc.vector.tensor_scalar(trips[:, :], flg[:, 6:7], float((G - VMAX) // 2), float(VMAX // 2),
                                                ALU.mult, ALU.add))
                own.did(nc.vector.tensor_scalar(wof[:, 1:G + 1], bnd[:, :, 0], flg[:, 6:7], None, ALU.mult))
                own.wait()
                own.did(nc.vector.tensor_copy(wst[:, :], wof[:, 1:VTAB + 1]))
                own.did(nc.vector.tensor_tensor(wcar[:, :], wof[:, 0:VTAB], wof[:, 1:VTAB + 1], ALU.subtract))
                own.wait()
                own.did(nc.vector.tensor_scalar(wnode[:, :], wst[:, :], iotap[:, :], None, ALU.add))
                own.did(nc.vector.tensor_scalar(wcar[:, :], wcar[:, :], iotap[:, :], None, ALU.add))
                own.wait()
                dve.wait_ge(sq_used, NBLK)
                for n in range(2):
                    own.did(nc.vector.tensor_reduce(nmx[0:P, n:n + 1], nrm[:, :, n * H:(n + 1) * H], AX.XY, ALU.max))
                own.wait()
                dve.sem_inc(nmax_in, 1)
                dve.wait_ge(nmax_back, 1)
                nc.vector.tensor_tensor(nbias[:, :], nmr[:, 0:1], nmr[:, 1:2], ALU.mult).then_inc(var_ready, 1)
                dve.wait_ge(dev_ready, 2 * NCH + 1)
                own.did(nc.vector.tensor_scalar(nbias[:, :], nbias[:, :], -1.0, None, ALU.mult))
                own.wait()



        with nc.Block() as block:
            cut = carve()
            rowbuf = cut([2 * T, 2 * D + H], parts=P)
            ind = cut([2, T, WIN], parts=P)
            indT = cut([2, GE], BF16)
            kwin = cut([2, 3 * KW], BF16)
            drow = cut([2, GE], I16)
            car = cut([2, WIN])
            osum = cut([2, AW])
            sco = cut([T, H], parts=P)
            idx = cut([2, T], I32, parts=P)
            k_ready, k_used = sem("key_rows_ready"), sem("scores_ready")
            kwin_in = [sem(f"key_window_in{u}") for u in range(2)]
            drow_in = [sem(f"dst_row_in{u}") for u in range(2)]
            row_in = [sem(f"row_in{t}") for t in range(2 * T)]
            indT_ready, car_ready = sem("indT_ready"), sem("car_ready")
            turn_ready, ind_ready = sem("turn_ready"), sem("ind_ready")
            exp_done, w_ready, agg_done = sem("exp_done"), sem("weighted_ready"), sem("summed")
            win_done, osum_ready = sem("window_done"), sem("osum_ready")
            att_out, att_stored, idx_ready = sem("att_out"), sem("att_stored"), sem("idx_ready")
            zeros = sem("zeros_ready")

            def seen(v, j, ahead):
                return PAIRS * v + j + 1 + ahead

            SCORES_AHEAD = 4
            EXP_AHEAD = 4
            WEIGHTED_AHEAD = 4
            SUMMED_AHEAD = 8
            KEYS_AHEAD = 8
            IND_AHEAD = 4

            def trip_count(eng):
                return eng.value_load(trips[0:1, 0:1], min_val=G // 2, max_val=VMAX // 2)

            @block.sync
            def _(sp):
                nt = trip_count(sp)
                sp.sem_inc(att_stored, 1)
                sp.wait_ge(zeros, 1)

                def store(v, u):
                    sp.wait_ge(osum_ready, v + 5)
                    sp.nop(nofuse=True)
                    sp.wait_ge(att_out, 16 * (v + 2))
                    sp.nop(nofuse=True)
                    sp.sem_inc(att_stored, 1)
                    w = sp.value_load(wof[0:1, bass.ds(v + 1, 1)], min_val=0, max_val=NWIN * WIN)
                    sp.dma_start(att[bass.ds(w, WIN), :], osum[:, u, :]).then_inc(att_out, 16)

                sp.dma_start(att[0:WIN, :], osum[:, 0, :]).then_inc(att_out, 16)
                def load(v, u):
                        w = sp.value_load(wof[0:1, bass.ds(v + 1, 1)], min_val=0, max_val=NWIN * WIN)
                        g = sp.value_load(gof[0:1, bass.ds(v, 1)], min_val=0, max_val=G - 1)
                        sp.wait_ge(k_ready, seen(v - 2, 3, KEYS_AHEAD))
                        sp.nop(nofuse=True)
                        sp.dma_start(kwin[:, u, :], k_tab[bass.ds(w, WIN), :]).then_inc(kwin_in[u], 16)
                        sp.wait_ge(indT_ready, v + 1)
                        sp.nop(nofuse=True)
                        sp.dma_start(drow[:, u, :], dst16[bass.ds(g, 1), :].rearrange("o e -> (o e)").partition_broadcast(128)
                                     ).then_inc(drow_in[u], 16)

                load(0, 0)
                with sp.Fori(0, nt) as i:
                    for u in range(2):
                        v = 2 * i + u
                        load(v + 1, 1 - u)
                        store(v - 1, 1 - u)
                store(2 * nt - 1, 1)
                sp.wait_ge(drow_in[0], 16 * nt + 16)
                sp.nop(nofuse=True)
                sp.wait_ge(att_out, 32 * nt + 32)
                sp.nop(nofuse=True)

            @block.gpsimd
            def _(pool):
                nt = trip_count(pool)
                pool.wait_ge(zeros, 1)

                def indices(v, u):
                    g = pool.value_load(gof[0:1, bass.ds(v, 1)], min_val=0, max_val=G - 1)
                    pool.wait_ge(k_used, seen(v - 2, 3, SCORES_AHEAD))
                    nc.gpsimd.tensor_copy(idx[:, u, :], srcs[:, bass.ds(g * T, T)]).then_inc(idx_ready, 1)

                indices(0, 0)
                with pool.Fori(0, nt) as i:
                    for u in range(2):
                        v = 2 * i + u
                        pool.wait_ge(idx_ready, v + 1)
                        for t in range(T):
                            if t == 6:
                                indices(v + 1, 1 - u)
                            if t % 2 == 0:
                                pool.wait_ge(agg_done, seen(v - 2, t // 2, SUMMED_AHEAD))
                                pool.nop(nofuse=True)
                            pool.indirect_dma_start(
                                out=rowbuf[:, u * T + t, 0:2 * D], out_offset=None, in_=qv_tab,
                                in_offset=bass.IndirectOffsetOnAxis(ap=idx[:, u, t:t + 1], axis=0)).then_inc(row_in[u * T + t], 16)

            @block.scalar
            def _(act):
                nt = trip_count(act)
                act.sem_inc(exp_done, EXP_AHEAD)
                act.sem_inc(ind_ready, IND_AHEAD)
                act.sem_inc(osum_ready, 3)
                act.wait_ge(zeros, 1)

                def take(v, u):
                    act.wait_ge(win_done, v + 2)
                    act.wait_ge(att_stored, v + 2)
                    nc.scalar.activation(osum[:, u, :], ps[:, 6 + u, 0:AW], ACT.Copy).then_inc(osum_ready, 1)

                def indicators(v, u):
                    for half in range(2):
                        act.wait_ge(turn_ready, 2 * v + half + 1)
                        if half == 0:
                            act.wait_ge(agg_done, seen(v - 2, 3, SUMMED_AHEAD))
                        nc.scalar.activation(ind[:, u, 4 * half:4 * half + 4, :],
                                             ps[0:P, 4 + half, 0:4 * WIN // 2].bitcast(BF16).rearrange("p (t w) -> p t w", w=WIN),
                                             ACT.Copy).then_inc(ind_ready, 1)

                indicators(0, 0)
                with act.Fori(0, nt) as i:
                    for u in range(2):
                        v = 2 * i + u

                        def weights(j):
                            act.wait_ge(k_used, seen(v, j, SCORES_AHEAD))
                            nc.scalar.activation(rowbuf[:, u * T + 2 * j:u * T + 2 * j + 2, 2 * D:2 * D + H], sco[:, 2 * j:2 * j + 2, :], ACT.Exp,
                                                 bias=nbias[0:P, :], scale=SCALE).then_inc(exp_done, 1)

                        for j in range(PAIRS):
                            weights(j)
                            if j == 1:
                                take(v - 1, 1 - u)
                            if j == 2:
                                indicators(v + 1, 1 - u)
                take(2 * nt - 1, 1)

            @block.tensor
            def _(pe):
                nt = trip_count(pe)
                pe.sem_inc(k_ready, KEYS_AHEAD - 1)
                pe.sem_inc(agg_done, SUMMED_AHEAD - PAIRS)
                pe.wait_ge(zeros, 1)

                def turn(v, u, half):
                    pe.wait_ge(ind_ready, 2 * v + half + 1 + IND_AHEAD - 2)
                    tiles = indT[:, u, :].rearrange("p (e t) -> p t e", t=T)
                    for t in range(4):
                        last = nc.tensor.transpose(ps[0:P, 4 + half, t * WIN // 2:(t + 1) * WIN // 2].bitcast(BF16),
                                                   tiles[:, 4 * half + t, :], identb[:, :])
                    last.then_inc(turn_ready, 1)

                for t in (2, 3):
                    last = nc.tensor.matmul(ps[0:P, t, 0:KW], indT[:, 1, 0:P], kwin[:, 1, 0:KW], start=True, stop=True)
                last.then_inc(k_ready, 1)

                def keys(n, v, u, j):
                    if j == 0:
                        pe.wait_ge(kwin_in[u], 16 * n + 16)
                    pe.wait_ge(k_used, seen(v, j - 2, SCORES_AHEAD))
                    tiles = indT[:, u, :].rearrange("p (e t) -> p t e", t=T)
                    for t in (2 * j, 2 * j + 1):
                        for c in range(3):
                            last = nc.tensor.matmul(ps[0:P, t % 4, 0:KW], tiles[:, t, :], kwin[:, u, c * KW:(c + 1) * KW],
                                                    start=(c == 0), stop=(c == 2))
                    last.then_inc(k_ready, 1)

                def add_up(v, u, j):
                    pe.wait_ge(w_ready, seen(v, j, WEIGHTED_AHEAD))
                    pe.wait_ge(ind_ready, 2 * v + j // 2 + 1 + IND_AHEAD)
                    if j == 0:
                        pe.wait_ge(osum_ready, v + 3)
                    for t in (2 * j, 2 * j + 1):
                        last = nc.tensor.matmul(ps[:, 6 + u, 0:AW], ind[:, u, t, :], rowbuf[:, u * T + t, D:2 * D + H],
                                                start=(t == 0), stop=False)
                    last.then_inc(agg_done, 1)

                def carry(v, u):
                    pe.wait_ge(osum_ready, v + 4)
                    pe.wait_ge(car_ready, v + 2)
                    nc.tensor.matmul(ps[:, 6 + u, 0:AW], car[:, u, :], osum[:, 1 - u, :], start=False, stop=True).then_inc(win_done, 1)

                def across(n, v, u):
                    pe.wait_ge(indT_ready, v + 3)
                    turn(v, u, 0)
                    turn(v, u, 1)
                    keys(n, v, u, 0)
                    add_up(v - 1, 1 - u, 2)
                    keys(n, v, u, 1)
                    add_up(v - 1, 1 - u, 3)
                    carry(v - 1, 1 - u)

                add_up(-1, 1, 0)
                add_up(-1, 1, 1)
                across(0, 0, 0)
                with pe.Fori(0, nt) as i:
                    for u in range(2):
                        v = 2 * i + u
                        keys(i, v, u, 2)
                        add_up(v, u, 0)
                        keys(i, v, u, 3)
                        add_up(v, u, 1)
                        across(i + u, v + 1, 1 - u)

            @block.vector
            def _(dve):
                nt = trip_count(dve)
                own = Steps(dve, sem("edge_dve"))
                dve.sem_inc(k_used, SCORES_AHEAD - 1)
                dve.sem_inc(w_ready, WEIGHTED_AHEAD - 1)
                dve.sem_inc(indT_ready, 2)
                own.did(nc.vector.memset(rowbuf[:, T:2 * T, :], 0.0))
                own.did(nc.vector.memset(ind[:, 1, :, :], 0.0))
                own.did(nc.vector.memset(osum, 0.0))
                own.did(nc.vector.memset(sco, 0.0))
                own.did(nc.vector.memset(indT[:, 1, :], 0.0))
                own.did(nc.vector.memset(kwin[:, 1, :], 0.0))
                nc.vector.memset(car[:, 1, :], 0.0).then_inc(car_ready, 1)
                own.wait()
                dve.sem_inc(zeros, 1)
                def to_window(n, v, u):
                    dve.wait_ge(drow_in[u], 16 * n + 16)
                    dve.wait_ge(k_ready, seen(v - 2, 3, KEYS_AHEAD))
                    nc.vector.tensor_scalar(indT[:, u, :], drow[:, u, :], wnode[:, bass.ds(v, 1)], None,
                                            ALU.is_equal).then_inc(indT_ready, 1)

                def shift(j, reduced):
                    bank = 2 * (j % 2)
                    dve.wait_ge(own.sem, reduced)
                    nc.vector.tensor_tensor(sco[:, 2 * j:2 * j + 2, :], sco[:, 2 * j:2 * j + 2, :],
                                            ps[0:P, bank:bank + 2, D:KW], ALU.subtract).then_inc(k_used, 1)

                dve.wait_ge(k_ready, seen(-1, 3, KEYS_AHEAD))
                to_window(0, 0, 0)
                with dve.Fori(0, nt) as i:
                    own.loop(i, 2 * 2 * PAIRS)
                    for u in range(2):
                        v = 2 * i + u

                        def weigh(v, u, j):
                            dve.wait_ge(exp_done, seen(v, j, EXP_AHEAD))
                            b = rowbuf[:, u * T + 2 * j:u * T + 2 * j + 2, :]
                            vals = b[:, :, D:2 * D].rearrange("p t (h d) -> p t h d", d=DH)
                            nc.vector.tensor_tensor(vals, vals, b[:, :, 2 * D:2 * D + H].unsqueeze(3).broadcast_to([P, 2, H, DH]),
                                                    ALU.mult).then_inc(w_ready, 1)

                        for j in range(PAIRS):
                            b = rowbuf[:, u * T + 2 * j:u * T + 2 * j + 2, :]
                            for t in (2 * j, 2 * j + 1):
                                dve.wait_ge(row_in[u * T + t], 16 * i + 16)
                            dve.wait_ge(k_ready, seen(v, j, KEYS_AHEAD))
                            bank = 2 * (j % 2)
                            reduced = own.base + own.n
                            own.did(nc.vector.tensor_tensor(b[:, :, 0:D], b[:, :, 0:D], ps[0:P, bank:bank + 2, 0:D], ALU.mult))
                            shift((j - 1) % PAIRS, reduced)
                            if j == 0:
                                nc.vector.tensor_scalar(car[:, u, :], iotaj[:, :], wcar[:, bass.ds(v, 1)], None,
                                                        ALU.is_equal).then_inc(car_ready, 1)
                            own.wait()
                            own.did(nc.vector.tensor_reduce(sco[:, 2 * j:2 * j + 2, :],
                                                            b[:, :, 0:D].rearrange("p t (h d) -> p t h d", d=DH), AX.X, ALU.add))
                            if j == 0:
                                weigh(v - 1, 1 - u, 3)
                            else:
                                weigh(v, u, j - 1)
                            if j == 1:
                                to_window(i + u, v + 1, 1 - u)
                own.end(nt)
                shift(PAIRS - 1, own.n)
                dve.wait_ge(exp_done, seen(2 * nt - 1, 3, EXP_AHEAD))
                b = rowbuf[:, 2 * T - 2:2 * T, :]
                vals = b[:, :, D:2 * D].rearrange("p t (h d) -> p t h d", d=DH)
                nc.vector.tensor_tensor(vals, vals, b[:, :, 2 * D:2 * D + H].unsqueeze(3).broadcast_to([P, 2, H, DH]),
                                        ALU.mult).then_inc(w_ready, 1)

        with nc.Block() as block:
            cut = carve()
            sums = cut([NBLK, AW], parts=P)
            yn = cut([CH, D], parts=P)
            yT = cut([2, CH * P])
            gT = cut([FF // 128, CH * P])
            h1T = cut([2, 2, P])
            h1s = cut([CH, D], parts=P)
            msg = cut([2, R * D], parts=P)
            rec = cut([CH, H], parts=P)
            vv = cut([6, CH], parts=P)
            att_in = sem("att_in")
            x1_ready, x_ready, yn_ready = sem("x1_ready"), sem("x_ready"), sem("yn_ready")
            t_psum, yT_ready = sem("turned"), sem("yT_ready")
            hid_psum, hid_ready = sem("hidden_psum"), sem("hidden_ready")
            ff_psum, ff_taken = sem("ff_psum"), sem("ff_taken")
            st_ready, h1_ready = sem("x2_statistics"), sem("h1_ready")
            h1t_psum, h1T_ready = sem("h1_turned"), sem("h1T_ready")
            msg_psum, msg_a, msg_v = sem("msg_psum"), sem("msg_by_act"), sem("msg_by_dve")
            loop_psum, loop_taken = sem("loop_psum"), sem("loop_taken")
            msg_out, msg_stored = sem("msg_out"), sem("msg_stored")
            PARTS = ((0, 3 * P), (3 * P, 2 * P))
            NPROD = FF // 128 * len(PARTS)
            hall_v = h_all.rearrange("(n r) d -> n (r d)", r=R)

            def rsqrt(own, var, r, t):
                own.did(nc.vector.tensor_scalar(t.bitcast(I32), var.bitcast(I32), 1, None, ALU.logical_shift_right))
                own.wait()
                own.did(nc.vector.tensor_scalar(r.bitcast(I32), t.bitcast(I32), -1.0, float(0x5F3759DF), ALU.mult, ALU.add))
                own.wait()
                for _ in range(3):
                    own.did(nc.vector.tensor_tensor(t, r, r, ALU.mult))
                    own.wait()
                    own.did(nc.vector.tensor_tensor(t, t, var, ALU.mult))
                    own.wait()
                    own.did(nc.vector.tensor_scalar(t, t, -0.5, 1.5, ALU.mult, ALU.add))
                    own.wait()
                    own.did(nc.vector.tensor_tensor(r, r, t, ALU.mult))
                    own.wait()
            MID_STEPS = 2 + CH + 2 * CH + 1 + 14 + CH * (3 + 14)


            @block.sync
            def _(sp):
                for c in range(NCH):
                    sp.dma_start(sums[:, c * CH:(c + 1) * CH, :],
                                 att[c * CH * P:(c + 1) * CH * P, :].rearrange("(b p) d -> p b d", p=P)).then_inc(att_in, 16)
                    sp.wait_ge(att_in, 16 * c + 16)
                with sp.Fori(0, NCH) as i:
                    for j in range(CH):
                        b = i * CH + j
                        sp.wait_ge(msg_a, 2 * b + 4)
                        sp.nop(nofuse=True)
                        sp.wait_ge(msg_v, 2 * b + 4)
                        sp.nop(nofuse=True)
                        sp.dma_start(hall_v[bass.ds(b * P, P), :], msg[:, j % 2, :]).then_inc(msg_out, 16)
                        sp.wait_ge(msg_out, 16 * b + 16)
                        sp.nop(nofuse=True)
                        sp.sem_inc(msg_stored, 1)

            @block.gpsimd
            def _(pool):
                own = Steps(pool, sem("mid_pool"))
                with pool.Fori(0, NCH) as i:
                    own.loop(i, CH)
                    for j in range(CH):
                        x_b = xs[:, bass.ds((i * CH + j) * D, D)]
                        pool.wait_ge(x1_ready, i * CH + j + 1)
                        pool.nop(nofuse=True)
                        own.did(nc.gpsimd.tensor_tensor(x_b, x_b, hs[:, bass.ds((i * CH + j) * D, D)], ALU.add))
                        own.wait()
                        pool.nop(nofuse=True)
                        nc.gpsimd.tensor_tensor(x_b, x_b, rowb[:, 0, :], ALU.add).then_inc(x_ready, 1)
                    for j in range(CH):
                        h_b = hs[:, bass.ds((i * CH + j) * D, D)]
                        pool.wait_ge(loop_taken, i * CH + j + 3)
                        pool.nop(nofuse=True)
                        nc.gpsimd.tensor_tensor(h_b, h_b, rowb[:, 1, :], ALU.add)

            @block.scalar
            def _(act):
                act.sem_inc(hid_ready, 2)
                act.sem_inc(msg_a, 2)
                with act.Fori(0, NCH) as i:
                    for j in range(CH):
                        act.wait_ge(t_psum, 2 * (i * CH + j) + 2)
                        for k in range(2):
                            nc.scalar.activation(yT[:, k, j * P:(j + 1) * P], ps[:, j % 2, k * P:k * P + P], ACT.Identity,
                                                 bias=cols[:, 3, k:k + 1], scale=cols[:, 2, k:k + 1]).then_inc(yT_ready, 1)
                    for f in range(FF // 128):
                        for m, (c, n) in enumerate(PARTS):
                            act.wait_ge(hid_psum, i * NPROD + 2 * f + m + 1)
                            nc.scalar.activation(gT[:, f, c:c + n], ps[:, 2 + m, 0:n], ACT.Gelu,
                                                 bias=bin_[:, f:f + 1]).then_inc(hid_ready, 1)
                    for j in range(CH):
                        b = i * CH + j
                        o = b * D
                        act.wait_ge(st_ready, b + 1)
                        nc.scalar.activation(h1s[:, j, :], xs[:, bass.ds(o, D)], ACT.Relu,
                                             bias=nmb[:, j:j + 1], scale=rsb[:, j:j + 1]).then_inc(h1_ready, 1)
                        act.wait_ge(h1t_psum, 2 * b + 2)
                        nc.scalar.activation(h1T[:, j % 2, :, :], ps[:, j % 2, 0:2 * P].rearrange("p (k n) -> p k n", k=2),
                                             ACT.Copy).then_inc(h1T_ready, 1)
                        act.wait_ge(msg_stored, b + (2 if j == 0 else 1))
                        for c in range(2):
                            act.wait_ge(msg_psum, 4 * b + c + 1)
                            nc.scalar.activation(msg[:, j % 2, c * 512:(c + 1) * 512], ps[0:P, 2 + c, :],
                                                 ACT.Copy).then_inc(msg_a, 1)

            @block.tensor
            def _(pe):
                with pe.Fori(0, NCH) as i:
                    pe.wait_ge(loop_taken, CH * i + 2)
                    for j in range(CH):
                        pe.wait_ge(yn_ready, i * CH + j + 1)
                        if j >= 2:
                            pe.wait_ge(yT_ready, 2 * (i * CH + j) - 2)
                        for k in range(2):
                            nc.tensor.transpose(ps[:, j % 2, k * P:k * P + P], yn[:, j, k * 128:k * 128 + 128],
                                                ident[0:P, 0:P]).then_inc(t_psum, 1)
                    pe.wait_ge(yT_ready, 2 * CH * i + 2 * CH)
                    pe.wait_ge(msg_a, 2 * CH * i + 2)
                    for f in range(FF // 128):
                        for m, (c, n) in enumerate(PARTS):
                            pe.wait_ge(hid_ready, i * NPROD + 2 * f + m + 1)
                            for k in range(2):
                                last = nc.tensor.matmul(ps[:, 2 + m, 0:n], win[:, k, f * 128:(f + 1) * 128], yT[:, k, c:c + n],
                                                        start=(k == 0), stop=(k == 1))
                            last.then_inc(hid_psum, 1)

                    def feed(j):
                        b = i * CH + j
                        pe.wait_ge(hid_ready, i * NPROD + NPROD + 2)
                        pe.wait_ge(ff_taken, b + (2 if j == 0 else 1))
                        for f in range(FF // 128):
                            last = nc.tensor.matmul(ps[0:P, 4 + j % 2, 0:D], gT[:, f, j * P:(j + 1) * P], wout[:, f, :],
                                                    start=(f == 0), stop=(f == FF // 128 - 1))
                        last.then_inc(ff_psum, 1)

                    def messages(j):
                        b = i * CH + j
                        pe.wait_ge(h1_ready, b + 1)
                        pe.wait_ge(loop_taken, b + (2 if j == 0 else 1))
                        for k in range(2):
                            nc.tensor.transpose(ps[:, j % 2, k * P:k * P + P], h1s[:, j, k * 128:k * 128 + 128],
                                                ident[0:P, 0:P]).then_inc(h1t_psum, 1)
                        pe.wait_ge(h1T_ready, b + 1)
                        for k in range(2):
                            last = nc.tensor.matmul(ps[0:P, j % 2, D:2 * D], h1T[:, j % 2, k, :], wloop[:, k, :],
                                                    start=(k == 0), stop=(k == 1))
                        last.then_inc(loop_psum, 1)
                        for c in range(4):
                            pe.wait_ge(msg_a if c < 2 else msg_v, 2 * b + c % 2 + 1)
                            for k in range(2):
                                last = nc.tensor.matmul(ps[0:P, (2, 3, 6, 7)[c], :], h1T[:, j % 2, k, :],
                                                        wrel[:, k, c * 512:(c + 1) * 512], start=(k == 0), stop=(k == 1))
                            last.then_inc(msg_psum, 1)

                    for j in range(CH + 1):
                        if j < CH:
                            feed(j)
                        if j >= 1:
                            messages(j - 1)

            @block.vector
            def _(dve):
                own = Steps(dve, sem("mid_dve"))
                dve.sem_inc(ff_taken, 2)
                dve.sem_inc(loop_taken, 2)
                dve.sem_inc(msg_v, 2)
                dve.sem_inc(msg_stored, 2)
                with dve.Fori(0, NCH) as i:
                    own.loop(i, MID_STEPS)
                    dve.wait_ge(att_in, 16 * i + 16)
                    s_c = sums[:, bass.ds(i * CH, CH), :]
                    own.did(nc.vector.tensor_scalar(rec, s_c[:, :, D:AW], TINY, None, ALU.max))
                    own.wait()
                    own.did(nc.vector.reciprocal(rec, rec))
                    own.wait()
                    for j in range(CH):
                        s_j = sums[:, bass.ds(i * CH + j, 1), 0:D].rearrange("p o (h d) -> p (o h) d", d=DH)
                        own.did(nc.vector.tensor_tensor(s_j, s_j, rec[:, j, :].unsqueeze(2).broadcast_to([P, H, DH]), ALU.mult))
                    own.wait()
                    for j in range(CH):
                        s_j = sums[:, bass.ds(i * CH + j, 1), 0:D].rearrange("p o d -> p (o d)")
                        h_j = hs[:, bass.ds((i * CH + j) * D, D)]
                        nc.vector.tensor_tensor(h_j, h_j, s_j, ALU.add).then_inc(x1_ready, 1)
                    for j in range(CH):
                        dve.wait_ge(x1_ready, i * CH + j + 1)
                        dve.nop(nofuse=True)
                        own.did(nc.vector.bn_stats(st6[:, j, :], hs[:, bass.ds((i * CH + j) * D, D)]))
                    own.wait()
                    dve.nop(nofuse=True)
                    for j in range(CH):
                        own.did(nc.vector.bn_aggr(mv[:, j, :], st6[:, j, :]))
                    own.wait()
                    own.did(nc.vector.tensor_scalar(vv[:, 0, :], mv[:, :, 1], EPS, None, ALU.add))
                    own.wait()
                    rsqrt(own, vv[:, 0, :], rs[:, :], vv[:, 1, :])
                    for j in range(CH):
                        nc.vector.tensor_scalar(yn[:, j, :], hs[:, bass.ds((i * CH + j) * D, D)], mv[:, j, 0:1], rs[:, j:j + 1],
                                                ALU.subtract, ALU.mult).then_inc(yn_ready, 1)
                    for j in range(CH + 1):
                        b = i * CH + j
                        if j < CH:
                            x_b = xs[:, bass.ds(b * D, D)]
                            dve.wait_ge(ff_psum, b + 1)
                            dve.wait_ge(x_ready, b + 1)
                            nc.vector.tensor_tensor(x_b, x_b, ps[0:P, 4 + j % 2, 0:D], ALU.add).then_inc(ff_taken, 1)
                            dve.wait_ge(ff_taken, b + 3)
                            dve.nop(nofuse=True)
                            own.did(nc.vector.bn_stats(st6b[:, j, :], x_b))
                            own.wait()
                            dve.nop(nofuse=True)
                            own.did(nc.vector.bn_aggr(mvb[:, j, :], st6b[:, j, :]))
                            own.wait()
                            own.did(nc.vector.tensor_scalar(vv[:, 2, j:j + 1], mvb[:, j, 1:2], EPS, None, ALU.add))
                            own.wait()
                            rsqrt(own, vv[:, 2, j:j + 1], rsb[:, j:j + 1], vv[:, 3, j:j + 1])
                            nc.vector.scalar_tensor_tensor(out=nmb[:, j:j + 1], in0=mvb[:, j, 0:1], scalar=-1.0, in1=rsb[:, j:j + 1],
                                                           op0=ALU.mult, op1=ALU.mult).then_inc(st_ready, 1)
                        if j >= 1:
                            h_b = hs[:, bass.ds((b - 1) * D, D)]
                            dve.wait_ge(loop_psum, b)
                            nc.vector.tensor_tensor(h_b, h1s[:, j - 1, :], ps[0:P, (j - 1) % 2, D:2 * D], ALU.add).then_inc(loop_taken, 1)
                            dve.wait_ge(msg_stored, b - 1 + (2 if j == 1 else 1))
                            for c in range(2, 4):
                                dve.wait_ge(msg_psum, 4 * (b - 1) + c + 1)
                                nc.vector.tensor_copy(msg[:, (j - 1) % 2, c * 512:(c + 1) * 512],
                                                      ps[0:P, 4 + c, :]).then_inc(msg_v, 1)

        with nc.Block() as block:
            cut = carve()
            rowbuf = cut([2 * T, D], parts=P)
            ind = cut([2, T, WIN], parts=P)
            dl = cut([2, T], parts=P)
            car = cut([2, WIN])
            osum = cut([2, D])
            idx = cut([2, T], I32, parts=P)
            row_in = [sem(f"message_in{t}") for t in range(2 * T)]
            dl_ready, ind_ready, car_ready, agg_done = sem("dl_ready"), sem("ind1_ready"), sem("car1_ready"), sem("summed1")
            win_done, osum_ready = sem("window1_done"), sem("osum1_ready")
            rel_out, rel_stored, idx_ready, zeros = sem("rel_out"), sem("rel_stored"), sem("idx1_ready"), sem("zeros1_ready")

            @block.sync
            def _(sp):
                nt = trip_count(sp)
                sp.sem_inc(rel_stored, 1)
                sp.wait_ge(zeros, 1)
                sp.dma_start(rel[0:WIN, :], osum[:, 1, :]).then_inc(rel_out, 16)
                with sp.Fori(0, nt) as i:
                    for u in range(2):
                        v = 2 * i + u
                        sp.wait_ge(osum_ready, v + 3)
                        sp.nop(nofuse=True)
                        sp.wait_ge(rel_out, 16 * (v + 1))
                        sp.nop(nofuse=True)
                        sp.sem_inc(rel_stored, 1)
                        w = sp.value_load(wof[0:1, bass.ds(v + 1, 1)], min_val=0, max_val=NWIN * WIN)
                        sp.dma_start(rel[bass.ds(w, WIN), :], osum[:, u, :]).then_inc(rel_out, 16)
                sp.wait_ge(rel_out, 32 * nt + 16)
                sp.nop(nofuse=True)

            @block.gpsimd
            def _(pool):
                nt = trip_count(pool)

                def indices(v, u):
                    g = pool.value_load(gof[0:1, bass.ds(v, 1)], min_val=0, max_val=G - 1)
                    pool.wait_ge(agg_done, 4 * v + 4)
                    nc.gpsimd.tensor_copy(idx[:, u, :], typs[:, bass.ds(g * T, T)]).then_inc(idx_ready, 1)

                indices(0, 0)
                with pool.Fori(0, nt) as i:
                    for u in range(2):
                        v = 2 * i + u
                        pool.wait_ge(idx_ready, v + 1)
                        for t in range(T):
                            if t == 6:
                                indices(v + 1, 1 - u)
                            if t % 2 == 0:
                                pool.wait_ge(agg_done, 4 * v + t // 2 + 1)
                                pool.nop(nofuse=True)
                            pool.indirect_dma_start(
                                out=rowbuf[:, u * T + t, :], out_offset=None, in_=h_all,
                                in_offset=bass.IndirectOffsetOnAxis(ap=idx[:, u, t:t + 1], axis=0)).then_inc(row_in[u * T + t], 16)

            @block.scalar
            def _(act):
                nt = trip_count(act)
                act.sem_inc(osum_ready, 2)
                with act.Fori(0, nt) as i:
                    for u in range(2):
                        v = 2 * i + u
                        act.wait_ge(win_done, v + 1)
                        act.wait_ge(rel_stored, v + 1)
                        nc.scalar.activation(osum[:, u, :], ps[:, 6 + u, 0:D], ACT.Copy).then_inc(osum_ready, 1)

            @block.tensor
            def _(pe):
                nt = trip_count(pe)
                pe.sem_inc(agg_done, 8)
                pe.wait_ge(zeros, 1)
                with pe.Fori(0, nt) as i:
                    for u in range(2):
                        v = 2 * i + u
                        pe.wait_ge(ind_ready, v + 1)
                        pe.wait_ge(osum_ready, v + 1)
                        for t in range(T):
                            pe.wait_ge(row_in[u * T + t], 16 * i + 16)
                            last = nc.tensor.matmul(ps[:, 6 + u, 0:D], ind[:, u, t, :], rowbuf[:, u * T + t, :],
                                                    start=(t == 0), stop=False)
                            if t % 2:
                                last.then_inc(agg_done, 1)
                        pe.wait_ge(osum_ready, v + 2)
                        pe.wait_ge(car_ready, v + 1)
                        nc.tensor.matmul(ps[:, 6 + u, 0:D], car[:, u, :], osum[:, 1 - u, :], start=False, stop=True).then_inc(win_done, 1)

            @block.vector
            def _(dve):
                nt = trip_count(dve)
                own = Steps(dve, sem("edge1_dve"))
                own.did(nc.vector.memset(osum, 0.0))
                own.wait()
                dve.sem_inc(zeros, 1)
                with dve.Fori(0, nt) as i:
                    for u in range(2):
                        v = 2 * i + u
                        g = dve.value_load(gof[0:1, bass.ds(v, 1)], min_val=0, max_val=G - 1)
                        dve.wait_ge(agg_done, 4 * v + 4)
                        dve.wait_ge(osum_ready, v + 1)
                        nc.vector.tensor_scalar(dl[:, u, :], dstf[:, bass.ds(g * T, T)], wst[0:P, bass.ds(v, 1)], None,
                                                ALU.subtract).then_inc(dl_ready, 1)
                        nc.vector.tensor_scalar(car[:, u, :], iotaj[:, :], wcar[:, bass.ds(v, 1)], None,
                                                ALU.is_equal).then_inc(car_ready, 1)
                        dve.wait_ge(dl_ready, v + 1)
                        for t in range(T):
                            last = nc.vector.tensor_scalar(ind[:, u, t, :], iotaj[0:P, :], dl[:, u, t:t + 1], None, ALU.is_equal)
                        last.then_inc(ind_ready, 1)

        with nc.Block() as block:
            cut = carve()
            z = cut([NBLK * D], parts=P)
            vv = cut([2, CH], parts=P)
            rel_in, z_ready, g_ready, n_ready, o_ready, out_sem = (
                sem(n) for n in ("rel_in", "z_ready", "gelu_ready", "normed_ready", "result_ready", "result_out"))

            @block.sync
            def _(sp):
                for c in range(NCH):
                    sp.dma_start(z[:, c * CH * D:(c + 1) * CH * D].rearrange("p (b d) -> p b d", d=D),
                                 rel[c * CH * P:(c + 1) * CH * P, :].rearrange("(b p) d -> p b d", p=P)).then_inc(rel_in, 16)
                    sp.wait_ge(rel_in, 16 * c + 16)
                with sp.Fori(0, NCH) as i:
                    for j in range(CH):
                        b = i * CH + j
                        sp.wait_ge(o_ready, b + 1)
                        sp.nop(nofuse=True)
                        sp.dma_start(out[bass.ds(b * P, P), :], z[:, bass.ds(b * D, D)]).then_inc(out_sem, 16)
                sp.wait_ge(out_sem, 16 * NBLK)

            @block.gpsimd
            def _(pool):
                own = Steps(pool, sem("last_pool"))
                with pool.Fori(0, NCH) as i:
                    own.loop(i, CH)
                    for j in range(CH):
                        b = i * CH + j
                        z_b = z[:, bass.ds(b * D, D)]
                        pool.wait_ge(n_ready, b + 1)
                        pool.nop(nofuse=True)
                        own.did(nc.gpsimd.tensor_tensor(z_b, z_b, rowb[:, 3, :], ALU.add))
                        own.wait()
                        pool.nop(nofuse=True)
                        nc.gpsimd.tensor_tensor(z_b, z_b, xs[:, bass.ds(b * D, D)], ALU.add).then_inc(o_ready, 1)

            @block.scalar
            def _(act):
                with act.Fori(0, NCH) as i:
                    for j in range(CH):
                        b = i * CH + j
                        z_b = z[:, bass.ds(b * D, D)]
                        act.wait_ge(z_ready, b + 1)
                        nc.scalar.activation(z_b, z_b, ACT.Gelu).then_inc(g_ready, 1)

            @block.vector
            def _(dve):
                own = Steps(dve, sem("last_dve"))
                with dve.Fori(0, NCH) as i:
                    dve.wait_ge(rel_in, 16 * i + 16)
                    for j in range(CH):
                        z_b = z[:, bass.ds((i * CH + j) * D, D)]
                        nc.vector.tensor_tensor(z_b, z_b, hs[:, bass.ds((i * CH + j) * D, D)], ALU.add).then_inc(z_ready, 1)
                with dve.Fori(0, NCH) as i:
                    own.loop(i, 2 * CH + 1 + 14 + CH)
                    for j in range(CH):
                        dve.wait_ge(g_ready, i * CH + j + 1)
                        dve.nop(nofuse=True)
                        own.did(nc.vector.bn_stats(st6[:, j, :], z[:, bass.ds((i * CH + j) * D, D)]))
                    own.wait()
                    dve.nop(nofuse=True)
                    for j in range(CH):
                        own.did(nc.vector.bn_aggr(mv[:, j, :], st6[:, j, :]))
                    own.wait()
                    own.did(nc.vector.tensor_scalar(vv[:, 0, :], mv[:, :, 1], EPS, None, ALU.add))
                    own.wait()
                    rsqrt(own, vv[:, 0, :], rs[:, :], vv[:, 1, :])
                    for j in range(CH):
                        z_b = z[:, bass.ds((i * CH + j) * D, D)]
                        own.did(nc.vector.tensor_scalar(z_b, z_b, mv[:, j, 0:1], rs[:, j:j + 1], ALU.subtract, ALU.mult))
                    own.wait()
                    for j in range(CH):
                        z_b = z[:, bass.ds((i * CH + j) * D, D)]
                        nc.vector.tensor_tensor(z_b, z_b, rowb[:, 2, :], ALU.mult).then_inc(n_ready, 1)


_INS = ['x', 'src', 'dst', 'edge_type_8', 'L0_gnn_Wqkv', 'L0_gnn_bqkv', 'L0_gnn_ln_attn_g', 'L0_gnn_ln_attn_b',
        'L0_gnn_ln_res_g', 'L0_gnn_ln_res_b', 'L0_gnn_W_in', 'L0_gnn_b_in', 'L0_gnn_W_out', 'L0_gnn_b_out',
        'L1_gnn_basis', 'L1_gnn_comp', 'L1_gnn_loop_w', 'L1_gnn_h_bias', 'L1_gnn_ln_gamma', 'L1_gnn_ln_beta']


def kernel(**inputs):
    import numpy as _np
    import concourse.bacc as _bacc
    from concourse import mybir as _mybir
    from concourse.bass_utils import run_bass_kernel_spmd as _run

    nc = _bacc.Bacc("TRN2", target_bir_lowering=False, num_devices=1)
    arrays, args = {}, []
    for name in _INS:
        a = _np.ascontiguousarray(inputs[name])
        arrays[f"in_{name}"] = a
        args.append(nc.dram_tensor(f"in_{name}", a.shape, _mybir.dt.from_np(a.dtype), kind="ExternalInput").ap())
    o = nc.dram_tensor("out", (N, D), _mybir.dt.float32, kind="ExternalOutput").ap()
    program(nc, *args, o)
    r = _run(nc, [arrays], core_ids=[0])
    return r.results[0]["out"]
```

```python
import concourse.bass as bass
from concourse import mybir
from contextlib import ExitStack

FP32 = mybir.dt.float32
BF16 = mybir.dt.bfloat16
I32 = mybir.dt.int32
I16 = mybir.dt.int16
ALU = mybir.AluOpType
ACT = mybir.ActivationFunctionType
AX = mybir.AxisListType
RMAX = bass.bass_isa.ReduceOp.max

N, D = 3125, 256
E = 50000
H = 8
DH = D // H
FF = 4 * D
R, NB = 8, 4
EPS = 1e-5
SCALE = float(D) ** -0.5
P = 125
NBLK = N // P
CH = 5
NCH = NBLK // CH
T = 8
PAIRS = T // 2
GE = P * T
G = E // GE
WIN = 128
NWIN = -(-N // WIN)
VMAX = G * NWIN
VTAB = G * (NWIN + 1)
AWORDS = 21380
KW = D + H
AW = D + H
NPAD = N + 3 * P
TINY = 1e-37
WIDE = 40.0
BIG = 1e30


class Steps:

    def __init__(self, eng, sem):
        self.eng, self.sem, self.n, self.base = eng, sem, 0, 0

    def did(self, ins):
        self.n += 1
        return ins.then_inc(self.sem, 1)

    def loop(self, i, per):
        self.per, self.first, self.i = per, self.n, i
        self.base = i * per

    def end(self, trips):
        assert self.n - self.first == self.per, (self.n - self.first, self.per)
        self.base = 0
        self.n = self.first + self.per * trips

    def wait(self):
        self.eng.wait_ge(self.sem, self.base + self.n)


def program(nc, x, src, dst, edge_type, Wqkv, bqkv, ga, ba, gr, br, W_in, b_in, W_out, b_out,
            basis, comp, loop_w, h_bias, gamma, beta, out):
    qv_tab = nc.dram_tensor("qv_tab", (N, 2 * D), FP32).ap()
    k_tab = nc.dram_tensor("k_tab", (NPAD, 3 * KW), BF16).ap()
    dst16 = nc.dram_tensor("dst16", (G, GE), I16).ap()
    bounds = nc.dram_tensor("bounds", (G, 2), FP32).ap()
    att = nc.dram_tensor("att", (NPAD, AW), FP32).ap()
    s_tab = nc.dram_tensor("s_tab", (G, H, GE), FP32).ap()
    m_tab = nc.dram_tensor("m_tab", (NPAD, H), FP32).ap()
    rel = nc.dram_tensor("rel", (NPAD, D), FP32).ap()
    h_all = nc.dram_tensor("h_all", (N * R, D), FP32).ap()

    x_v = x.rearrange("(b p) d -> p b d", p=P)
    out_v = out.rearrange("(b p) d -> p b d", p=P)
    ctx = ExitStack()
    with ctx:
        def sb(name, shape, dt=FP32):
            return ctx.enter_context(nc.sbuf_tensor(name, shape, dt))

        def sem(name):
            return ctx.enter_context(nc.semaphore(name))

        ps = ctx.enter_context(nc.psum_tensor("ps", [128, 8, 512], FP32))
        xs = sb("xs", [P, NBLK * D])
        hs = sb("hs", [P, NBLK * D])
        srcs = sb("srcs", [P, G * T], I32)
        dsti = sb("dsti", [P, G * T], I32)
        typs = sb("typs", [P, G * T], I32)
        dstf = sb("dstf", [P, G * T])
        gof = sb("gof", [1, VTAB], I32)
        wof = sb("wof", [128, VTAB + 1], I32)
        wnode = sb("wnode", [128, VTAB])
        wcar = sb("wcar", [128, VTAB])
        wst = sb("wst", [128, VTAB])
        bnd = sb("bnd", [128, G, 2])
        flg = sb("flg", [128, 8])
        trips = sb("trips", [128, 2], I32)
        wide = trips[:, 1:2]
        iotap = sb("iotap", [128, 1])
        iotai = sb("iotai", [128, 128], I32)
        iotaj = sb("iotaj", [128, 128])
        ident = sb("ident", [128, 128])
        identb = sb("identb", [128, 128], BF16)
        win = sb("win", [128, 2, FF])
        wout = sb("wout", [128, FF // 128, D])
        wrel = sb("wrel", [128, 2, R * D])
        wloop = sb("wloop", [128, 2, D])
        cmpb = sb("cmpb", [128, R * NB])
        cols = sb("cols", [128, 4, 2])
        bin_ = sb("bin_", [128, FF // 128])
        rowb = sb("rowb", [P, 4, D])
        st6 = sb("st6", [P, CH, 6])
        mv = sb("mv", [P, CH, 2])
        rs = sb("rs", [P, CH])
        nm = sb("nm", [P, CH])
        st6b = sb("st6b", [P, CH, 6])
        mvb = sb("mvb", [P, CH, 2])
        rsb = sb("rsb", [P, CH])
        nmb = sb("nmb", [P, CH])
        nrm = sb("nrm", [P, NBLK, 2 * H])
        nmx = sb("nmx", [128, 2])
        nmr = sb("nmr", [128, 2])
        nbias = sb("nbias", [128, 1])
        A = sb("arena", [128, AWORDS])

        def carve():
            at = [0]

            def cut(shape, dt=FP32, parts=128):
                n = 1
                for s in shape:
                    n *= s
                words = n if dt in (FP32, I32) else (n + 1) // 2
                v = A[0:parts, at[0]:at[0] + words]
                at[0] += words
                assert at[0] <= AWORDS, at[0]
                if dt != FP32:
                    v = v.bitcast(dt)
                if len(shape) == 1:
                    return v
                names = "abcd"[:len(shape)]
                pat = "p (%s) -> p %s" % (" ".join(names), " ".join(names))
                return v.rearrange(pat, **{c: s for c, s in zip(names[1:], shape[1:])})
            return cut

        s_x, s_w, s_e, s_b = sem("x_loaded"), sem("weights_loaded"), sem("edges_loaded"), sem("bounds_back")
        s_w2, s_const = sem("later_weights_loaded"), sem("constants_ready")

        with nc.Block() as block:
            cut = carve()
            hn = cut([CH, D], parts=P)
            hT = cut([CH, 2, P])
            qvst = cut([CH, 2 * D], parts=P)
            kf = cut([CH, D], parts=P)
            r1 = cut([CH, D], parts=P)
            sq = cut([CH, 2 * D], parts=P)
            kst = cut([CH, 3, KW], BF16, parts=P)
            zero = cut([2 * AW], parts=P)
            wtmp = cut([4, 2, D])
            wq = cut([2, 3 * D])
            bq = cut([3 * D], parts=P)
            base = cut([NB, 2, D])
            rows = cut([GE], I32, parts=G)
            rows16 = cut([GE], I16, parts=G)
            st_ready, h_ready = sem("st_ready"), sem("h_ready")
            var_ready, dev_ready = sem("var_ready"), sem("dev_ready")
            hn_ready, hT_in_psum, hT_ready = sem("hn_ready"), sem("hT_in_psum"), sem("hT_ready")
            qkv_ready, qkv_taken = sem("qkv_ready"), sem("qkv_taken")
            kh_ready, r1_ready, km_ready, kl_ready = (sem(n) for n in ("kh_ready", "r1_ready", "km_ready", "kl_ready"))
            sq_ready, sq_used = sem("sq_ready"), sem("sq_used")
            qv_out, k_out, stored, zeroed, z_out = (sem(n) for n in ("qv_out", "k_out", "stored", "zeroed", "z_out"))
            d16, bout = sem("dst16_stored"), sem("bounds_stored")
            cast, mm, ident_ready = sem("rows_cast"), sem("bounds_found"), sem("ident_ready")
            nmax_in, nmax_back = sem("nmax_in"), sem("nmax_back")

            @block.sync
            def _(sp):
                sp.dma_start(rows, dst.rearrange("(g e) -> g e", g=G)).then_inc(s_b, 16)
                sp.dma_start(xs[:, :].rearrange("p (b d) -> p b d", d=D), x_v).then_inc(s_x, 16)
                for tab, a in ((srcs, src), (dsti, dst), (typs, edge_type)):
                    sp.dma_start(tab[:, :].rearrange("p (g t) -> p g t", t=T),
                                 a.rearrange("(g p t) -> p g t", p=P, t=T)).then_inc(s_e, 16)
                for o, c in ((0, 0), (1, 2), (2, 1)):
                    sp.dma_start(wq[:, :, o * D:(o + 1) * D],
                                 Wqkv[:, c * D:(c + 1) * D].rearrange("(k p) n -> p k n", p=128)).then_inc(s_w, 16)
                    sp.dma_start(bq[:, o * D:(o + 1) * D],
                                 bqkv[c * D:(c + 1) * D].partition_broadcast(P)).then_inc(s_w, 16)
                for n, a in enumerate((ga, ba, gr, br)):
                    sp.dma_start(cols[:, n, :], a.rearrange("(k p) -> p k", p=128),
                                 allow_slow_non_contiguous=True).then_inc(s_w, 16)
                sp.dma_start(bin_[:, :], b_in.rearrange("(k p) -> p k", p=128),
                             allow_slow_non_contiguous=True).then_inc(s_w2, 16)
                for n, a in enumerate((b_out, h_bias, gamma, beta)):
                    sp.dma_start(rowb[:, n, :], a.partition_broadcast(P)).then_inc(s_w2, 16)
                sp.dma_start(cmpb[:, :], comp.rearrange("r b -> (r b)").partition_broadcast(128)).then_inc(s_w2, 16)
                sp.dma_start(base, basis.rearrange("b (k p) o -> p b k o", p=128)).then_inc(s_w2, 16)
                sp.dma_start(wloop[:, :, :], loop_w.rearrange("(k p) n -> p k n", p=128)).then_inc(s_w2, 16)
                sp.dma_start(win[:, :, :], W_in.rearrange("(k p) n -> p k n", p=128)).then_inc(s_w2, 16)
                sp.dma_start(wout[:, :, :], W_out.rearrange("(k p) n -> p k n", p=128)).then_inc(s_w2, 16)
                sp.wait_ge(cast, 1)
                sp.dma_start(dst16, rows16).then_inc(d16, 16)
                sp.wait_ge(mm, 2)
                sp.dma_start(bounds, flg[0:G, 0:2]).then_inc(bout, 16)
                sp.wait_ge(bout, 16)
                sp.dma_start(bnd[:, :, :], bounds.partition_broadcast(128)).then_inc(s_b, 16)
                sp.wait_ge(zeroed, 2)
                for c in range(NPAD // P // 2):
                    sp.dma_start(att[c * 2 * P:(c + 1) * 2 * P, :].rearrange("(b p) d -> p b d", p=P),
                                 zero[:, 0:2 * AW].rearrange("p (b d) -> p b d", d=AW)).then_inc(z_out, 16)
                    sp.dma_start(rel[c * 2 * P:(c + 1) * 2 * P, :].rearrange("(b p) d -> p b d", p=P),
                                 zero[:, 0:2 * D].rearrange("p (b d) -> p b d", d=D)).then_inc(z_out, 16)
                for c in range(N, NPAD, P):
                    sp.dma_start(k_tab[c:c + P, :], zero.bitcast(BF16)[:, 0:3 * KW]).then_inc(z_out, 16)
                with sp.Fori(0, NCH) as i:
                    for j in range(CH):
                        b = i * CH + j
                        sp.wait_ge(qkv_taken, 2 * b + 12)
                        sp.dma_start(qv_tab[bass.ds(b * P, P), :], qvst[:, j, :]).then_inc(qv_out, 16)
                        sp.wait_ge(kl_ready, b + 1)
                        sp.dma_start(k_tab[bass.ds(b * P, P), :], kst[:, j, :, :].rearrange("p c d -> p (c d)")).then_inc(k_out, 16)
                        sp.wait_ge(qv_out, 16 * b + 16)
                        sp.wait_ge(k_out, 16 * b + 16)
                        sp.sem_inc(stored, 1)
                sp.wait_ge(d16, 16)
                sp.wait_ge(s_b, 32)
                sp.wait_ge(z_out, 16 * (NPAD // P + (NPAD - N) // P))

            @block.gpsimd
            def _(pool):
                own = Steps(pool, sem("pre_pool"))
                nc.gpsimd.iota(wof[:, 1:VTAB + 1].rearrange("p (w g) -> p w g", g=G), pattern=[[WIN, NWIN + 1], [0, G]],
                               base=0, channel_multiplier=0).then_inc(s_const, 1)
                nc.gpsimd.iota(gof[:, :].rearrange("p (w g) -> p w g", g=G), pattern=[[0, NWIN + 1], [1, G]],
                               base=0, channel_multiplier=0).then_inc(s_const, 1)
                nc.gpsimd.iota(iotai[:, :], pattern=[[1, 128]], base=0, channel_multiplier=0).then_inc(s_const, 1)
                nc.gpsimd.iota(trips[:, 0:1], pattern=[[0, 1]], base=0, channel_multiplier=1).then_inc(s_const, 1)
                nc.gpsimd.memset(wof[:, 0:1], 0).then_inc(s_const, 1)
                nc.gpsimd.memset(nmx[:, :], 0.0).then_inc(s_const, 1)
                nc.gpsimd.memset(zero, 0.0).then_inc(zeroed, 1)
                nc.gpsimd.memset(kst[:, :, :, D:KW], 0.0).then_inc(zeroed, 1)
                pool.wait_ge(s_w2, 16 * 10)
                for r in range(R):
                    w = wrel[:, :, r * D:(r + 1) * D]
                    own.did(nc.gpsimd.tensor_scalar(w, base[:, 0, :, :], cmpb[:, r * NB:r * NB + 1], None, ALU.mult))
                for n in range(1, NB):
                    for half in range(2):
                        relations = range(half * R // 2, (half + 1) * R // 2)
                        for r in relations:
                            own.did(nc.gpsimd.tensor_scalar(wtmp[:, r % 4, :, :], base[:, n, :, :],
                                                            cmpb[:, r * NB + n:r * NB + n + 1], None, ALU.mult))
                        own.wait()
                        for r in relations:
                            w = wrel[:, :, r * D:(r + 1) * D]
                            own.did(nc.gpsimd.tensor_tensor(w, w, wtmp[:, r % 4, :, :], ALU.add))
                        own.wait()
                own.wait()
                pool.wait_ge(nmax_in, 1)
                nc.gpsimd.partition_all_reduce(nmr[:, :], nmx[:, :], 128, RMAX).then_inc(nmax_back, 1)

            @block.scalar
            def _(act):
                act.wait_ge(s_x, 16)
                act.wait_ge(s_w, 16 * 10)
                with act.Fori(0, NCH) as i:
                    act.wait_ge(var_ready, 2 * i + 1)
                    nc.scalar.activation(rs[:, :], rs[:, :], ACT.Sqrt).then_inc(dev_ready, 1)
                    act.wait_ge(st_ready, i + 1)
                    for j in range(CH):
                        o = (i * CH + j) * D
                        nc.scalar.activation(hs[:, bass.ds(o, D)], xs[:, bass.ds(o, D)], ACT.Relu,
                                             bias=nm[:, j:j + 1], scale=rs[:, j:j + 1]).then_inc(h_ready, 1)
                    act.wait_ge(var_ready, 2 * i + 2)
                    nc.scalar.activation(rsb[:, :], rsb[:, :], ACT.Sqrt).then_inc(dev_ready, 1)
                    for j in range(CH + 2):
                        b = i * CH + j
                        if j < CH:
                            act.wait_ge(hT_in_psum, 2 * b + 2)
                            for k in range(2):
                                nc.scalar.activation(hT[:, j, k, :], ps[:, j % 2, k * P:k * P + P], ACT.Identity,
                                                     bias=cols[:, 1, k:k + 1], scale=cols[:, 0, k:k + 1]).then_inc(hT_ready, 1)
                        if 1 <= j <= CH:
                            act.wait_ge(qkv_taken, 2 * b + 10)
                            nc.scalar.activation(kst[:, j - 1, 0, 0:D], kf[:, j - 1, :], ACT.Copy).then_inc(kh_ready, 1)
                            nc.scalar.activation(sq[:, j - 1, 0:D], qvst[:, j - 1, 0:D], ACT.Square).then_inc(sq_ready, 1)
                            nc.scalar.activation(sq[:, j - 1, D:2 * D], kf[:, j - 1, :], ACT.Square).then_inc(sq_ready, 1)
                        if j >= 2:
                            act.wait_ge(r1_ready, b - 1)
                            nc.scalar.activation(kst[:, j - 2, 1, 0:D], r1[:, j - 2, :], ACT.Copy).then_inc(km_ready, 1)
                act.wait_ge(var_ready, 2 * NCH + 1)
                nc.scalar.activation(nbias[:, :], nbias[:, :], ACT.Sqrt, scale=SCALE * SCALE).then_inc(dev_ready, 1)

            @block.tensor
            def _(pe):
                pe.wait_ge(s_w, 16 * 10)
                pe.wait_ge(ident_ready, 1)

                def turn(b, j):
                    pe.wait_ge(hn_ready, b + 1)
                    for k in range(2):
                        nc.tensor.transpose(ps[:, j % 2, k * P:k * P + P], hn[:, j, k * 128:k * 128 + 128],
                                            ident[0:P, 0:P]).then_inc(hT_in_psum, 1)

                def project(b, j):
                    pe.wait_ge(hT_ready, 2 * b + 2)
                    pe.wait_ge(qkv_taken, 2 * b + (10 if j == 0 else 6 if j == 1 else 8))
                    for c, bank, n in ((0, 2 + j % 2, 2 * D), (2 * D, 4 + j % 2, D)):
                        for k in range(2):
                            last = nc.tensor.matmul(ps[0:P, bank, 0:n], hT[:, j, k, :], wq[:, k, c:c + n],
                                                    start=(k == 0), stop=(k == 1))
                    last.then_inc(qkv_ready, 1)

                with pe.Fori(0, NCH) as i:
                    for j in range(CH + 1):
                        if j < CH:
                            turn(i * CH + j, j)
                        if j >= 1:
                            project(i * CH + j - 1, j - 1)

            @block.vector
            def _(dve):
                own = Steps(dve, sem("pre_dve"))
                dve.wait_ge(s_b, 16)
                nc.vector.tensor_copy(rows16, rows).then_inc(cast, 1)
                nc.vector.tensor_reduce(flg[0:G, 0:1], rows, AX.X, ALU.min).then_inc(mm, 1)
                nc.vector.tensor_reduce(flg[0:G, 1:2], rows, AX.X, ALU.max).then_inc(mm, 1)
                dve.sem_inc(qkv_taken, 10)
                dve.sem_inc(stored, CH)
                dve.wait_ge(s_const, 6)
                own.did(nc.vector.tensor_copy(iotaj[:, :], iotai[:, :]))
                own.did(nc.vector.tensor_copy(iotap[:, :], trips[:, 0:1]))
                own.wait()
                own.did(nc.vector.tensor_scalar(ident[:, :], iotaj[:, :], iotap[:, :], None, ALU.is_equal))
                own.did(nc.vector.tensor_scalar(identb[:, :], iotaj[:, :], iotap[:, :], None, ALU.is_equal))
                own.wait()
                dve.sem_inc(ident_ready, 1)
                dve.wait_ge(s_x, 16)
                dve.wait_ge(s_w, 16 * 10)
                dve.wait_ge(zeroed, 2)
                with dve.Fori(0, NCH) as i:
                    own.loop(i, 4 * CH + 2)

                    def stats(tile, st, m, r, n, done):
                        for j in range(CH):
                            if done is not None:
                                dve.wait_ge(done, i * CH + j + 1)
                            own.did(nc.vector.bn_stats(st[:, j, :], tile(j)))
                        own.wait()
                        dve.nop(nofuse=True)
                        for j in range(CH):
                            own.did(nc.vector.bn_aggr(m[:, j, :], st[:, j, :]))
                        own.wait()
                        nc.vector.tensor_scalar(r[:, :], m[:, :, 1], EPS, None, ALU.add).then_inc(var_ready, 1)
                        dve.wait_ge(dev_ready, 2 * i + n + 1)
                        own.did(nc.vector.reciprocal(r[:, :], r[:, :]))
                        own.wait()

                    def x_(j):
                        return xs[:, bass.ds((i * CH + j) * D, D)]

                    def h_(j):
                        return hs[:, bass.ds((i * CH + j) * D, D)]

                    stats(x_, st6, mv, rs, 0, None)
                    nc.vector.scalar_tensor_tensor(out=nm[:, :], in0=mv[:, :, 0], scalar=-1.0, in1=rs[:, :],
                                                   op0=ALU.mult, op1=ALU.mult).then_inc(st_ready, 1)
                    stats(h_, st6b, mvb, rsb, 1, h_ready)
                    for j in range(CH):
                        nc.vector.tensor_scalar(hn[:, j, :], h_(j), mvb[:, j, 0:1], rsb[:, j:j + 1],
                                                ALU.subtract, ALU.mult).then_inc(hn_ready, 1)
                    for j in range(CH + 3):
                        b = i * CH + j
                        if j < CH:
                            dve.wait_ge(qkv_ready, b + 1)
                            dve.wait_ge(stored, b + 1)
                            nc.vector.tensor_tensor(qvst[:, j, :], ps[0:P, 2 + j % 2, :], bq[:, 0:2 * D],
                                                    ALU.add).then_inc(qkv_taken, 1)
                            nc.vector.tensor_tensor(kf[:, j, :], ps[0:P, 4 + j % 2, 0:D], bq[:, 2 * D:3 * D],
                                                    ALU.add).then_inc(qkv_taken, 1)
                        if 1 <= j <= CH:
                            dve.wait_ge(kh_ready, b)
                            nc.vector.tensor_tensor(r1[:, j - 1, :], kf[:, j - 1, :], kst[:, j - 1, 0, 0:D],
                                                    ALU.subtract).then_inc(r1_ready, 1)
                            dve.wait_ge(sq_ready, 2 * b)
                            nc.vector.tensor_reduce(nrm[:, bass.ds(b - 1, 1), :].rearrange("p o h -> p (o h)"),
                                                    sq[:, j - 1, :].rearrange("p (h d) -> p h d", d=DH),
                                                    AX.X, ALU.add).then_inc(sq_used, 1)
                        if 3 <= j:
                            dve.wait_ge(km_ready, b - 2)
                            nc.vector.tensor_tensor(kst[:, j - 3, 2, 0:D], r1[:, j - 3, :], kst[:, j - 3, 1, 0:D],
                                                    ALU.subtract).then_inc(kl_ready, 1)
                own.end(NCH)
                dve.wait_ge(s_e, 48)
                own.did(nc.vector.tensor_copy(dstf[:, :], dsti[:, :]))
                own.did(nc.vector.scalar_tensor_tensor(out=typs[:, :], in0=srcs[:, :], scalar=float(R), in1=typs[:, :],
                                                       op0=ALU.mult, op1=ALU.add))
                dve.wait_ge(s_b, 32)
                own.did(nc.vector.tensor_tensor(wst[:, 0:G], bnd[:, :, 1], bnd[:, :, 0], ALU.subtract))
                own.did(nc.vector.tensor_tensor(wst[:, G:2 * G - 1], bnd[:, 1:G, 0], bnd[:, 0:G - 1, 0], ALU.subtract))
                own.wait()
                own.did(nc.vector.tensor_reduce(flg[:, 2:3], wst[:, 0:G], AX.X, ALU.max))
                own.did(nc.vector.tensor_reduce(flg[:, 3:4], wst[:, G:2 * G - 1], AX.X, ALU.min))
                own.wait()
                own.did(nc.vector.tensor_scalar(flg[:, 4:5], flg[:, 2:3], float(WIN - 1), None, ALU.is_le))
                own.did(nc.vector.tensor_scalar(flg[:, 5:6], flg[:, 3:4], 0.0, None, ALU.is_ge))
                own.wait()
                own.did(nc.vector.tensor_tensor(flg[:, 6:7], flg[:, 4:5], flg[:, 5:6], ALU.mult))
                own.wait()
                own.did(nc.vector.tensor_scalar(trips[:, 0:1], flg[:, 6:7], float((G - VMAX) // 2), float(VMAX // 2),
                                                ALU.mult, ALU.add))
                own.did(nc.vector.tensor_scalar(wof[:, 1:G + 1], bnd[:, :, 0], flg[:, 6:7], None, ALU.mult))
                own.wait()
                own.did(nc.vector.tensor_copy(wst[:, :], wof[:, 1:VTAB + 1]))
                own.did(nc.vector.tensor_tensor(wcar[:, :], wof[:, 0:VTAB], wof[:, 1:VTAB + 1], ALU.subtract))
                own.wait()
                own.did(nc.vector.tensor_scalar(wnode[:, :], wst[:, :], iotap[:, :], None, ALU.add))
                own.did(nc.vector.tensor_scalar(wcar[:, :], wcar[:, :], iotap[:, :], None, ALU.add))
                own.wait()
                dve.wait_ge(sq_used, NBLK)
                for n in range(2):
                    own.did(nc.vector.tensor_reduce(nmx[0:P, n:n + 1], nrm[:, :, n * H:(n + 1) * H], AX.XY, ALU.max))
                own.wait()
                dve.sem_inc(nmax_in, 1)
                dve.wait_ge(nmax_back, 1)
                nc.vector.tensor_tensor(nbias[:, :], nmr[:, 0:1], nmr[:, 1:2], ALU.mult).then_inc(var_ready, 1)
                dve.wait_ge(dev_ready, 2 * NCH + 1)
                own.did(nc.vector.tensor_scalar(wide, nbias[:, :], WIDE, None, ALU.is_gt))
                own.did(nc.vector.tensor_scalar(flg[:, 7:8], nbias[:, :], WIDE, -1.0, ALU.is_le, ALU.mult))
                own.wait()
                own.did(nc.vector.tensor_scalar(nbias[:, :], nbias[:, :], BIG, flg[:, 7:8], ALU.min, ALU.mult))
                own.wait()



        with nc.Block() as block:
            cut = carve()
            rowbuf = cut([2 * T, 2 * D + H], parts=P)
            ind = cut([2, T, WIN], parts=P)
            indT = cut([2, GE], BF16)
            kwin = cut([2, 3 * KW], BF16)
            drow = cut([2, GE], I16)
            car = cut([2, WIN])
            osum = cut([2, AW])
            sco = cut([T, H], parts=P)
            idx = cut([2, T], I32, parts=P)
            k_ready, k_used = sem("key_rows_ready"), sem("scores_ready")
            kwin_in = [sem(f"key_window_in{u}") for u in range(2)]
            drow_in = [sem(f"dst_row_in{u}") for u in range(2)]
            row_in = [sem(f"row_in{t}") for t in range(2 * T)]
            indT_ready, car_ready = sem("indT_ready"), sem("car_ready")
            turn_ready, ind_ready = sem("turn_ready"), sem("ind_ready")
            exp_done, w_ready, agg_done = sem("exp_done"), sem("weighted_ready"), sem("summed")
            win_done, osum_ready = sem("window_done"), sem("osum_ready")
            att_out, att_stored, idx_ready = sem("att_out"), sem("att_stored"), sem("idx_ready")
            zeros = sem("zeros_ready")

            def seen(v, j, ahead):
                return PAIRS * v + j + 1 + ahead

            SCORES_AHEAD = 4
            EXP_AHEAD = 4
            WEIGHTED_AHEAD = 4
            SUMMED_AHEAD = 8
            KEYS_AHEAD = 8
            IND_AHEAD = 4

            def trip_count(eng):
                return eng.value_load(trips[0:1, 0:1], min_val=G // 2, max_val=VMAX // 2)

            cut = carve()
            mq = cut([T, 2 * D], parts=P)
            mk = cut([T, 3 * KW], BF16, parts=P)
            mk32 = cut([T, D], parts=P)
            msc = cut([H, T], parts=P)
            midx = cut([2, T], I32, parts=P)
            cut = carve()
            ball = cut([H, GE])
            bmask = cut([GE])
            brow = cut([GE], I16)
            bmax = cut([H])
            mwin = cut([H])
            mneg = cut([H], parts=P)
            mall = cut([NBLK, H], parts=P)
            mrest = cut([NBLK, H], parts=P)
            mparts = cut([3, NBLK, H], BF16, parts=P)
            mi_ready, mrow_in, msc_ready, msc_used = (sem(n) for n in ("max_indices", "max_rows_in", "max_scores", "max_rows_used"))
            msc_out, msc_stored, mneg_ready, mneg_out = (sem(n) for n in ("max_scores_out", "max_scores_stored", "lowest_ready", "lowest_out"))
            mv_in, mwin_ready, mwin_out = (sem(n) for n in ("max_visit_in", "window_max_ready", "window_max_out"))
            mall_in, mparts_ready, shifts_out = sem("maxima_in"), sem("shift_parts_ready"), sem("shifts_out")

            def is_wide(eng):
                return eng.value_load(wide[0:1, 0:1], min_val=0, max_val=1)

            def maxima_sync(sp, nt):
                sp.sem_inc(msc_stored, 1)
                with sp.Fori(0, G) as g:
                    sp.wait_ge(msc_ready, g + 1)
                    sp.nop(nofuse=True)
                    sp.dma_start(s_tab[bass.ds(g, 1), :, :].rearrange("o h (p t) -> p (o h) t", t=T), msc).then_inc(msc_out, 16)
                    sp.wait_ge(msc_out, 16 * g + 16)
                    sp.nop(nofuse=True)
                    sp.sem_inc(msc_stored, 1)
                sp.wait_ge(mneg_ready, 1)
                for b in range(NPAD // P):
                    sp.dma_start(m_tab[b * P:(b + 1) * P, :], mneg).then_inc(mneg_out, 16)
                sp.wait_ge(mneg_out, 16 * (NPAD // P))
                with sp.Fori(0, 2 * nt) as v:
                    w = sp.value_load(wof[0:1, bass.ds(v + 1, 1)], min_val=0, max_val=NWIN * WIN)
                    g = sp.value_load(gof[0:1, bass.ds(v, 1)], min_val=0, max_val=G - 1)
                    sp.dma_start(ball.rearrange("p h e -> p (h e)"), s_tab[bass.ds(g, 1), :, :].rearrange("o h e -> (o h e)")
                                 .partition_broadcast(128)).then_inc(mv_in, 16)
                    sp.dma_start(brow, dst16[bass.ds(g, 1), :].rearrange("o e -> (o e)").partition_broadcast(128)).then_inc(mv_in, 16)
                    sp.dma_start(mwin, m_tab[bass.ds(w, WIN), :]).then_inc(mv_in, 16)
                    sp.wait_ge(mwin_ready, v + 1)
                    sp.nop(nofuse=True)
                    sp.dma_start(m_tab[bass.ds(w, WIN), :], mwin).then_inc(mwin_out, 16)
                    sp.wait_ge(mwin_out, 16 * v + 16)
                    sp.nop(nofuse=True)
                sp.dma_start(mall, m_tab[0:N, :].rearrange("(b p) h -> p b h", p=P)).then_inc(mall_in, 16)
                sp.wait_ge(mparts_ready, 1)
                for c in range(3):
                    sp.dma_start(k_tab[0:N, c * KW + D:(c + 1) * KW].rearrange("(b p) h -> p b h", p=P),
                                 mparts[:, c, :, :]).then_inc(shifts_out, 16)
                sp.wait_ge(shifts_out, 48)

            def maxima_gpsimd(pool):
                with pool.Fori(0, G) as g:
                    pool.wait_ge(msc_used, g + 1)
                    nc.gpsimd.tensor_copy(midx[:, 0, :], srcs[:, bass.ds(g * T, T)]).then_inc(mi_ready, 1)
                    nc.gpsimd.tensor_copy(midx[:, 1, :], dsti[:, bass.ds(g * T, T)]).then_inc(mi_ready, 1)
                    pool.wait_ge(mi_ready, 2 * g + 2)
                    pool.nop(nofuse=True)
                    for t in range(T):
                        pool.indirect_dma_start(
                            out=mq[:, t, :], out_offset=None, in_=qv_tab,
                            in_offset=bass.IndirectOffsetOnAxis(ap=midx[:, 0, t:t + 1], axis=0)).then_inc(mrow_in, 16)
                        pool.indirect_dma_start(
                            out=mk[:, t, :], out_offset=None, in_=k_tab,
                            in_offset=bass.IndirectOffsetOnAxis(ap=midx[:, 1, t:t + 1], axis=0)).then_inc(mrow_in, 16)

            def maxima_vector(dve, nt):
                own = Steps(dve, sem("maxima_dve"))
                dve.sem_inc(msc_used, 1)
                with dve.Fori(0, G) as g:
                    own.loop(g, 3)
                    dve.wait_ge(mrow_in, 32 * T * g + 32 * T)
                    dve.wait_ge(msc_stored, g + 1)
                    own.did(nc.vector.tensor_tensor(mk32, mk[:, :, 0:D], mk[:, :, KW:KW + D], ALU.add))
                    own.wait()
                    own.did(nc.vector.tensor_tensor(mk32, mk32, mk[:, :, 2 * KW:2 * KW + D], ALU.add))
                    own.wait()
                    own.did(nc.vector.tensor_tensor(mk32, mk32, mq[:, :, 0:D], ALU.mult))
                    own.wait()
                    nc.vector.tensor_reduce(msc.rearrange("p h t -> p t h"), mk32.rearrange("p t (h d) -> p t h d", d=DH),
                                            AX.X, ALU.add).then_inc(msc_ready, 1)
                    dve.wait_ge(msc_ready, g + 1)
                    dve.nop(nofuse=True)
                    dve.sem_inc(msc_used, 1)
                own.end(G)
                dve.wait_ge(msc_stored, G + 1)
                nc.vector.memset(mneg, -BIG).then_inc(mneg_ready, 1)
                with dve.Fori(0, 2 * nt) as v:
                    own.loop(v, 4)
                    dve.wait_ge(mv_in, 48 * v + 48)
                    own.did(nc.vector.tensor_scalar(bmask, brow, wnode[:, bass.ds(v, 1)], None, ALU.is_equal))
                    own.wait()
                    own.did(nc.vector.tensor_scalar(bmask, bmask, -1.0, BIG, ALU.add, ALU.mult))
                    own.wait()
                    own.did(nc.vector.tensor_tensor(ball, ball, bmask.unsqueeze(1).broadcast_to([128, H, GE]), ALU.add))
                    own.wait()
                    own.did(nc.vector.tensor_reduce(bmax, ball, AX.X, ALU.max))
                    own.wait()
                    nc.vector.tensor_tensor(mwin, mwin, bmax, ALU.max).then_inc(mwin_ready, 1)
                own.end(2 * nt)
                dve.wait_ge(mall_in, 16)
                own.did(nc.vector.tensor_copy(mparts[:, 0, :, :], mall))
                own.wait()
                own.did(nc.vector.tensor_tensor(mrest, mall, mparts[:, 0, :, :], ALU.subtract))
                own.wait()
                own.did(nc.vector.tensor_copy(mparts[:, 1, :, :], mrest))
                own.wait()
                nc.vector.tensor_tensor(mparts[:, 2, :, :], mrest, mparts[:, 1, :, :], ALU.subtract).then_inc(mparts_ready, 1)
                dve.wait_ge(shifts_out, 48)

            @block.sync
            def _(sp):
                nt = trip_count(sp)
                with sp.If(is_wide(sp)):
                    maxima_sync(sp, nt)
                sp.sem_inc(att_stored, 1)
                sp.wait_ge(zeros, 1)

                def store(v, u):
                    sp.wait_ge(osum_ready, v + 5)
                    sp.nop(nofuse=True)
                    sp.wait_ge(att_out, 16 * (v + 2))
                    sp.nop(nofuse=True)
                    sp.sem_inc(att_stored, 1)
                    w = sp.value_load(wof[0:1, bass.ds(v + 1, 1)], min_val=0, max_val=NWIN * WIN)
                    sp.dma_start(att[bass.ds(w, WIN), :], osum[:, u, :]).then_inc(att_out, 16)

                sp.dma_start(att[0:WIN, :], osum[:, 0, :]).then_inc(att_out, 16)
                def load(v, u):
                        w = sp.value_load(wof[0:1, bass.ds(v + 1, 1)], min_val=0, max_val=NWIN * WIN)
                        g = sp.value_load(gof[0:1, bass.ds(v, 1)], min_val=0, max_val=G - 1)
                        sp.wait_ge(k_ready, seen(v - 2, 3, KEYS_AHEAD))
                        sp.nop(nofuse=True)
                        sp.dma_start(kwin[:, u, :], k_tab[bass.ds(w, WIN), :]).then_inc(kwin_in[u], 16)
                        sp.wait_ge(indT_ready, v + 1)
                        sp.nop(nofuse=True)
                        sp.dma_start(drow[:, u, :], dst16[bass.ds(g, 1), :].rearrange("o e -> (o e)").partition_broadcast(128)
                                     ).then_inc(drow_in[u], 16)

                load(0, 0)
                with sp.Fori(0, nt) as i:
                    for u in range(2):
                        v = 2 * i + u
                        load(v + 1, 1 - u)
                        store(v - 1, 1 - u)
                store(2 * nt - 1, 1)
                sp.wait_ge(drow_in[0], 16 * nt + 16)
                sp.nop(nofuse=True)
                sp.wait_ge(att_out, 32 * nt + 32)
                sp.nop(nofuse=True)

            @block.gpsimd
            def _(pool):
                nt = trip_count(pool)
                with pool.If(is_wide(pool)):
                    maxima_gpsimd(pool)
                pool.wait_ge(zeros, 1)

                def indices(v, u):
                    g = pool.value_load(gof[0:1, bass.ds(v, 1)], min_val=0, max_val=G - 1)
                    pool.wait_ge(k_used, seen(v - 2, 3, SCORES_AHEAD))
                    nc.gpsimd.tensor_copy(idx[:, u, :], srcs[:, bass.ds(g * T, T)]).then_inc(idx_ready, 1)

                indices(0, 0)
                with pool.Fori(0, nt) as i:
                    for u in range(2):
                        v = 2 * i + u
                        pool.wait_ge(idx_ready, v + 1)
                        for t in range(T):
                            if t == 6:
                                indices(v + 1, 1 - u)
                            if t % 2 == 0:
                                pool.wait_ge(agg_done, seen(v - 2, t // 2, SUMMED_AHEAD))
                                pool.nop(nofuse=True)
                            pool.indirect_dma_start(
                                out=rowbuf[:, u * T + t, 0:2 * D], out_offset=None, in_=qv_tab,
                                in_offset=bass.IndirectOffsetOnAxis(ap=idx[:, u, t:t + 1], axis=0)).then_inc(row_in[u * T + t], 16)

            @block.scalar
            def _(act):
                nt = trip_count(act)
                act.sem_inc(exp_done, EXP_AHEAD)
                act.sem_inc(ind_ready, IND_AHEAD)
                act.sem_inc(osum_ready, 3)
                act.wait_ge(zeros, 1)

                def take(v, u):
                    act.wait_ge(win_done, v + 2)
                    act.wait_ge(att_stored, v + 2)
                    nc.scalar.activation(osum[:, u, :], ps[:, 6 + u, 0:AW], ACT.Copy).then_inc(osum_ready, 1)

                def indicators(v, u):
                    for half in range(2):
                        act.wait_ge(turn_ready, 2 * v + half + 1)
                        if half == 0:
                            act.wait_ge(agg_done, seen(v - 2, 3, SUMMED_AHEAD))
                        nc.scalar.activation(ind[:, u, 4 * half:4 * half + 4, :],
                                             ps[0:P, 4 + half, 0:4 * WIN // 2].bitcast(BF16).rearrange("p (t w) -> p t w", w=WIN),
                                             ACT.Copy).then_inc(ind_ready, 1)

                indicators(0, 0)
                with act.Fori(0, nt) as i:
                    for u in range(2):
                        v = 2 * i + u

                        def weights(j):
                            act.wait_ge(k_used, seen(v, j, SCORES_AHEAD))
                            nc.scalar.activation(rowbuf[:, u * T + 2 * j:u * T + 2 * j + 2, 2 * D:2 * D + H], sco[:, 2 * j:2 * j + 2, :], ACT.Exp,
                                                 bias=nbias[0:P, :], scale=SCALE).then_inc(exp_done, 1)

                        for j in range(PAIRS):
                            weights(j)
                            if j == 1:
                                take(v - 1, 1 - u)
                            if j == 2:
                                indicators(v + 1, 1 - u)
                take(2 * nt - 1, 1)

            @block.tensor
            def _(pe):
                nt = trip_count(pe)
                pe.sem_inc(k_ready, KEYS_AHEAD - 1)
                pe.sem_inc(agg_done, SUMMED_AHEAD - PAIRS)
                pe.wait_ge(zeros, 1)

                def turn(v, u, half):
                    pe.wait_ge(ind_ready, 2 * v + half + 1 + IND_AHEAD - 2)
                    tiles = indT[:, u, :].rearrange("p (e t) -> p t e", t=T)
                    for t in range(4):
                        last = nc.tensor.transpose(ps[0:P, 4 + half, t * WIN // 2:(t + 1) * WIN // 2].bitcast(BF16),
                                                   tiles[:, 4 * half + t, :], identb[:, :])
                    last.then_inc(turn_ready, 1)

                for t in (2, 3):
                    last = nc.tensor.matmul(ps[0:P, t, 0:KW], indT[:, 1, 0:P], kwin[:, 1, 0:KW], start=True, stop=True)
                last.then_inc(k_ready, 1)

                def keys(n, v, u, j):
                    if j == 0:
                        pe.wait_ge(kwin_in[u], 16 * n + 16)
                    pe.wait_ge(k_used, seen(v, j - 2, SCORES_AHEAD))
                    tiles = indT[:, u, :].rearrange("p (e t) -> p t e", t=T)
                    for t in (2 * j, 2 * j + 1):
                        for c in range(3):
                            last = nc.tensor.matmul(ps[0:P, t % 4, 0:KW], tiles[:, t, :], kwin[:, u, c * KW:(c + 1) * KW],
                                                    start=(c == 0), stop=(c == 2))
                    last.then_inc(k_ready, 1)

                def add_up(v, u, j):
                    pe.wait_ge(w_ready, seen(v, j, WEIGHTED_AHEAD))
                    pe.wait_ge(ind_ready, 2 * v + j // 2 + 1 + IND_AHEAD)
                    if j == 0:
                        pe.wait_ge(osum_ready, v + 3)
                    for t in (2 * j, 2 * j + 1):
                        last = nc.tensor.matmul(ps[:, 6 + u, 0:AW], ind[:, u, t, :], rowbuf[:, u * T + t, D:2 * D + H],
                                                start=(t == 0), stop=False)
                    last.then_inc(agg_done, 1)

                def carry(v, u):
                    pe.wait_ge(osum_ready, v + 4)
                    pe.wait_ge(car_ready, v + 2)
                    nc.tensor.matmul(ps[:, 6 + u, 0:AW], car[:, u, :], osum[:, 1 - u, :], start=False, stop=True).then_inc(win_done, 1)

                def across(n, v, u):
                    pe.wait_ge(indT_ready, v + 3)
                    turn(v, u, 0)
                    turn(v, u, 1)
                    keys(n, v, u, 0)
                    add_up(v - 1, 1 - u, 2)
                    keys(n, v, u, 1)
                    add_up(v - 1, 1 - u, 3)
                    carry(v - 1, 1 - u)

                add_up(-1, 1, 0)
                add_up(-1, 1, 1)
                across(0, 0, 0)
                with pe.Fori(0, nt) as i:
                    for u in range(2):
                        v = 2 * i + u
                        keys(i, v, u, 2)
                        add_up(v, u, 0)
                        keys(i, v, u, 3)
                        add_up(v, u, 1)
                        across(i + u, v + 1, 1 - u)

            @block.vector
            def _(dve):
                nt = trip_count(dve)
                with dve.If(is_wide(dve)):
                    maxima_vector(dve, nt)
                own = Steps(dve, sem("edge_dve"))
                dve.sem_inc(k_used, SCORES_AHEAD - 1)
                dve.sem_inc(w_ready, WEIGHTED_AHEAD - 1)
                dve.sem_inc(indT_ready, 2)
                own.did(nc.vector.memset(rowbuf[:, T:2 * T, :], 0.0))
                own.did(nc.vector.memset(ind[:, 1, :, :], 0.0))
                own.did(nc.vector.memset(osum, 0.0))
                own.did(nc.vector.memset(sco, 0.0))
                own.did(nc.vector.memset(indT[:, 1, :], 0.0))
                own.did(nc.vector.memset(kwin[:, 1, :], 0.0))
                nc.vector.memset(car[:, 1, :], 0.0).then_inc(car_ready, 1)
                own.wait()
                dve.sem_inc(zeros, 1)
                def to_window(n, v, u):
                    dve.wait_ge(drow_in[u], 16 * n + 16)
                    dve.wait_ge(k_ready, seen(v - 2, 3, KEYS_AHEAD))
                    nc.vector.tensor_scalar(indT[:, u, :], drow[:, u, :], wnode[:, bass.ds(v, 1)], None,
                                            ALU.is_equal).then_inc(indT_ready, 1)

                def shift(j, reduced):
                    bank = 2 * (j % 2)
                    dve.wait_ge(own.sem, reduced)
                    nc.vector.tensor_tensor(sco[:, 2 * j:2 * j + 2, :], sco[:, 2 * j:2 * j + 2, :],
                                            ps[0:P, bank:bank + 2, D:KW], ALU.subtract).then_inc(k_used, 1)

                dve.wait_ge(k_ready, seen(-1, 3, KEYS_AHEAD))
                to_window(0, 0, 0)
                with dve.Fori(0, nt) as i:
                    own.loop(i, 2 * 2 * PAIRS)
                    for u in range(2):
                        v = 2 * i + u

                        def weigh(v, u, j):
                            dve.wait_ge(exp_done, seen(v, j, EXP_AHEAD))
                            b = rowbuf[:, u * T + 2 * j:u * T + 2 * j + 2, :]
                            vals = b[:, :, D:2 * D].rearrange("p t (h d) -> p t h d", d=DH)
                            nc.vector.tensor_tensor(vals, vals, b[:, :, 2 * D:2 * D + H].unsqueeze(3).broadcast_to([P, 2, H, DH]),
                                                    ALU.mult).then_inc(w_ready, 1)

                        for j in range(PAIRS):
                            b = rowbuf[:, u * T + 2 * j:u * T + 2 * j + 2, :]
                            for t in (2 * j, 2 * j + 1):
                                dve.wait_ge(row_in[u * T + t], 16 * i + 16)
                            dve.wait_ge(k_ready, seen(v, j, KEYS_AHEAD))
                            bank = 2 * (j % 2)
                            reduced = own.base + own.n
                            own.did(nc.vector.tensor_tensor(b[:, :, 0:D], b[:, :, 0:D], ps[0:P, bank:bank + 2, 0:D], ALU.mult))
                            shift((j - 1) % PAIRS, reduced)
                            if j == 0:
                                nc.vector.tensor_scalar(car[:, u, :], iotaj[:, :], wcar[:, bass.ds(v, 1)], None,
                                                        ALU.is_equal).then_inc(car_ready, 1)
                            own.wait()
                            own.did(nc.vector.tensor_reduce(sco[:, 2 * j:2 * j + 2, :],
                                                            b[:, :, 0:D].rearrange("p t (h d) -> p t h d", d=DH), AX.X, ALU.add))
                            if j == 0:
                                weigh(v - 1, 1 - u, 3)
                            else:
                                weigh(v, u, j - 1)
                            if j == 1:
                                to_window(i + u, v + 1, 1 - u)
                own.end(nt)
                shift(PAIRS - 1, own.n)
                dve.wait_ge(exp_done, seen(2 * nt - 1, 3, EXP_AHEAD))
                b = rowbuf[:, 2 * T - 2:2 * T, :]
                vals = b[:, :, D:2 * D].rearrange("p t (h d) -> p t h d", d=DH)
                nc.vector.tensor_tensor(vals, vals, b[:, :, 2 * D:2 * D + H].unsqueeze(3).broadcast_to([P, 2, H, DH]),
                                        ALU.mult).then_inc(w_ready, 1)

        with nc.Block() as block:
            cut = carve()
            sums = cut([NBLK, AW], parts=P)
            yn = cut([CH, D], parts=P)
            yT = cut([2, CH * P])
            gT = cut([FF // 128, CH * P])
            h1T = cut([2, 2, P])
            h1s = cut([CH, D], parts=P)
            msg = cut([2, R * D], parts=P)
            rec = cut([CH, H], parts=P)
            vv = cut([6, CH], parts=P)
            att_in = sem("att_in")
            x1_ready, x_ready, yn_ready = sem("x1_ready"), sem("x_ready"), sem("yn_ready")
            t_psum, yT_ready = sem("turned"), sem("yT_ready")
            hid_psum, hid_ready = sem("hidden_psum"), sem("hidden_ready")
            ff_psum, ff_taken = sem("ff_psum"), sem("ff_taken")
            st_ready, h1_ready = sem("x2_statistics"), sem("h1_ready")
            h1t_psum, h1T_ready = sem("h1_turned"), sem("h1T_ready")
            msg_psum, msg_a, msg_v = sem("msg_psum"), sem("msg_by_act"), sem("msg_by_dve")
            loop_psum, loop_taken = sem("loop_psum"), sem("loop_taken")
            msg_out, msg_stored = sem("msg_out"), sem("msg_stored")
            PARTS = ((0, 3 * P), (3 * P, 2 * P))
            NPROD = FF // 128 * len(PARTS)
            hall_v = h_all.rearrange("(n r) d -> n (r d)", r=R)

            def rsqrt(own, var, r, t):
                own.did(nc.vector.tensor_scalar(t.bitcast(I32), var.bitcast(I32), 1, None, ALU.logical_shift_right))
                own.wait()
                own.did(nc.vector.tensor_scalar(r.bitcast(I32), t.bitcast(I32), -1.0, float(0x5F3759DF), ALU.mult, ALU.add))
                own.wait()
                for _ in range(3):
                    own.did(nc.vector.tensor_tensor(t, r, r, ALU.mult))
                    own.wait()
                    own.did(nc.vector.tensor_tensor(t, t, var, ALU.mult))
                    own.wait()
                    own.did(nc.vector.tensor_scalar(t, t, -0.5, 1.5, ALU.mult, ALU.add))
                    own.wait()
                    own.did(nc.vector.tensor_tensor(r, r, t, ALU.mult))
                    own.wait()
            MID_STEPS = 2 + CH + 2 * CH + 1 + 14 + CH * (3 + 14)


            @block.sync
            def _(sp):
                for c in range(NCH):
                    sp.dma_start(sums[:, c * CH:(c + 1) * CH, :],
                                 att[c * CH * P:(c + 1) * CH * P, :].rearrange("(b p) d -> p b d", p=P)).then_inc(att_in, 16)
                    sp.wait_ge(att_in, 16 * c + 16)
                with sp.Fori(0, NCH) as i:
                    for j in range(CH):
                        b = i * CH + j
                        sp.wait_ge(msg_a, 2 * b + 4)
                        sp.nop(nofuse=True)
                        sp.wait_ge(msg_v, 2 * b + 4)
                        sp.nop(nofuse=True)
                        sp.dma_start(hall_v[bass.ds(b * P, P), :], msg[:, j % 2, :]).then_inc(msg_out, 16)
                        sp.wait_ge(msg_out, 16 * b + 16)
                        sp.nop(nofuse=True)
                        sp.sem_inc(msg_stored, 1)

            @block.gpsimd
            def _(pool):
                own = Steps(pool, sem("mid_pool"))

                def residual(i):
                    for j in range(CH):
                        x_b = xs[:, bass.ds((i * CH + j) * D, D)]
                        pool.wait_ge(x1_ready, i * CH + j + 1)
                        pool.nop(nofuse=True)
                        own.did(nc.gpsimd.tensor_tensor(x_b, x_b, hs[:, bass.ds((i * CH + j) * D, D)], ALU.add))
                        own.wait()
                        pool.nop(nofuse=True)
                        nc.gpsimd.tensor_tensor(x_b, x_b, rowb[:, 0, :], ALU.add).then_inc(x_ready, 1)

                def biased(i):
                    for j in range(CH):
                        h_b = hs[:, bass.ds((i * CH + j) * D, D)]
                        pool.wait_ge(loop_taken, i * CH + j + 3)
                        pool.nop(nofuse=True)
                        nc.gpsimd.tensor_tensor(h_b, h_b, rowb[:, 1, :], ALU.add)

                residual(0)
                with pool.Fori(0, NCH - 1) as i:
                    own.loop(i, CH)
                    residual(i + 1)
                    biased(i)
                own.end(NCH - 1)
                biased(NCH - 1)

            @block.scalar
            def _(act):
                act.sem_inc(hid_ready, 2)
                act.sem_inc(msg_a, 2)

                def y_features(i, j):
                    act.wait_ge(t_psum, 2 * (i * CH + j) + 3)
                    for k in range(2):
                        nc.scalar.activation(yT[:, k, j * P:(j + 1) * P], ps[:, j % 2, D + k * P:D + k * P + P], ACT.Identity,
                                             bias=cols[:, 3, k:k + 1], scale=cols[:, 2, k:k + 1]).then_inc(yT_ready, 1)

                def chunk(i, last):
                    for f in range(FF // 128):
                        for m, (c, n) in enumerate(PARTS):
                            act.wait_ge(hid_psum, i * NPROD + 2 * f + m + 1)
                            nc.scalar.activation(gT[:, f, c:c + n], ps[:, 2 + m, 0:n], ACT.Gelu,
                                                 bias=bin_[:, f:f + 1]).then_inc(hid_ready, 1)
                    for j in range(CH):
                        b = i * CH + j
                        o = b * D
                        act.wait_ge(st_ready, b + 1)
                        nc.scalar.activation(h1s[:, j, :], xs[:, bass.ds(o, D)], ACT.Relu,
                                             bias=nmb[:, j:j + 1], scale=rsb[:, j:j + 1]).then_inc(h1_ready, 1)
                        act.wait_ge(h1t_psum, 2 * b + 2)
                        if not last:
                            act.wait_ge(t_psum, 2 * (b + CH) + 3)
                        nc.scalar.activation(h1T[:, j % 2, :, :], ps[:, j % 2, 0:2 * P].rearrange("p (k n) -> p k n", k=2),
                                             ACT.Copy).then_inc(h1T_ready, 1)
                        if not last:
                            y_features(i + 1, j)
                        act.wait_ge(msg_stored, b + (2 if j == 0 else 1))
                        for c in range(2):
                            act.wait_ge(msg_psum, 4 * b + c + 1)
                            nc.scalar.activation(msg[:, j % 2, c * 512:(c + 1) * 512], ps[0:P, 2 + c, :],
                                                 ACT.Copy).then_inc(msg_a, 1)

                for j in range(CH):
                    y_features(0, j)
                with act.Fori(0, NCH - 1) as i:
                    chunk(i, False)
                chunk(NCH - 1, True)

            @block.tensor
            def _(pe):
                def turn_y(i, j):
                    pe.wait_ge(yn_ready, i * CH + j + 1)
                    for k in range(2):
                        nc.tensor.transpose(ps[:, j % 2, D + k * P:D + k * P + P], yn[:, j, k * 128:k * 128 + 128],
                                            ident[0:P, 0:P]).then_inc(t_psum, 1)

                def hidden(i):
                    pe.wait_ge(yT_ready, 2 * CH * i + 2 * CH)
                    pe.wait_ge(msg_a, 2 * CH * i + 2)
                    for f in range(FF // 128):
                        for m, (c, n) in enumerate(PARTS):
                            pe.wait_ge(hid_ready, i * NPROD + 2 * f + m + 1)
                            for k in range(2):
                                last = nc.tensor.matmul(ps[:, 2 + m, 0:n], win[:, k, f * 128:(f + 1) * 128], yT[:, k, c:c + n],
                                                        start=(k == 0), stop=(k == 1))
                            last.then_inc(hid_psum, 1)

                def feed(i, j):
                    b = i * CH + j
                    pe.wait_ge(hid_ready, i * NPROD + NPROD + 2)
                    pe.wait_ge(ff_taken, b + (2 if j == 0 else 1))
                    for f in range(FF // 128):
                        last = nc.tensor.matmul(ps[0:P, 4 + j % 2, 0:D], gT[:, f, j * P:(j + 1) * P], wout[:, f, :],
                                                start=(f == 0), stop=(f == FF // 128 - 1))
                    last.then_inc(ff_psum, 1)

                def turn(i, j, last):
                    b = i * CH + j
                    pe.wait_ge(h1_ready, b + 1)
                    pe.wait_ge(loop_taken, b + (2 if j == 0 else 1))
                    for k in range(2):
                        nc.tensor.transpose(ps[:, j % 2, k * P:k * P + P], h1s[:, j, k * 128:k * 128 + 128],
                                            ident[0:P, 0:P]).then_inc(h1t_psum, 1)
                    if not last:
                        turn_y(i + 1, j)

                def messages(i, j, last):
                    b = i * CH + j
                    pe.wait_ge(h1T_ready, b + 1)
                    for c in range(4):
                        pe.wait_ge(msg_a if c < 2 else msg_v, 2 * b + c % 2 + 1)
                        for k in range(2):
                            prod = nc.tensor.matmul(ps[0:P, (2, 3, 6, 7)[c], :], h1T[:, j % 2, k, :],
                                                    wrel[:, k, c * 512:(c + 1) * 512], start=(k == 0), stop=(k == 1))
                        prod.then_inc(msg_psum, 1)
                    if not last:
                        pe.wait_ge(yT_ready, 2 * (b + CH) + 2)
                    for k in range(2):
                        prod = nc.tensor.matmul(ps[0:P, j % 2, 0:D], h1T[:, j % 2, k, :], wloop[:, k, :],
                                                start=(k == 0), stop=(k == 1))
                    prod.then_inc(loop_psum, 1)

                def chunk(i, last):
                    hidden(i)
                    for j in range(CH + 2):
                        if j >= 2:
                            turn(i, j - 2, last)
                        if j < CH:
                            feed(i, j)
                        if j >= 2:
                            messages(i, j - 2, last)

                pe.wait_ge(loop_taken, 2)
                for j in range(CH):
                    if j >= 2:
                        pe.wait_ge(yT_ready, 2 * j - 2)
                    turn_y(0, j)
                with pe.Fori(0, NCH - 1) as i:
                    chunk(i, False)
                chunk(NCH - 1, True)

            @block.vector
            def _(dve):
                own = Steps(dve, sem("mid_dve"))
                dve.sem_inc(ff_taken, 2)
                dve.sem_inc(loop_taken, 2)
                dve.sem_inc(t_psum, 1)
                dve.sem_inc(msg_v, 2)
                dve.sem_inc(msg_stored, 2)
                def prepare(i):
                    dve.wait_ge(att_in, 16 * i + 16)
                    s_c = sums[:, bass.ds(i * CH, CH), :]
                    own.did(nc.vector.tensor_scalar(rec, s_c[:, :, D:AW], TINY, None, ALU.max))
                    own.wait()
                    own.did(nc.vector.reciprocal(rec, rec))
                    own.wait()
                    for j in range(CH):
                        s_j = sums[:, bass.ds(i * CH + j, 1), 0:D].rearrange("p o (h d) -> p (o h) d", d=DH)
                        own.did(nc.vector.tensor_tensor(s_j, s_j, rec[:, j, :].unsqueeze(2).broadcast_to([P, H, DH]), ALU.mult))
                    own.wait()
                    for j in range(CH):
                        s_j = sums[:, bass.ds(i * CH + j, 1), 0:D].rearrange("p o d -> p (o d)")
                        h_j = hs[:, bass.ds((i * CH + j) * D, D)]
                        nc.vector.tensor_tensor(h_j, h_j, s_j, ALU.add).then_inc(x1_ready, 1)
                    for j in range(CH):
                        dve.wait_ge(x1_ready, i * CH + j + 1)
                        dve.nop(nofuse=True)
                        own.did(nc.vector.bn_stats(st6[:, j, :], hs[:, bass.ds((i * CH + j) * D, D)]))
                    own.wait()
                    dve.nop(nofuse=True)
                    for j in range(CH):
                        own.did(nc.vector.bn_aggr(mv[:, j, :], st6[:, j, :]))
                    own.wait()
                    own.did(nc.vector.tensor_scalar(vv[:, 0, :], mv[:, :, 1], EPS, None, ALU.add))
                    own.wait()
                    rsqrt(own, vv[:, 0, :], rs[:, :], vv[:, 1, :])
                    dve.wait_ge(t_psum, 2 * CH * i + 1)
                    for j in range(CH):
                        nc.vector.tensor_scalar(yn[:, j, :], hs[:, bass.ds((i * CH + j) * D, D)], mv[:, j, 0:1], rs[:, j:j + 1],
                                                ALU.subtract, ALU.mult).then_inc(yn_ready, 1)

                def finish(i):
                    for j in range(CH + 2):
                        b = i * CH + j
                        if j < CH:
                            x_b = xs[:, bass.ds(b * D, D)]
                            dve.wait_ge(ff_psum, b + 1)
                            dve.wait_ge(x_ready, b + 1)
                            nc.vector.tensor_tensor(x_b, x_b, ps[0:P, 4 + j % 2, 0:D], ALU.add).then_inc(ff_taken, 1)
                            dve.wait_ge(ff_taken, b + 3)
                            dve.nop(nofuse=True)
                            own.did(nc.vector.bn_stats(st6b[:, j, :], x_b))
                            own.wait()
                            dve.nop(nofuse=True)
                            own.did(nc.vector.bn_aggr(mvb[:, j, :], st6b[:, j, :]))
                            own.wait()
                            own.did(nc.vector.tensor_scalar(vv[:, 2, j:j + 1], mvb[:, j, 1:2], EPS, None, ALU.add))
                            own.wait()
                            rsqrt(own, vv[:, 2, j:j + 1], rsb[:, j:j + 1], vv[:, 3, j:j + 1])
                            nc.vector.scalar_tensor_tensor(out=nmb[:, j:j + 1], in0=mvb[:, j, 0:1], scalar=-1.0, in1=rsb[:, j:j + 1],
                                                           op0=ALU.mult, op1=ALU.mult).then_inc(st_ready, 1)
                        if j >= 2:
                            h_b = hs[:, bass.ds((b - 2) * D, D)]
                            dve.wait_ge(msg_stored, b - 2 + (2 if j == 2 else 1))
                            for c in range(2, 4):
                                dve.wait_ge(msg_psum, 4 * (b - 2) + c + 1)
                                nc.vector.tensor_copy(msg[:, j % 2, c * 512:(c + 1) * 512],
                                                      ps[0:P, 4 + c, :]).then_inc(msg_v, 1)
                            dve.wait_ge(loop_psum, b - 1)
                            nc.vector.tensor_tensor(h_b, h1s[:, j - 2, :], ps[0:P, j % 2, 0:D], ALU.add).then_inc(loop_taken, 1)

                prepare(0)
                with dve.Fori(0, NCH - 1) as i:
                    own.loop(i, MID_STEPS)
                    prepare(i + 1)
                    finish(i)
                own.end(NCH - 1)
                finish(NCH - 1)

        with nc.Block() as block:
            cut = carve()
            rowbuf = cut([2 * T, D], parts=P)
            ind = cut([2, T, WIN], parts=P)
            dl = cut([2, T], parts=P)
            car = cut([2, WIN])
            osum = cut([2, D])
            idx = cut([2, T], I32, parts=P)
            row_in = [sem(f"message_in{t}") for t in range(2 * T)]
            dl_ready, ind_ready, car_ready, agg_done = sem("dl_ready"), sem("ind1_ready"), sem("car1_ready"), sem("summed1")
            win_done, osum_ready = sem("window1_done"), sem("osum1_ready")
            rel_out, rel_stored, idx_ready, zeros = sem("rel_out"), sem("rel_stored"), sem("idx1_ready"), sem("zeros1_ready")

            @block.sync
            def _(sp):
                nt = trip_count(sp)
                sp.sem_inc(rel_stored, 1)
                sp.wait_ge(zeros, 1)
                sp.dma_start(rel[0:WIN, :], osum[:, 1, :]).then_inc(rel_out, 16)
                with sp.Fori(0, nt) as i:
                    for u in range(2):
                        v = 2 * i + u
                        sp.wait_ge(osum_ready, v + 3)
                        sp.nop(nofuse=True)
                        sp.wait_ge(rel_out, 16 * (v + 1))
                        sp.nop(nofuse=True)
                        sp.sem_inc(rel_stored, 1)
                        w = sp.value_load(wof[0:1, bass.ds(v + 1, 1)], min_val=0, max_val=NWIN * WIN)
                        sp.dma_start(rel[bass.ds(w, WIN), :], osum[:, u, :]).then_inc(rel_out, 16)
                sp.wait_ge(rel_out, 32 * nt + 16)
                sp.nop(nofuse=True)

            @block.gpsimd
            def _(pool):
                nt = trip_count(pool)

                def indices(v, u):
                    g = pool.value_load(gof[0:1, bass.ds(v, 1)], min_val=0, max_val=G - 1)
                    pool.wait_ge(agg_done, 4 * v + 4)
                    nc.gpsimd.tensor_copy(idx[:, u, :], typs[:, bass.ds(g * T, T)]).then_inc(idx_ready, 1)

                indices(0, 0)
                with pool.Fori(0, nt) as i:
                    for u in range(2):
                        v = 2 * i + u
                        pool.wait_ge(idx_ready, v + 1)
                        for t in range(T):
                            if t == 6:
                                indices(v + 1, 1 - u)
                            if t % 2 == 0:
                                pool.wait_ge(agg_done, 4 * v + t // 2 + 1)
                                pool.nop(nofuse=True)
                            pool.indirect_dma_start(
                                out=rowbuf[:, u * T + t, :], out_offset=None, in_=h_all,
                                in_offset=bass.IndirectOffsetOnAxis(ap=idx[:, u, t:t + 1], axis=0)).then_inc(row_in[u * T + t], 16)

            @block.scalar
            def _(act):
                nt = trip_count(act)
                act.sem_inc(osum_ready, 2)
                with act.Fori(0, nt) as i:
                    for u in range(2):
                        v = 2 * i + u
                        act.wait_ge(win_done, v + 1)
                        act.wait_ge(rel_stored, v + 1)
                        nc.scalar.activation(osum[:, u, :], ps[:, 6 + u, 0:D], ACT.Copy).then_inc(osum_ready, 1)

            @block.tensor
            def _(pe):
                nt = trip_count(pe)
                pe.sem_inc(agg_done, 8)
                pe.wait_ge(zeros, 1)
                with pe.Fori(0, nt) as i:
                    for u in range(2):
                        v = 2 * i + u
                        pe.wait_ge(ind_ready, v + 1)
                        pe.wait_ge(osum_ready, v + 1)
                        for t in range(T):
                            pe.wait_ge(row_in[u * T + t], 16 * i + 16)
                            last = nc.tensor.matmul(ps[:, 6 + u, 0:D], ind[:, u, t, :], rowbuf[:, u * T + t, :],
                                                    start=(t == 0), stop=False)
                            if t % 2:
                                last.then_inc(agg_done, 1)
                        pe.wait_ge(osum_ready, v + 2)
                        pe.wait_ge(car_ready, v + 1)
                        nc.tensor.matmul(ps[:, 6 + u, 0:D], car[:, u, :], osum[:, 1 - u, :], start=False, stop=True).then_inc(win_done, 1)

            @block.vector
            def _(dve):
                nt = trip_count(dve)
                own = Steps(dve, sem("edge1_dve"))
                own.did(nc.vector.memset(osum, 0.0))
                own.wait()
                dve.sem_inc(zeros, 1)
                with dve.Fori(0, nt) as i:
                    for u in range(2):
                        v = 2 * i + u
                        g = dve.value_load(gof[0:1, bass.ds(v, 1)], min_val=0, max_val=G - 1)
                        dve.wait_ge(agg_done, 4 * v + 4)
                        dve.wait_ge(osum_ready, v + 1)
                        nc.vector.tensor_scalar(dl[:, u, :], dstf[:, bass.ds(g * T, T)], wst[0:P, bass.ds(v, 1)], None,
                                                ALU.subtract).then_inc(dl_ready, 1)
                        nc.vector.tensor_scalar(car[:, u, :], iotaj[:, :], wcar[:, bass.ds(v, 1)], None,
                                                ALU.is_equal).then_inc(car_ready, 1)
                        dve.wait_ge(dl_ready, v + 1)
                        for t in range(T):
                            last = nc.vector.tensor_scalar(ind[:, u, t, :], iotaj[0:P, :], dl[:, u, t:t + 1], None, ALU.is_equal)
                        last.then_inc(ind_ready, 1)

        with nc.Block() as block:
            cut = carve()
            z = cut([NBLK * D], parts=P)
            vv = cut([2, CH], parts=P)
            rel_in, z_ready, g_ready, n_ready, o_ready, out_sem = (
                sem(n) for n in ("rel_in", "z_ready", "gelu_ready", "normed_ready", "result_ready", "result_out"))

            @block.sync
            def _(sp):
                for c in range(NCH):
                    sp.dma_start(z[:, c * CH * D:(c + 1) * CH * D].rearrange("p (b d) -> p b d", d=D),
                                 rel[c * CH * P:(c + 1) * CH * P, :].rearrange("(b p) d -> p b d", p=P)).then_inc(rel_in, 16)
                    sp.wait_ge(rel_in, 16 * c + 16)
                with sp.Fori(0, NCH) as i:
                    for j in range(CH):
                        b = i * CH + j
                        sp.wait_ge(o_ready, b + 1)
                        sp.nop(nofuse=True)
                        sp.dma_start(out[bass.ds(b * P, P), :], z[:, bass.ds(b * D, D)]).then_inc(out_sem, 16)
                sp.wait_ge(out_sem, 16 * NBLK)

            @block.gpsimd
            def _(pool):
                own = Steps(pool, sem("last_pool"))
                with pool.Fori(0, NCH) as i:
                    own.loop(i, CH)
                    for j in range(CH):
                        b = i * CH + j
                        z_b = z[:, bass.ds(b * D, D)]
                        pool.wait_ge(n_ready, b + 1)
                        pool.nop(nofuse=True)
                        own.did(nc.gpsimd.tensor_tensor(z_b, z_b, rowb[:, 3, :], ALU.add))
                        own.wait()
                        pool.nop(nofuse=True)
                        nc.gpsimd.tensor_tensor(z_b, z_b, xs[:, bass.ds(b * D, D)], ALU.add).then_inc(o_ready, 1)

            @block.scalar
            def _(act):
                with act.Fori(0, NCH) as i:
                    for j in range(CH):
                        b = i * CH + j
                        z_b = z[:, bass.ds(b * D, D)]
                        act.wait_ge(z_ready, b + 1)
                        nc.scalar.activation(z_b, z_b, ACT.Gelu).then_inc(g_ready, 1)

            @block.vector
            def _(dve):
                own = Steps(dve, sem("last_dve"))
                with dve.Fori(0, NCH) as i:
                    dve.wait_ge(rel_in, 16 * i + 16)
                    for j in range(CH):
                        z_b = z[:, bass.ds((i * CH + j) * D, D)]
                        nc.vector.tensor_tensor(z_b, z_b, hs[:, bass.ds((i * CH + j) * D, D)], ALU.add).then_inc(z_ready, 1)
                with dve.Fori(0, NCH) as i:
                    own.loop(i, 2 * CH + 1 + 14 + CH)
                    for j in range(CH):
                        dve.wait_ge(g_ready, i * CH + j + 1)
                        dve.nop(nofuse=True)
                        own.did(nc.vector.bn_stats(st6[:, j, :], z[:, bass.ds((i * CH + j) * D, D)]))
                    own.wait()
                    dve.nop(nofuse=True)
                    for j in range(CH):
                        own.did(nc.vector.bn_aggr(mv[:, j, :], st6[:, j, :]))
                    own.wait()
                    own.did(nc.vector.tensor_scalar(vv[:, 0, :], mv[:, :, 1], EPS, None, ALU.add))
                    own.wait()
                    rsqrt(own, vv[:, 0, :], rs[:, :], vv[:, 1, :])
                    for j in range(CH):
                        z_b = z[:, bass.ds((i * CH + j) * D, D)]
                        own.did(nc.vector.tensor_scalar(z_b, z_b, mv[:, j, 0:1], rs[:, j:j + 1], ALU.subtract, ALU.mult))
                    own.wait()
                    for j in range(CH):
                        z_b = z[:, bass.ds((i * CH + j) * D, D)]
                        nc.vector.tensor_tensor(z_b, z_b, rowb[:, 2, :], ALU.mult).then_inc(n_ready, 1)


_INS = ['x', 'src', 'dst', 'edge_type_8', 'L0_gnn_Wqkv', 'L0_gnn_bqkv', 'L0_gnn_ln_attn_g', 'L0_gnn_ln_attn_b',
        'L0_gnn_ln_res_g', 'L0_gnn_ln_res_b', 'L0_gnn_W_in', 'L0_gnn_b_in', 'L0_gnn_W_out', 'L0_gnn_b_out',
        'L1_gnn_basis', 'L1_gnn_comp', 'L1_gnn_loop_w', 'L1_gnn_h_bias', 'L1_gnn_ln_gamma', 'L1_gnn_ln_beta']


def kernel(**inputs):
    import numpy as _np
    import concourse.bacc as _bacc
    from concourse import mybir as _mybir
    from concourse.bass_utils import run_bass_kernel_spmd as _run

    nc = _bacc.Bacc("TRN2", target_bir_lowering=False, num_devices=1)
    arrays, args = {}, []
    for name in _INS:
        a = _np.ascontiguousarray(inputs[name])
        arrays[f"in_{name}"] = a
        args.append(nc.dram_tensor(f"in_{name}", a.shape, _mybir.dt.from_np(a.dtype), kind="ExternalInput").ap())
    o = nc.dram_tensor("out", (N, D), _mybir.dt.float32, kind="ExternalOutput").ap()
    program(nc, *args, o)
    r = _run(nc, [arrays], core_ids=[0])
    return r.results[0]["out"]
```

```python
import concourse.bass as bass
from concourse import mybir
from contextlib import ExitStack

FP32 = mybir.dt.float32
BF16 = mybir.dt.bfloat16
I32 = mybir.dt.int32
I16 = mybir.dt.int16
ALU = mybir.AluOpType
ACT = mybir.ActivationFunctionType
AX = mybir.AxisListType
RMAX = bass.bass_isa.ReduceOp.max

N, D = 3125, 256
E = 50000
H = 8
DH = D // H
FF = 4 * D
R, NB = 8, 4
EPS = 1e-5
SCALE = float(D) ** -0.5
P = 125
NBLK = N // P
CH = 5
NCH = NBLK // CH
T = 8
PAIRS = T // 2
GE = P * T
G = E // GE
WIN = 128
NWIN = -(-N // WIN)
VMAX = G * NWIN
VTAB = G * (NWIN + 1)
AWORDS = 21380
KW = D + H
AW = D + H
RP = 5
NPAD = N + 3 * P
TINY = 1e-37
WIDE = 40.0
BIG = 1e30


class Steps:

    def __init__(self, eng, sem):
        self.eng, self.sem, self.n, self.base = eng, sem, 0, 0

    def did(self, ins):
        self.n += 1
        return ins.then_inc(self.sem, 1)

    def loop(self, i, per):
        self.per, self.first, self.i = per, self.n, i
        self.base = i * per

    def end(self, trips):
        assert self.n - self.first == self.per, (self.n - self.first, self.per)
        self.base = 0
        self.n = self.first + self.per * trips

    def wait(self):
        self.eng.wait_ge(self.sem, self.base + self.n)


def program(nc, x, src, dst, edge_type, Wqkv, bqkv, ga, ba, gr, br, W_in, b_in, W_out, b_out,
            basis, comp, loop_w, h_bias, gamma, beta, out):
    qv_tab = nc.dram_tensor("qv_tab", (N, 2 * D), FP32).ap()
    k_tab = nc.dram_tensor("k_tab", (NPAD, 3 * KW), BF16).ap()
    dst16 = nc.dram_tensor("dst16", (G, GE), I16).ap()
    bounds = nc.dram_tensor("bounds", (G, 2), FP32).ap()
    att = nc.dram_tensor("att", (NPAD, AW), FP32).ap()
    s_tab = nc.dram_tensor("s_tab", (G, H, GE), FP32).ap()
    m_tab = nc.dram_tensor("m_tab", (NPAD, H), FP32).ap()
    rel = nc.dram_tensor("rel", (NPAD, D), FP32).ap()
    h_all = nc.dram_tensor("h_all", (N * R, D), FP32).ap()

    x_v = x.rearrange("(b p) d -> p b d", p=P)
    out_v = out.rearrange("(b p) d -> p b d", p=P)
    ctx = ExitStack()
    with ctx:
        def sb(name, shape, dt=FP32):
            return ctx.enter_context(nc.sbuf_tensor(name, shape, dt))

        def sem(name):
            return ctx.enter_context(nc.semaphore(name))

        ps = ctx.enter_context(nc.psum_tensor("ps", [128, 8, 512], FP32))
        xs = sb("xs", [P, NBLK * D])
        hs = sb("hs", [P, NBLK * D])
        srcs = sb("srcs", [P, G * T], I32)
        dsti = sb("dsti", [P, G * T], I32)
        typs = sb("typs", [P, G * T], I32)
        dstf = sb("dstf", [P, G * T])
        gof = sb("gof", [1, VTAB], I32)
        wof = sb("wof", [128, VTAB + 1], I32)
        wnode = sb("wnode", [128, VTAB])
        wcar = sb("wcar", [128, VTAB])
        wst = sb("wst", [128, VTAB])
        bnd = sb("bnd", [128, G, 2])
        flg = sb("flg", [128, 8])
        trips = sb("trips", [128, 2], I32)
        wide = trips[:, 1:2]
        iotap = sb("iotap", [128, 1])
        iotai = sb("iotai", [128, 128], I32)
        iotaj = sb("iotaj", [128, 128])
        ident = sb("ident", [128, 128])
        identb = sb("identb", [128, 128], BF16)
        win = sb("win", [128, 2, FF])
        wout = sb("wout", [128, FF // 128, D])
        wrel = sb("wrel", [128, 2, R * D])
        wloop = sb("wloop", [128, 2, D])
        cmpb = sb("cmpb", [128, R * NB])
        cols = sb("cols", [128, 4, 2])
        bin_ = sb("bin_", [128, FF // 128])
        rowb = sb("rowb", [P, 4, D])
        st6 = sb("st6", [P, CH, 6])
        mv = sb("mv", [P, CH, 2])
        rs = sb("rs", [P, CH])
        nm = sb("nm", [P, CH])
        st6b = sb("st6b", [P, CH, 6])
        mvb = sb("mvb", [P, CH, 2])
        rsb = sb("rsb", [P, CH])
        nmb = sb("nmb", [P, CH])
        nrm = sb("nrm", [P, 2, NBLK])
        nmx = sb("nmx", [128, 2])
        nmr = sb("nmr", [128, 2])
        nbias = sb("nbias", [128, 1])
        A = sb("arena", [128, AWORDS])

        def carve():
            at = [0]

            def cut(shape, dt=FP32, parts=128):
                n = 1
                for s in shape:
                    n *= s
                words = n if dt in (FP32, I32) else (n + 1) // 2
                v = A[0:parts, at[0]:at[0] + words]
                at[0] += words
                assert at[0] <= AWORDS, at[0]
                if dt != FP32:
                    v = v.bitcast(dt)
                if len(shape) == 1:
                    return v
                names = "abcd"[:len(shape)]
                pat = "p (%s) -> p %s" % (" ".join(names), " ".join(names))
                return v.rearrange(pat, **{c: s for c, s in zip(names[1:], shape[1:])})
            return cut

        s_x0, s_x, s_w, s_e, s_b = sem("first_x_loaded"), sem("x_loaded"), sem("weights_loaded"), sem("edges_loaded"), sem("bounds_back")
        s_w2, s_basis, s_const = sem("later_weights_loaded"), sem("basis_loaded"), sem("constants_ready")

        with nc.Block() as block:
            cut = carve()
            hn = cut([CH, D], parts=P)
            hT = cut([CH, 2, P])
            qvst = cut([CH, 2 * D], parts=P)
            kf = cut([CH, D], parts=P)
            r1 = cut([CH, D], parts=P)
            sq = cut([3, 2, D], parts=P)
            kst = cut([CH, 3, KW], BF16, parts=P)
            zero = cut([CH, AW], parts=P)
            wtmp = cut([4, 2, D])
            wq = cut([2, 3 * D])
            bq = cut([3 * D], parts=P)
            base = cut([NB, 2, D])
            rows = cut([GE], I32, parts=G)
            rows16 = cut([GE], I16, parts=G)
            st_ready, h_ready = sem("st_ready"), sem("h_ready")
            var_ready, dev_ready = sem("var_ready"), sem("dev_ready")
            hn_ready, hT_in_psum, hT_ready = sem("hn_ready"), sem("hT_in_psum"), sem("hT_ready")
            qkv_ready, qkv_taken = sem("qkv_ready"), sem("qkv_taken")
            kh_ready, r1_ready, km_ready, kl_ready = (sem(n) for n in ("kh_ready", "r1_ready", "km_ready", "kl_ready"))
            sq_ready = sem("sq_ready")
            stored = [sem(f"tables_stored{j}") for j in range(CH)]
            zeroed, z_out, w_done = sem("zeroed"), sem("z_out"), sem("relation_weights_by_dve")
            d16, bout = sem("dst16_stored"), sem("bounds_stored")
            cast, mm, ident_ready = sem("rows_cast"), sem("bounds_found"), sem("ident_ready")
            nmax_in, nmax_back = sem("nmax_in"), sem("nmax_back")

            @block.sync
            def _(sp):
                sp.dma_start(rows, dst.rearrange("(g e) -> g e", g=G)).then_inc(s_b, 16)
                xs_v = xs[:, :].rearrange("p (b d) -> p b d", d=D)
                sp.dma_start(xs_v[:, 0:CH, :], x_v[:, 0:CH, :]).then_inc(s_x0, 16)
                for n, a in enumerate((ga, ba, gr, br)):
                    sp.dma_start(cols[:, n, :], a.rearrange("(k p) -> p k", p=128),
                                 allow_slow_non_contiguous=True).then_inc(s_w, 16)
                for o, c in ((0, 0), (1, 2), (2, 1)):
                    sp.dma_start(wq[:, :, o * D:(o + 1) * D],
                                 Wqkv[:, c * D:(c + 1) * D].rearrange("(k p) n -> p k n", p=128)).then_inc(s_w, 16)
                    sp.dma_start(bq[:, o * D:(o + 1) * D],
                                 bqkv[c * D:(c + 1) * D].partition_broadcast(P)).then_inc(s_w, 16)
                sp.wait_ge(cast, 1)
                sp.dma_start(dst16, rows16).then_inc(d16, 16)
                sp.wait_ge(mm, 2)
                sp.dma_start(bounds, flg[0:G, 0:2]).then_inc(bout, 16)
                sp.wait_ge(bout, 16)
                sp.dma_start(bnd[:, :, :], bounds.partition_broadcast(128)).then_inc(s_b, 16)
                sp.dma_start(xs_v[:, CH:NBLK, :], x_v[:, CH:NBLK, :]).then_inc(s_x, 16)
                sp.dma_start(cmpb[:, :], comp.rearrange("r b -> (r b)").partition_broadcast(128)).then_inc(s_basis, 16)
                sp.dma_start(base, basis.rearrange("b (k p) o -> p b k o", p=128)).then_inc(s_basis, 16)
                for tab, a in ((srcs, src), (dsti, dst), (typs, edge_type)):
                    sp.dma_start(tab[:, :].rearrange("p (g t) -> p g t", t=T),
                                 a.rearrange("(g p t) -> p g t", p=P, t=T)).then_inc(s_e, 16)
                sp.dma_start(bin_[:, :], b_in.rearrange("(k p) -> p k", p=128),
                             allow_slow_non_contiguous=True).then_inc(s_w2, 16)
                for n, a in enumerate((b_out, h_bias, gamma, beta)):
                    sp.dma_start(rowb[:, n, :], a.partition_broadcast(P)).then_inc(s_w2, 16)
                sp.wait_ge(zeroed, 2)
                for c in range(N, NPAD, P):
                    sp.dma_start(att[c:c + P, :], zero[:, 0, :]).then_inc(z_out, 16)
                    sp.dma_start(k_tab[c:c + P, :], zero.rearrange("p b d -> p (b d)").bitcast(BF16)[:, 0:3 * KW]).then_inc(z_out, 16)
                with sp.Fori(0, NCH) as i:
                    sp.dma_start(att[bass.ds(i * CH * P, CH * P), :].rearrange("(b p) d -> p b d", p=P), zero).then_inc(z_out, 16)
                    for j in range(CH):
                        b = i * CH + j
                        sp.wait_ge(qkv_taken, 2 * b + 12)
                        sp.dma_start(qv_tab[bass.ds(b * P, P), :], qvst[:, j, :]).then_inc(stored[j], 16)
                        sp.wait_ge(kl_ready, b + 1)
                        sp.dma_start(k_tab[bass.ds(b * P, P), :], kst[:, j, :, :].rearrange("p c d -> p (c d)")).then_inc(stored[j], 16)
                sp.dma_start(wloop[:, :, :], loop_w.rearrange("(k p) n -> p k n", p=128)).then_inc(s_w2, 16)
                sp.dma_start(win[:, :, :], W_in.rearrange("(k p) n -> p k n", p=128)).then_inc(s_w2, 16)
                sp.dma_start(wout[:, :, :], W_out.rearrange("(k p) n -> p k n", p=128)).then_inc(s_w2, 16)
                for j in range(CH):
                    sp.wait_ge(stored[j], 32 * NCH + 32)
                sp.wait_ge(d16, 16)
                sp.wait_ge(s_b, 32)
                sp.wait_ge(z_out, 16 * (NCH + 2 * (NPAD - N) // P))

            @block.gpsimd
            def _(pool):
                own = Steps(pool, sem("pre_pool"))
                nc.gpsimd.iota(wof[:, 1:VTAB + 1].rearrange("p (w g) -> p w g", g=G), pattern=[[WIN, NWIN + 1], [0, G]],
                               base=0, channel_multiplier=0).then_inc(s_const, 1)
                nc.gpsimd.iota(gof[:, :].rearrange("p (w g) -> p w g", g=G), pattern=[[0, NWIN + 1], [1, G]],
                               base=0, channel_multiplier=0).then_inc(s_const, 1)
                nc.gpsimd.iota(iotai[:, :], pattern=[[1, 128]], base=0, channel_multiplier=0).then_inc(s_const, 1)
                nc.gpsimd.iota(trips[:, 0:1], pattern=[[0, 1]], base=0, channel_multiplier=1).then_inc(s_const, 1)
                nc.gpsimd.memset(wof[:, 0:1], 0).then_inc(s_const, 1)
                nc.gpsimd.memset(nmx[:, :], 0.0).then_inc(s_const, 1)
                nc.gpsimd.memset(zero, 0.0).then_inc(zeroed, 1)
                nc.gpsimd.memset(kst[:, :, :, D:KW], 0.0).then_inc(zeroed, 1)
                pool.wait_ge(s_basis, 32)
                for r in range(RP):
                    w = wrel[:, :, r * D:(r + 1) * D]
                    own.did(nc.gpsimd.tensor_scalar(w, base[:, 0, :, :], cmpb[:, r * NB:r * NB + 1], None, ALU.mult))
                for n in range(1, NB):
                    for half in range(2):
                        relations = range(half * RP // 2, (half + 1) * RP // 2)
                        for r in relations:
                            own.did(nc.gpsimd.tensor_scalar(wtmp[:, r % 4, :, :], base[:, n, :, :],
                                                            cmpb[:, r * NB + n:r * NB + n + 1], None, ALU.mult))
                        own.wait()
                        for r in relations:
                            w = wrel[:, :, r * D:(r + 1) * D]
                            own.did(nc.gpsimd.tensor_tensor(w, w, wtmp[:, r % 4, :, :], ALU.add))
                        own.wait()
                own.wait()
                pool.wait_ge(nmax_in, 1)
                nc.gpsimd.partition_all_reduce(nmr[:, :], nmx[:, :], 128, RMAX).then_inc(nmax_back, 1)

            @block.scalar
            def _(act):
                def root_x(i):
                    act.wait_ge(var_ready, 2 * i + 1)
                    nc.scalar.activation(rs[:, :], rs[:, :], ACT.Sqrt).then_inc(dev_ready, 1)

                def relu(i, blocks):
                    act.wait_ge(st_ready, i + 1)
                    for j in blocks:
                        o = (i * CH + j) * D
                        nc.scalar.activation(hs[:, bass.ds(o, D)], xs[:, bass.ds(o, D)], ACT.Relu,
                                             bias=nm[:, j:j + 1], scale=rs[:, j:j + 1]).then_inc(h_ready, 1)

                def root_h(i):
                    act.wait_ge(var_ready, 2 * i + 2)
                    nc.scalar.activation(rsb[:, :], rsb[:, :], ACT.Sqrt).then_inc(dev_ready, 1)

                def features(i, j):
                    act.wait_ge(hT_in_psum, 2 * (i * CH + j) + 3)
                    for k in range(2):
                        nc.scalar.activation(hT[:, j, k, :], ps[:, j % 2, k * P:k * P + P], ACT.Identity,
                                             bias=cols[:, 1, k:k + 1], scale=cols[:, 0, k:k + 1]).then_inc(hT_ready, 1)

                def chunk(i, last):
                    for j in range(CH + 2):
                        b = i * CH + j
                        if 1 <= j < CH:
                            features(i, j)
                        if j == 0 and not last:
                            root_x(i + 1)
                        if j == 4 and not last:
                            root_h(i + 1)
                        if 1 <= j <= CH:
                            act.wait_ge(qkv_taken, 2 * b + 10)
                            nc.scalar.activation(kst[:, j - 1, 0, 0:D], kf[:, j - 1, :], ACT.Copy).then_inc(kh_ready, 1)
                            act.wait_ge(sq_ready, 2 * b + 6)
                            nc.scalar.activation(sq[:, (j - 1) % 3, 0, :], qvst[:, j - 1, 0:D], ACT.Square,
                                                 accum_out=nrm[:, 0, bass.ds(b - 1, 1)]).then_inc(sq_ready, 1)
                            nc.scalar.activation(sq[:, (j - 1) % 3, 1, :], kf[:, j - 1, :], ACT.Square,
                                                 accum_out=nrm[:, 1, bass.ds(b - 1, 1)]).then_inc(sq_ready, 1)
                        if not last and j == 1:
                            act.wait_ge(s_x, 16)
                        if not last and 1 <= j <= 3:
                            relu(i + 1, ((0, 1), (2, 3), (4,))[j - 1])
                        if not last and j == CH:
                            features(i + 1, 0)
                        if j >= 2:
                            act.wait_ge(r1_ready, b - 1)
                            nc.scalar.activation(kst[:, j - 2, 1, 0:D], r1[:, j - 2, :], ACT.Copy).then_inc(km_ready, 1)

                act.sem_inc(sq_ready, 2 * CH)
                act.wait_ge(s_x0, 16)
                root_x(0)
                relu(0, range(CH))
                root_h(0)
                act.wait_ge(s_w, 16 * 10)
                features(0, 0)
                with act.Fori(0, NCH - 1) as i:
                    chunk(i, False)
                chunk(NCH - 1, True)
                act.wait_ge(var_ready, 2 * NCH + 1)
                nc.scalar.activation(nbias[:, :], nbias[:, :], ACT.Sqrt, scale=SCALE * SCALE).then_inc(dev_ready, 1)

            @block.tensor
            def _(pe):
                pe.wait_ge(s_w, 16 * 10)
                pe.wait_ge(ident_ready, 1)

                def turn(b, j):
                    pe.wait_ge(hn_ready, b + 1)
                    for k in range(2):
                        nc.tensor.transpose(ps[:, j % 2, k * P:k * P + P], hn[:, j, k * 128:k * 128 + 128],
                                            ident[0:P, 0:P]).then_inc(hT_in_psum, 1)

                def project(b, j):
                    pe.wait_ge(hT_ready, 2 * b + 2)
                    pe.wait_ge(qkv_taken, 2 * b + (10 if j == 0 else 6 if j == 1 else 8))
                    for c, bank, n in ((0, 2 + j % 2, 2 * D), (2 * D, 4 + j % 2, D)):
                        for k in range(2):
                            last = nc.tensor.matmul(ps[0:P, bank, 0:n], hT[:, j, k, :], wq[:, k, c:c + n],
                                                    start=(k == 0), stop=(k == 1))
                    last.then_inc(qkv_ready, 1)

                def chunk(i, last):
                    for j in range(1, CH + 1):
                        if j < CH:
                            turn(i * CH + j, j)
                        project(i * CH + j - 1, j - 1)
                    if not last:
                        turn(i * CH + CH, 0)

                turn(0, 0)
                with pe.Fori(0, NCH - 1) as i:
                    chunk(i, False)
                chunk(NCH - 1, True)

            @block.vector
            def _(dve):
                own = Steps(dve, sem("pre_dve"))
                dve.wait_ge(s_b, 16)
                nc.vector.tensor_copy(rows16, rows).then_inc(cast, 1)
                nc.vector.tensor_reduce(flg[0:G, 0:1], rows, AX.X, ALU.min).then_inc(mm, 1)
                nc.vector.tensor_reduce(flg[0:G, 1:2], rows, AX.X, ALU.max).then_inc(mm, 1)
                dve.sem_inc(qkv_taken, 10)
                for j in range(CH):
                    dve.sem_inc(stored[j], 32)
                dve.wait_ge(s_const, 6)
                own.did(nc.vector.tensor_copy(iotaj[:, :], iotai[:, :]))
                own.did(nc.vector.tensor_copy(iotap[:, :], trips[:, 0:1]))
                own.wait()
                own.did(nc.vector.tensor_scalar(ident[:, :], iotaj[:, :], iotap[:, :], None, ALU.is_equal))
                own.did(nc.vector.tensor_scalar(identb[:, :], iotaj[:, :], iotap[:, :], None, ALU.is_equal))
                own.wait()
                dve.sem_inc(ident_ready, 1)

                def spread(i, st, m, r):
                    own.wait()
                    dve.nop(nofuse=True)
                    for j in range(CH):
                        own.did(nc.vector.bn_aggr(m[:, j, :], st[:, j, :]))
                    own.wait()
                    nc.vector.tensor_scalar(r[:, :], m[:, :, 1], EPS, None, ALU.add).then_inc(var_ready, 1)

                def x_stats(i):
                    for j in range(CH):
                        own.did(nc.vector.bn_stats(st6[:, j, :], xs[:, bass.ds((i * CH + j) * D, D)]))
                    spread(i, st6, mv, rs)

                def x_scale(i):
                    dve.wait_ge(dev_ready, 2 * i + 1)
                    own.did(nc.vector.reciprocal(rs[:, :], rs[:, :]))
                    own.wait()
                    nc.vector.scalar_tensor_tensor(out=nm[:, :], in0=mv[:, :, 0], scalar=-1.0, in1=rs[:, :],
                                                   op0=ALU.mult, op1=ALU.mult).then_inc(st_ready, 1)

                def h_stats(i, blocks):
                    for j in blocks:
                        dve.wait_ge(h_ready, i * CH + j + 1)
                        dve.nop(nofuse=True)
                        own.did(nc.vector.bn_stats(st6b[:, j, :], hs[:, bass.ds((i * CH + j) * D, D)]))

                def normalize(i):
                    dve.wait_ge(dev_ready, 2 * i + 2)
                    own.did(nc.vector.reciprocal(rsb[:, :], rsb[:, :]))
                    own.wait()
                    dve.wait_ge(hT_in_psum, 2 * CH * i + 1)
                    for j in range(CH):
                        nc.vector.tensor_scalar(hn[:, j, :], hs[:, bass.ds((i * CH + j) * D, D)], mvb[:, j, 0:1],
                                                rsb[:, j:j + 1], ALU.subtract, ALU.mult).then_inc(hn_ready, 1)

                def chunk(i, last):
                    if not last:
                        dve.wait_ge(s_x, 16)
                        x_stats(i + 1)
                    for j in range(CH + 3):
                        b = i * CH + j
                        if j == 4 and not last:
                            h_stats(i + 1, (4,))
                            spread(i + 1, st6b, mvb, rsb)
                        if j < CH:
                            dve.wait_ge(qkv_ready, b + 1)
                            dve.wait_ge(stored[j], 32 * i + 32)
                            nc.vector.tensor_tensor(qvst[:, j, :], ps[0:P, 2 + j % 2, :], bq[:, 0:2 * D],
                                                    ALU.add).then_inc(qkv_taken, 1)
                            nc.vector.tensor_tensor(kf[:, j, :], ps[0:P, 4 + j % 2, 0:D], bq[:, 2 * D:3 * D],
                                                    ALU.add).then_inc(qkv_taken, 1)
                        if not last:
                            if j == 0:
                                x_scale(i + 1)
                            if 2 <= j <= 3:
                                h_stats(i + 1, ((0, 1), (2, 3))[j - 2])
                        if 1 <= j <= CH:
                            dve.wait_ge(kh_ready, b)
                            nc.vector.tensor_tensor(r1[:, j - 1, :], kf[:, j - 1, :], kst[:, j - 1, 0, 0:D],
                                                    ALU.subtract).then_inc(r1_ready, 1)
                        if 3 <= j:
                            dve.wait_ge(km_ready, b - 2)
                            nc.vector.tensor_tensor(kst[:, j - 3, 2, 0:D], r1[:, j - 3, :], kst[:, j - 3, 1, 0:D],
                                                    ALU.subtract).then_inc(kl_ready, 1)
                        if j == 4 and not last:
                            normalize(i + 1)
                        if last and j < NB:
                            if j == 0:
                                dve.wait_ge(s_basis, 32)
                            else:
                                dve.wait_ge(w_done, (R - RP) * j)
                            for r in range(RP, R):
                                w = wrel[:, :, r * D:(r + 1) * D]
                                c = cmpb[:, r * NB + j:r * NB + j + 1]
                                if j == 0:
                                    nc.vector.tensor_scalar(w, base[:, 0, :, :], c, None, ALU.mult).then_inc(w_done, 1)
                                else:
                                    nc.vector.scalar_tensor_tensor(out=w, in0=base[:, j, :, :], scalar=c, in1=w,
                                                                   op0=ALU.mult, op1=ALU.add).then_inc(w_done, 1)

                dve.sem_inc(hT_in_psum, 1)
                dve.wait_ge(s_x0, 16)
                x_stats(0)
                x_scale(0)
                h_stats(0, range(CH))
                spread(0, st6b, mvb, rsb)
                normalize(0)
                dve.wait_ge(s_b, 32)
                own.did(nc.vector.tensor_tensor(wst[:, 0:G], bnd[:, :, 1], bnd[:, :, 0], ALU.subtract))
                own.did(nc.vector.tensor_tensor(wst[:, G:2 * G - 1], bnd[:, 1:G, 0], bnd[:, 0:G - 1, 0], ALU.subtract))
                own.wait()
                own.did(nc.vector.tensor_reduce(flg[:, 2:3], wst[:, 0:G], AX.X, ALU.max))
                own.did(nc.vector.tensor_reduce(flg[:, 3:4], wst[:, G:2 * G - 1], AX.X, ALU.min))
                own.wait()
                own.did(nc.vector.tensor_scalar(flg[:, 4:5], flg[:, 2:3], float(WIN - 1), None, ALU.is_le))
                own.did(nc.vector.tensor_scalar(flg[:, 5:6], flg[:, 3:4], 0.0, None, ALU.is_ge))
                own.wait()
                own.did(nc.vector.tensor_tensor(flg[:, 6:7], flg[:, 4:5], flg[:, 5:6], ALU.mult))
                own.wait()
                own.did(nc.vector.tensor_scalar(trips[:, 0:1], flg[:, 6:7], float((G - VMAX) // 2), float(VMAX // 2),
                                                ALU.mult, ALU.add))
                own.did(nc.vector.tensor_scalar(wof[:, 1:G + 1], bnd[:, :, 0], flg[:, 6:7], None, ALU.mult))
                own.wait()
                own.did(nc.vector.tensor_copy(wst[:, :], wof[:, 1:VTAB + 1]))
                own.did(nc.vector.tensor_tensor(wcar[:, :], wof[:, 0:VTAB], wof[:, 1:VTAB + 1], ALU.subtract))
                own.wait()
                own.did(nc.vector.tensor_scalar(wnode[:, :], wst[:, :], iotap[:, :], None, ALU.add))
                own.did(nc.vector.tensor_scalar(wcar[:, :], wcar[:, :], iotap[:, :], None, ALU.add))
                own.wait()
                dve.wait_ge(s_w, 16 * 10)
                dve.wait_ge(zeroed, 2)
                with dve.Fori(0, NCH - 1) as i:
                    own.loop(i, 4 * CH + 2)
                    chunk(i, False)
                own.end(NCH - 1)
                chunk(NCH - 1, True)
                dve.wait_ge(s_e, 48)
                own.did(nc.vector.tensor_copy(dstf[:, :], dsti[:, :]))
                own.did(nc.vector.scalar_tensor_tensor(out=typs[:, :], in0=srcs[:, :], scalar=float(R), in1=typs[:, :],
                                                       op0=ALU.mult, op1=ALU.add))
                dve.wait_ge(sq_ready, 2 * NBLK + 2 * CH)
                for n in range(2):
                    own.did(nc.vector.tensor_reduce(nmx[0:P, n:n + 1], nrm[:, n, :], AX.X, ALU.max))
                own.wait()
                dve.sem_inc(nmax_in, 1)
                dve.wait_ge(nmax_back, 1)
                nc.vector.tensor_tensor(nbias[:, :], nmr[:, 0:1], nmr[:, 1:2], ALU.mult).then_inc(var_ready, 1)
                dve.wait_ge(dev_ready, 2 * NCH + 1)
                own.did(nc.vector.tensor_scalar(wide, nbias[:, :], WIDE, None, ALU.is_gt))
                own.did(nc.vector.tensor_scalar(flg[:, 7:8], nbias[:, :], WIDE, -1.0, ALU.is_le, ALU.mult))
                own.wait()
                own.did(nc.vector.tensor_scalar(nbias[:, :], nbias[:, :], BIG, flg[:, 7:8], ALU.min, ALU.mult))
                own.wait()



        with nc.Block() as block:
            cut = carve()
            rowbuf = cut([2 * T, 2 * D + H], parts=P)
            ind = cut([2, T, WIN], parts=P)
            indT = cut([2, GE], BF16)
            kwin = cut([2, 3 * KW], BF16)
            drow = cut([2, GE], I16)
            car = cut([2, WIN])
            osum = cut([2, AW])
            sco = cut([T, H], parts=P)
            idx = cut([2, T], I32, parts=P)
            k_ready, k_used = sem("key_rows_ready"), sem("scores_ready")
            kwin_in = [sem(f"key_window_in{u}") for u in range(2)]
            drow_in = [sem(f"dst_row_in{u}") for u in range(2)]
            row_in = [sem(f"row_in{t}") for t in range(2 * T)]
            indT_ready, car_ready = sem("indT_ready"), sem("car_ready")
            turn_ready, ind_ready = sem("turn_ready"), sem("ind_ready")
            exp_done, w_ready, agg_done = sem("exp_done"), sem("weighted_ready"), sem("summed")
            win_done, osum_ready = sem("window_done"), sem("osum_ready")
            att_out, att_stored, idx_ready = sem("att_out"), sem("att_stored"), sem("idx_ready")
            zeros = sem("zeros_ready")

            def seen(v, j, ahead):
                return PAIRS * v + j + 1 + ahead

            SCORES_AHEAD = 4
            EXP_AHEAD = 4
            WEIGHTED_AHEAD = 4
            SUMMED_AHEAD = 8
            KEYS_AHEAD = 8
            IND_AHEAD = 4

            def trip_count(eng):
                return eng.value_load(trips[0:1, 0:1], min_val=G // 2, max_val=VMAX // 2)

            cut = carve()
            mq = cut([T, 2 * D], parts=P)
            mk = cut([T, 3 * KW], BF16, parts=P)
            mk32 = cut([T, D], parts=P)
            msc = cut([H, T], parts=P)
            midx = cut([2, T], I32, parts=P)
            cut = carve()
            ball = cut([H, GE])
            bmask = cut([GE])
            brow = cut([GE], I16)
            bmax = cut([H])
            mwin = cut([H])
            mneg = cut([H], parts=P)
            mall = cut([NBLK, H], parts=P)
            mrest = cut([NBLK, H], parts=P)
            mparts = cut([3, NBLK, H], BF16, parts=P)
            mi_ready, mrow_in, msc_ready, msc_used = (sem(n) for n in ("max_indices", "max_rows_in", "max_scores", "max_rows_used"))
            msc_out, msc_stored, mneg_ready, mneg_out = (sem(n) for n in ("max_scores_out", "max_scores_stored", "lowest_ready", "lowest_out"))
            mv_in, mwin_ready, mwin_out = (sem(n) for n in ("max_visit_in", "window_max_ready", "window_max_out"))
            mall_in, mparts_ready, shifts_out = sem("maxima_in"), sem("shift_parts_ready"), sem("shifts_out")

            def is_wide(eng):
                return eng.value_load(wide[0:1, 0:1], min_val=0, max_val=1)

            def maxima_sync(sp, nt):
                sp.sem_inc(msc_stored, 1)
                with sp.Fori(0, G) as g:
                    sp.wait_ge(msc_ready, g + 1)
                    sp.nop(nofuse=True)
                    sp.dma_start(s_tab[bass.ds(g, 1), :, :].rearrange("o h (p t) -> p (o h) t", t=T), msc).then_inc(msc_out, 16)
                    sp.wait_ge(msc_out, 16 * g + 16)
                    sp.nop(nofuse=True)
                    sp.sem_inc(msc_stored, 1)
                sp.wait_ge(mneg_ready, 1)
                for b in range(NPAD // P):
                    sp.dma_start(m_tab[b * P:(b + 1) * P, :], mneg).then_inc(mneg_out, 16)
                sp.wait_ge(mneg_out, 16 * (NPAD // P))
                with sp.Fori(0, 2 * nt) as v:
                    w = sp.value_load(wof[0:1, bass.ds(v + 1, 1)], min_val=0, max_val=NWIN * WIN)
                    g = sp.value_load(gof[0:1, bass.ds(v, 1)], min_val=0, max_val=G - 1)
                    sp.dma_start(ball.rearrange("p h e -> p (h e)"), s_tab[bass.ds(g, 1), :, :].rearrange("o h e -> (o h e)")
                                 .partition_broadcast(128)).then_inc(mv_in, 16)
                    sp.dma_start(brow, dst16[bass.ds(g, 1), :].rearrange("o e -> (o e)").partition_broadcast(128)).then_inc(mv_in, 16)
                    sp.dma_start(mwin, m_tab[bass.ds(w, WIN), :]).then_inc(mv_in, 16)
                    sp.wait_ge(mwin_ready, v + 1)
                    sp.nop(nofuse=True)
                    sp.dma_start(m_tab[bass.ds(w, WIN), :], mwin).then_inc(mwin_out, 16)
                    sp.wait_ge(mwin_out, 16 * v + 16)
                    sp.nop(nofuse=True)
                sp.dma_start(mall, m_tab[0:N, :].rearrange("(b p) h -> p b h", p=P)).then_inc(mall_in, 16)
                sp.wait_ge(mparts_ready, 1)
                for c in range(3):
                    sp.dma_start(k_tab[0:N, c * KW + D:(c + 1) * KW].rearrange("(b p) h -> p b h", p=P),
                                 mparts[:, c, :, :]).then_inc(shifts_out, 16)
                sp.wait_ge(shifts_out, 48)

            def maxima_gpsimd(pool):
                with pool.Fori(0, G) as g:
                    pool.wait_ge(msc_used, g + 1)
                    nc.gpsimd.tensor_copy(midx[:, 0, :], srcs[:, bass.ds(g * T, T)]).then_inc(mi_ready, 1)
                    nc.gpsimd.tensor_copy(midx[:, 1, :], dsti[:, bass.ds(g * T, T)]).then_inc(mi_ready, 1)
                    pool.wait_ge(mi_ready, 2 * g + 2)
                    pool.nop(nofuse=True)
                    for t in range(T):
                        pool.indirect_dma_start(
                            out=mq[:, t, :], out_offset=None, in_=qv_tab,
                            in_offset=bass.IndirectOffsetOnAxis(ap=midx[:, 0, t:t + 1], axis=0)).then_inc(mrow_in, 16)
                        pool.indirect_dma_start(
                            out=mk[:, t, :], out_offset=None, in_=k_tab,
                            in_offset=bass.IndirectOffsetOnAxis(ap=midx[:, 1, t:t + 1], axis=0)).then_inc(mrow_in, 16)

            def maxima_vector(dve, nt):
                own = Steps(dve, sem("maxima_dve"))
                dve.sem_inc(msc_used, 1)
                with dve.Fori(0, G) as g:
                    own.loop(g, 3)
                    dve.wait_ge(mrow_in, 32 * T * g + 32 * T)
                    dve.wait_ge(msc_stored, g + 1)
                    own.did(nc.vector.tensor_tensor(mk32, mk[:, :, 0:D], mk[:, :, KW:KW + D], ALU.add))
                    own.wait()
                    own.did(nc.vector.tensor_tensor(mk32, mk32, mk[:, :, 2 * KW:2 * KW + D], ALU.add))
                    own.wait()
                    own.did(nc.vector.tensor_tensor(mk32, mk32, mq[:, :, 0:D], ALU.mult))
                    own.wait()
                    nc.vector.tensor_reduce(msc.rearrange("p h t -> p t h"), mk32.rearrange("p t (h d) -> p t h d", d=DH),
                                            AX.X, ALU.add).then_inc(msc_ready, 1)
                    dve.wait_ge(msc_ready, g + 1)
                    dve.nop(nofuse=True)
                    dve.sem_inc(msc_used, 1)
                own.end(G)
                dve.wait_ge(msc_stored, G + 1)
                nc.vector.memset(mneg, -BIG).then_inc(mneg_ready, 1)
                with dve.Fori(0, 2 * nt) as v:
                    own.loop(v, 4)
                    dve.wait_ge(mv_in, 48 * v + 48)
                    own.did(nc.vector.tensor_scalar(bmask, brow, wnode[:, bass.ds(v, 1)], None, ALU.is_equal))
                    own.wait()
                    own.did(nc.vector.tensor_scalar(bmask, bmask, -1.0, BIG, ALU.add, ALU.mult))
                    own.wait()
                    own.did(nc.vector.tensor_tensor(ball, ball, bmask.unsqueeze(1).broadcast_to([128, H, GE]), ALU.add))
                    own.wait()
                    own.did(nc.vector.tensor_reduce(bmax, ball, AX.X, ALU.max))
                    own.wait()
                    nc.vector.tensor_tensor(mwin, mwin, bmax, ALU.max).then_inc(mwin_ready, 1)
                own.end(2 * nt)
                dve.wait_ge(mall_in, 16)
                own.did(nc.vector.tensor_copy(mparts[:, 0, :, :], mall))
                own.wait()
                own.did(nc.vector.tensor_tensor(mrest, mall, mparts[:, 0, :, :], ALU.subtract))
                own.wait()
                own.did(nc.vector.tensor_copy(mparts[:, 1, :, :], mrest))
                own.wait()
                nc.vector.tensor_tensor(mparts[:, 2, :, :], mrest, mparts[:, 1, :, :], ALU.subtract).then_inc(mparts_ready, 1)
                dve.wait_ge(shifts_out, 48)

            @block.sync
            def _(sp):
                nt = trip_count(sp)
                with sp.If(is_wide(sp)):
                    maxima_sync(sp, nt)
                sp.sem_inc(att_stored, 1)

                def store(v, u):
                    sp.wait_ge(osum_ready, v + 5)
                    sp.nop(nofuse=True)
                    sp.wait_ge(att_out, 16 * (v + 2))
                    sp.nop(nofuse=True)
                    sp.sem_inc(att_stored, 1)
                    w = sp.value_load(wof[0:1, bass.ds(v + 1, 1)], min_val=0, max_val=NWIN * WIN)
                    sp.dma_start(att[bass.ds(w, WIN), :], osum[:, u, :]).then_inc(att_out, 16)

                def load_keys(v, u):
                    w = sp.value_load(wof[0:1, bass.ds(v + 1, 1)], min_val=0, max_val=NWIN * WIN)
                    sp.wait_ge(k_ready, seen(v - 2, 3, KEYS_AHEAD))
                    sp.nop(nofuse=True)
                    sp.dma_start(kwin[:, u, :], k_tab[bass.ds(w, WIN), :]).then_inc(kwin_in[u], 16)

                def load_dst(v, u):
                    g = sp.value_load(gof[0:1, bass.ds(v, 1)], min_val=0, max_val=G - 1)
                    sp.wait_ge(indT_ready, v + 1)
                    sp.nop(nofuse=True)
                    sp.dma_start(drow[:, u, :], dst16[bass.ds(g, 1), :].rearrange("o e -> (o e)").partition_broadcast(128)
                                 ).then_inc(drow_in[u], 16)

                load_keys(0, 0)
                load_dst(0, 0)
                load_dst(1, 1)
                sp.wait_ge(zeros, 1)
                sp.dma_start(att[0:WIN, :], osum[:, 0, :]).then_inc(att_out, 16)
                with sp.Fori(0, nt) as i:
                    for u in range(2):
                        v = 2 * i + u
                        load_keys(v + 1, 1 - u)
                        load_dst(v + 2, u)
                        store(v - 1, 1 - u)
                store(2 * nt - 1, 1)
                sp.wait_ge(drow_in[0], 16 * nt + 16)
                sp.nop(nofuse=True)
                sp.wait_ge(drow_in[1], 16 * nt + 16)
                sp.nop(nofuse=True)
                sp.wait_ge(att_out, 32 * nt + 32)
                sp.nop(nofuse=True)

            @block.gpsimd
            def _(pool):
                nt = trip_count(pool)
                with pool.If(is_wide(pool)):
                    maxima_gpsimd(pool)
                    pool.wait_ge(zeros, 1)

                with pool.Fori(0, nt) as i:
                    for u in range(2):
                        v = 2 * i + u
                        pool.wait_ge(idx_ready, v + 1)
                        for t in range(T):
                            if t % 2 == 0:
                                pool.wait_ge(agg_done, seen(v - 2, t // 2, SUMMED_AHEAD))
                                pool.nop(nofuse=True)
                            pool.indirect_dma_start(
                                out=rowbuf[:, u * T + t, 0:2 * D], out_offset=None, in_=qv_tab,
                                in_offset=bass.IndirectOffsetOnAxis(ap=idx[:, u, t:t + 1], axis=0)).then_inc(row_in[u * T + t], 16)

            @block.scalar
            def _(act):
                nt = trip_count(act)
                act.sem_inc(exp_done, EXP_AHEAD)
                act.sem_inc(ind_ready, IND_AHEAD)
                act.sem_inc(osum_ready, 3)
                with act.If(is_wide(act)):
                    act.wait_ge(zeros, 1)

                def indices(v, u):
                    g = act.value_load(gof[0:1, bass.ds(v, 1)], min_val=0, max_val=G - 1)
                    nc.scalar.activation(idx[:, u, :], srcs[:, bass.ds(g * T, T)], ACT.Copy).then_inc(idx_ready, 1)

                indices(0, 0)
                act.wait_ge(zeros, 1)

                def take(v, u):
                    act.wait_ge(win_done, v + 2)
                    act.wait_ge(att_stored, v + 2)
                    nc.scalar.activation(osum[:, u, :], ps[:, 6 + u, 0:AW], ACT.Copy).then_inc(osum_ready, 1)

                def indicators(v, u):
                    for half in range(2):
                        act.wait_ge(turn_ready, 2 * v + half + 1)
                        if half == 0:
                            act.wait_ge(agg_done, seen(v - 2, 3, SUMMED_AHEAD))
                        nc.scalar.activation(ind[:, u, 4 * half:4 * half + 4, :],
                                             ps[0:P, 4 + half, 0:4 * WIN // 2].bitcast(BF16).rearrange("p (t w) -> p t w", w=WIN),
                                             ACT.Copy).then_inc(ind_ready, 1)

                indicators(0, 0)
                with act.Fori(0, nt) as i:
                    for u in range(2):
                        v = 2 * i + u

                        def weights(j):
                            act.wait_ge(k_used, seen(v, j, SCORES_AHEAD))
                            nc.scalar.activation(rowbuf[:, u * T + 2 * j:u * T + 2 * j + 2, 2 * D:2 * D + H], sco[:, 2 * j:2 * j + 2, :], ACT.Exp,
                                                 bias=nbias[0:P, :], scale=SCALE).then_inc(exp_done, 1)

                        for j in range(PAIRS):
                            weights(j)
                            if j == 0:
                                indices(v + 1, 1 - u)
                            if j == 1:
                                take(v - 1, 1 - u)
                            if j == 2:
                                indicators(v + 1, 1 - u)
                take(2 * nt - 1, 1)

            @block.tensor
            def _(pe):
                nt = trip_count(pe)
                pe.sem_inc(k_ready, KEYS_AHEAD - 1)
                pe.sem_inc(agg_done, SUMMED_AHEAD - PAIRS)
                pe.wait_ge(zeros, 1)

                def turn(v, u, half):
                    pe.wait_ge(ind_ready, 2 * v + half + 1 + IND_AHEAD - 2)
                    tiles = indT[:, u, :].rearrange("p (e t) -> p t e", t=T)
                    for t in range(4):
                        last = nc.tensor.transpose(ps[0:P, 4 + half, t * WIN // 2:(t + 1) * WIN // 2].bitcast(BF16),
                                                   tiles[:, 4 * half + t, :], identb[:, :])
                    last.then_inc(turn_ready, 1)

                for t in (2, 3):
                    last = nc.tensor.matmul(ps[0:P, t, 0:KW], indT[:, 1, 0:P], kwin[:, 1, 0:KW], start=True, stop=True)
                last.then_inc(k_ready, 1)

                def keys(n, v, u, j):
                    if j == 0:
                        pe.wait_ge(kwin_in[u], 16 * n + 16)
                    pe.wait_ge(k_used, seen(v, j - 2, SCORES_AHEAD))
                    tiles = indT[:, u, :].rearrange("p (e t) -> p t e", t=T)
                    for t in (2 * j, 2 * j + 1):
                        for c in range(3):
                            last = nc.tensor.matmul(ps[0:P, t % 4, 0:KW], tiles[:, t, :], kwin[:, u, c * KW:(c + 1) * KW],
                                                    start=(c == 0), stop=(c == 2))
                    last.then_inc(k_ready, 1)

                def add_up(v, u, j):
                    pe.wait_ge(w_ready, seen(v, j, WEIGHTED_AHEAD))
                    pe.wait_ge(ind_ready, 2 * v + j // 2 + 1 + IND_AHEAD)
                    if j == 0:
                        pe.wait_ge(osum_ready, v + 3)
                    for t in (2 * j, 2 * j + 1):
                        last = nc.tensor.matmul(ps[:, 6 + u, 0:AW], ind[:, u, t, :], rowbuf[:, u * T + t, D:2 * D + H],
                                                start=(t == 0), stop=False)
                    last.then_inc(agg_done, 1)

                def carry(v, u):
                    pe.wait_ge(osum_ready, v + 4)
                    pe.wait_ge(car_ready, v + 2)
                    nc.tensor.matmul(ps[:, 6 + u, 0:AW], car[:, u, :], osum[:, 1 - u, :], start=False, stop=True).then_inc(win_done, 1)

                def across(n, v, u):
                    pe.wait_ge(indT_ready, v + 3)
                    keys(n, v, u, 0)
                    turn(v, u, 0)
                    turn(v, u, 1)
                    add_up(v - 1, 1 - u, 2)
                    keys(n, v, u, 1)
                    add_up(v - 1, 1 - u, 3)
                    carry(v - 1, 1 - u)

                add_up(-1, 1, 0)
                add_up(-1, 1, 1)
                across(0, 0, 0)
                with pe.Fori(0, nt) as i:
                    for u in range(2):
                        v = 2 * i + u
                        keys(i, v, u, 2)
                        add_up(v, u, 0)
                        keys(i, v, u, 3)
                        add_up(v, u, 1)
                        across(i + u, v + 1, 1 - u)

            @block.vector
            def _(dve):
                nt = trip_count(dve)
                with dve.If(is_wide(dve)):
                    maxima_vector(dve, nt)
                own = Steps(dve, sem("edge_dve"))
                dve.sem_inc(k_used, SCORES_AHEAD - 1)
                dve.sem_inc(w_ready, WEIGHTED_AHEAD - 1)
                dve.sem_inc(indT_ready, 2)
                own.did(nc.vector.memset(rowbuf[:, T:2 * T, D:2 * D + H], 0.0))
                own.did(nc.vector.memset(ind[:, 1, :, :], 0.0))
                own.did(nc.vector.memset(osum, 0.0))
                own.did(nc.vector.memset(sco, 0.0))
                own.did(nc.vector.memset(indT[:, 1, :], 0.0))
                own.did(nc.vector.memset(kwin[:, 1, :], 0.0))
                nc.vector.memset(car[:, 1, :], 0.0).then_inc(car_ready, 1)
                own.wait()
                dve.sem_inc(zeros, 1)
                def to_window(n, v, u):
                    dve.wait_ge(drow_in[u], 16 * n + 16)
                    dve.wait_ge(k_ready, seen(v - 2, 3, KEYS_AHEAD))
                    nc.vector.tensor_scalar(indT[:, u, :], drow[:, u, :], wnode[:, bass.ds(v, 1)], None,
                                            ALU.is_equal).then_inc(indT_ready, 1)

                def shift(j, reduced):
                    bank = 2 * (j % 2)
                    dve.wait_ge(own.sem, reduced)
                    nc.vector.tensor_tensor(sco[:, 2 * j:2 * j + 2, :], sco[:, 2 * j:2 * j + 2, :],
                                            ps[0:P, bank:bank + 2, D:KW], ALU.subtract).then_inc(k_used, 1)

                dve.wait_ge(k_ready, seen(-1, 3, KEYS_AHEAD))
                to_window(0, 0, 0)
                with dve.Fori(0, nt) as i:
                    own.loop(i, 2 * 2 * PAIRS)
                    for u in range(2):
                        v = 2 * i + u

                        def weigh(v, u, j):
                            dve.wait_ge(exp_done, seen(v, j, EXP_AHEAD))
                            b = rowbuf[:, u * T + 2 * j:u * T + 2 * j + 2, :]
                            vals = b[:, :, D:2 * D].rearrange("p t (h d) -> p t h d", d=DH)
                            nc.vector.tensor_tensor(vals, vals, b[:, :, 2 * D:2 * D + H].unsqueeze(3).broadcast_to([P, 2, H, DH]),
                                                    ALU.mult).then_inc(w_ready, 1)

                        for j in range(PAIRS):
                            b = rowbuf[:, u * T + 2 * j:u * T + 2 * j + 2, :]
                            for t in (2 * j, 2 * j + 1):
                                dve.wait_ge(row_in[u * T + t], 16 * i + 16)
                            dve.wait_ge(k_ready, seen(v, j, KEYS_AHEAD))
                            bank = 2 * (j % 2)
                            reduced = own.base + own.n
                            own.did(nc.vector.tensor_tensor(b[:, :, 0:D], b[:, :, 0:D], ps[0:P, bank:bank + 2, 0:D], ALU.mult))
                            shift((j - 1) % PAIRS, reduced)
                            if j == 0:
                                nc.vector.tensor_scalar(car[:, u, :], iotaj[:, :], wcar[:, bass.ds(v, 1)], None,
                                                        ALU.is_equal).then_inc(car_ready, 1)
                            own.wait()
                            own.did(nc.vector.tensor_reduce(sco[:, 2 * j:2 * j + 2, :],
                                                            b[:, :, 0:D].rearrange("p t (h d) -> p t h d", d=DH), AX.X, ALU.add))
                            if j == 0:
                                weigh(v - 1, 1 - u, 3)
                            else:
                                weigh(v, u, j - 1)
                            if j == 1:
                                to_window(i + u, v + 1, 1 - u)
                own.end(nt)
                shift(PAIRS - 1, own.n)
                dve.wait_ge(exp_done, seen(2 * nt - 1, 3, EXP_AHEAD))
                b = rowbuf[:, 2 * T - 2:2 * T, :]
                vals = b[:, :, D:2 * D].rearrange("p t (h d) -> p t h d", d=DH)
                nc.vector.tensor_tensor(vals, vals, b[:, :, 2 * D:2 * D + H].unsqueeze(3).broadcast_to([P, 2, H, DH]),
                                        ALU.mult).then_inc(w_ready, 1)

        with nc.Block() as block:
            cut = carve()
            sums = cut([NBLK, AW], parts=P)
            yn = cut([CH, D], parts=P)
            yT = cut([2, CH * P])
            gT = cut([FF // 128, CH * P])
            h1T = cut([2, 2, P])
            h1s = cut([CH, D], parts=P)
            msg = cut([2, R * D], parts=P)
            rec = cut([CH, H], parts=P)
            vv = cut([6, CH], parts=P)
            zero = cut([2 * D], parts=P)
            zeroed, z_out = sem("rel_zeros_ready"), sem("rel_zeros_out")
            att_in = sem("att_in")
            x1_ready, x_ready, yn_ready = sem("x1_ready"), sem("x_ready"), sem("yn_ready")
            t_psum, yT_ready = sem("turned"), sem("yT_ready")
            hid_psum, hid_ready = sem("hidden_psum"), sem("hidden_ready")
            ff_psum, ff_taken = sem("ff_psum"), sem("ff_taken")
            st_ready, h1_ready = sem("x2_statistics"), sem("h1_ready")
            h1t_psum, h1T_ready = sem("h1_turned"), sem("h1T_ready")
            msg_psum, msg_a, msg_v = sem("msg_psum"), sem("msg_by_act"), sem("msg_by_dve")
            h1_kept = sem("h1_kept")
            msg_out, msg_stored = sem("msg_out"), sem("msg_stored")
            PARTS = ((0, 3 * P), (3 * P, 2 * P))
            NPROD = FF // 128 * len(PARTS)
            hall_v = h_all.rearrange("(n r) d -> n (r d)", r=R)

            def rsqrt(own, var, r, t):
                own.did(nc.vector.tensor_scalar(t.bitcast(I32), var.bitcast(I32), 1, None, ALU.logical_shift_right))
                own.wait()
                own.did(nc.vector.tensor_scalar(r.bitcast(I32), t.bitcast(I32), -1.0, float(0x5F3759DF), ALU.mult, ALU.add))
                own.wait()
                for _ in range(3):
                    own.did(nc.vector.tensor_tensor(t, r, r, ALU.mult))
                    own.wait()
                    own.did(nc.vector.tensor_tensor(t, t, var, ALU.mult))
                    own.wait()
                    own.did(nc.vector.tensor_scalar(t, t, -0.5, 1.5, ALU.mult, ALU.add))
                    own.wait()
                    own.did(nc.vector.tensor_tensor(r, r, t, ALU.mult))
                    own.wait()
            MID_STEPS = 2 + CH + 2 * CH + 1 + 14 + CH * (3 + 14)


            @block.sync
            def _(sp):
                for c in range(NCH):
                    sp.dma_start(sums[:, c * CH:(c + 1) * CH, :],
                                 att[c * CH * P:(c + 1) * CH * P, :].rearrange("(b p) d -> p b d", p=P)).then_inc(att_in, 16)
                    sp.wait_ge(att_in, 16 * c + 16)
                sp.wait_ge(zeroed, 1)
                for c in range(NPAD // P // 2):
                    sp.dma_start(rel[c * 2 * P:(c + 1) * 2 * P, :].rearrange("(b p) d -> p b d", p=P),
                                 zero.rearrange("p (b d) -> p b d", d=D)).then_inc(z_out, 16)
                with sp.Fori(0, NCH) as i:
                    for j in range(CH):
                        b = i * CH + j
                        sp.wait_ge(msg_a, 2 * b + 4)
                        sp.nop(nofuse=True)
                        sp.wait_ge(msg_v, 2 * b + 4)
                        sp.nop(nofuse=True)
                        sp.dma_start(hall_v[bass.ds(b * P, P), :], msg[:, j % 2, :]).then_inc(msg_out, 16)
                        sp.wait_ge(msg_out, 16 * b + 16)
                        sp.nop(nofuse=True)
                        sp.sem_inc(msg_stored, 1)
                sp.wait_ge(z_out, 16 * (NPAD // P // 2))

            @block.gpsimd
            def _(pool):
                own = Steps(pool, sem("mid_pool"))

                def residual(i):
                    for j in range(CH):
                        x_b = xs[:, bass.ds((i * CH + j) * D, D)]
                        pool.wait_ge(x1_ready, i * CH + j + 1)
                        pool.nop(nofuse=True)
                        own.did(nc.gpsimd.tensor_tensor(x_b, x_b, hs[:, bass.ds((i * CH + j) * D, D)], ALU.add))
                        own.wait()
                        pool.nop(nofuse=True)
                        nc.gpsimd.tensor_tensor(x_b, x_b, rowb[:, 0, :], ALU.add).then_inc(x_ready, 1)

                def keep(i):
                    for j in range(CH):
                        x_b = xs[:, bass.ds((i * CH + j) * D, D)]
                        pool.wait_ge(h1_ready, i * CH + j + 1)
                        pool.nop(nofuse=True)
                        nc.gpsimd.tensor_copy(hs[:, bass.ds((i * CH + j) * D, D)], h1s[:, j, :]).then_inc(h1_kept, 1)
                        nc.gpsimd.tensor_tensor(x_b, x_b, rowb[:, 3, :], ALU.add)

                nc.gpsimd.memset(zero, 0.0).then_inc(zeroed, 1)
                pool.wait_ge(s_w2, 16 * 8)
                residual(0)
                with pool.Fori(0, NCH - 1) as i:
                    own.loop(i, CH)
                    residual(i + 1)
                    keep(i)
                own.end(NCH - 1)
                keep(NCH - 1)

            @block.scalar
            def _(act):
                act.wait_ge(s_w2, 16 * 8)
                act.sem_inc(hid_ready, 2)
                act.sem_inc(msg_a, 2)
                act.sem_inc(h1_kept, CH)

                def y_features(i, j):
                    act.wait_ge(t_psum, 2 * (i * CH + j) + 3)
                    for k in range(2):
                        nc.scalar.activation(yT[:, k, j * P:(j + 1) * P], ps[:, j % 2, D + k * P:D + k * P + P], ACT.Identity,
                                             bias=cols[:, 3, k:k + 1], scale=cols[:, 2, k:k + 1]).then_inc(yT_ready, 1)

                def chunk(i, last):
                    for f in range(FF // 128):
                        for m, (c, n) in enumerate(PARTS):
                            act.wait_ge(hid_psum, i * NPROD + 2 * f + m + 1)
                            nc.scalar.activation(gT[:, f, c:c + n], ps[:, 2 + m, 0:n], ACT.Gelu,
                                                 bias=bin_[:, f:f + 1]).then_inc(hid_ready, 1)
                    for j in range(CH):
                        b = i * CH + j
                        o = b * D
                        act.wait_ge(st_ready, b + 1)
                        act.wait_ge(h1_kept, b + 1)
                        nc.scalar.activation(h1s[:, j, :], xs[:, bass.ds(o, D)], ACT.Relu,
                                             bias=nmb[:, j:j + 1], scale=rsb[:, j:j + 1]).then_inc(h1_ready, 1)
                        act.wait_ge(h1t_psum, 2 * b + 2)
                        if not last:
                            act.wait_ge(t_psum, 2 * (b + CH) + 3)
                        nc.scalar.activation(h1T[:, j % 2, :, :], ps[:, j % 2, 0:2 * P].rearrange("p (k n) -> p k n", k=2),
                                             ACT.Copy).then_inc(h1T_ready, 1)
                        if not last:
                            y_features(i + 1, j)
                        act.wait_ge(msg_stored, b + (2 if j == 0 else 1))
                        for c in range(2):
                            act.wait_ge(msg_psum, 4 * b + c + 1)
                            nc.scalar.activation(msg[:, j % 2, c * 512:(c + 1) * 512], ps[0:P, 2 + c, :],
                                                 ACT.Copy).then_inc(msg_a, 1)

                for j in range(CH):
                    y_features(0, j)
                with act.Fori(0, NCH - 1) as i:
                    chunk(i, False)
                chunk(NCH - 1, True)

            @block.tensor
            def _(pe):
                def turn_y(i, j):
                    pe.wait_ge(yn_ready, i * CH + j + 1)
                    for k in range(2):
                        nc.tensor.transpose(ps[:, j % 2, D + k * P:D + k * P + P], yn[:, j, k * 128:k * 128 + 128],
                                            ident[0:P, 0:P]).then_inc(t_psum, 1)

                def hidden(i):
                    pe.wait_ge(yT_ready, 2 * CH * i + 2 * CH)
                    pe.wait_ge(msg_a, 2 * CH * i + 2)
                    for f in range(FF // 128):
                        for m, (c, n) in enumerate(PARTS):
                            pe.wait_ge(hid_ready, i * NPROD + 2 * f + m + 1)
                            for k in range(2):
                                last = nc.tensor.matmul(ps[:, 2 + m, 0:n], win[:, k, f * 128:(f + 1) * 128], yT[:, k, c:c + n],
                                                        start=(k == 0), stop=(k == 1))
                            last.then_inc(hid_psum, 1)

                def feed(i, j):
                    b = i * CH + j
                    pe.wait_ge(hid_ready, i * NPROD + NPROD + 2)
                    pe.wait_ge(ff_taken, b + (2 if j == 0 else 1))
                    for f in range(FF // 128):
                        last = nc.tensor.matmul(ps[0:P, 4 + j % 2, 0:D], gT[:, f, j * P:(j + 1) * P], wout[:, f, :],
                                                start=(f == 0), stop=(f == FF // 128 - 1))
                    last.then_inc(ff_psum, 1)

                def turn(i, j, last):
                    b = i * CH + j
                    pe.wait_ge(h1_ready, b + 1)
                    for k in range(2):
                        nc.tensor.transpose(ps[:, j % 2, k * P:k * P + P], h1s[:, j, k * 128:k * 128 + 128],
                                            ident[0:P, 0:P]).then_inc(h1t_psum, 1)
                    if not last:
                        turn_y(i + 1, j)

                def messages(i, j, last):
                    b = i * CH + j
                    pe.wait_ge(h1T_ready, b + 1)
                    for c in range(4):
                        pe.wait_ge(msg_a if c < 2 else msg_v, 2 * b + c % 2 + 1)
                        for k in range(2):
                            prod = nc.tensor.matmul(ps[0:P, (2, 3, 6, 7)[c], :], h1T[:, j % 2, k, :],
                                                    wrel[:, k, c * 512:(c + 1) * 512], start=(k == 0), stop=(k == 1))
                        prod.then_inc(msg_psum, 1)
                    if not last:
                        pe.wait_ge(yT_ready, 2 * (b + CH) + 2)

                def chunk(i, last):
                    hidden(i)
                    for j in range(CH + 2):
                        if j >= 2:
                            turn(i, j - 2, last)
                        if j < CH:
                            feed(i, j)
                        if j >= 2:
                            messages(i, j - 2, last)

                pe.wait_ge(s_w2, 16 * 8)
                for j in range(CH):
                    if j >= 2:
                        pe.wait_ge(yT_ready, 2 * j - 2)
                    turn_y(0, j)
                with pe.Fori(0, NCH - 1) as i:
                    chunk(i, False)
                chunk(NCH - 1, True)

            @block.vector
            def _(dve):
                own = Steps(dve, sem("mid_dve"))
                dve.sem_inc(ff_taken, 2)
                dve.sem_inc(t_psum, 1)
                dve.sem_inc(msg_v, 2)
                dve.sem_inc(msg_stored, 2)
                def prepare(i):
                    dve.wait_ge(att_in, 16 * i + 16)
                    s_c = sums[:, bass.ds(i * CH, CH), :]
                    own.did(nc.vector.tensor_scalar(rec, s_c[:, :, D:AW], TINY, None, ALU.max))
                    own.wait()
                    own.did(nc.vector.reciprocal(rec, rec))
                    own.wait()
                    for j in range(CH):
                        s_j = sums[:, bass.ds(i * CH + j, 1), 0:D].rearrange("p o (h d) -> p (o h) d", d=DH)
                        own.did(nc.vector.tensor_tensor(s_j, s_j, rec[:, j, :].unsqueeze(2).broadcast_to([P, H, DH]), ALU.mult))
                    own.wait()
                    for j in range(CH):
                        s_j = sums[:, bass.ds(i * CH + j, 1), 0:D].rearrange("p o d -> p (o d)")
                        h_j = hs[:, bass.ds((i * CH + j) * D, D)]
                        nc.vector.tensor_tensor(h_j, h_j, s_j, ALU.add).then_inc(x1_ready, 1)
                    for j in range(CH):
                        dve.wait_ge(x1_ready, i * CH + j + 1)
                        dve.nop(nofuse=True)
                        own.did(nc.vector.bn_stats(st6[:, j, :], hs[:, bass.ds((i * CH + j) * D, D)]))
                    own.wait()
                    dve.nop(nofuse=True)
                    for j in range(CH):
                        own.did(nc.vector.bn_aggr(mv[:, j, :], st6[:, j, :]))
                    own.wait()
                    own.did(nc.vector.tensor_scalar(vv[:, 0, :], mv[:, :, 1], EPS, None, ALU.add))
                    own.wait()
                    rsqrt(own, vv[:, 0, :], rs[:, :], vv[:, 1, :])
                    dve.wait_ge(t_psum, 2 * CH * i + 1)
                    for j in range(CH):
                        nc.vector.tensor_scalar(yn[:, j, :], hs[:, bass.ds((i * CH + j) * D, D)], mv[:, j, 0:1], rs[:, j:j + 1],
                                                ALU.subtract, ALU.mult).then_inc(yn_ready, 1)

                def finish(i):
                    for j in range(CH + 2):
                        b = i * CH + j
                        if j < CH:
                            x_b = xs[:, bass.ds(b * D, D)]
                            dve.wait_ge(ff_psum, b + 1)
                            dve.wait_ge(x_ready, b + 1)
                            nc.vector.tensor_tensor(x_b, x_b, ps[0:P, 4 + j % 2, 0:D], ALU.add).then_inc(ff_taken, 1)
                            dve.wait_ge(ff_taken, b + 3)
                            dve.nop(nofuse=True)
                            own.did(nc.vector.bn_stats(st6b[:, j, :], x_b))
                            own.wait()
                            dve.nop(nofuse=True)
                            own.did(nc.vector.bn_aggr(mvb[:, j, :], st6b[:, j, :]))
                            own.wait()
                            own.did(nc.vector.tensor_scalar(vv[:, 2, j:j + 1], mvb[:, j, 1:2], EPS, None, ALU.add))
                            own.wait()
                            rsqrt(own, vv[:, 2, j:j + 1], rsb[:, j:j + 1], vv[:, 3, j:j + 1])
                            nc.vector.scalar_tensor_tensor(out=nmb[:, j:j + 1], in0=mvb[:, j, 0:1], scalar=-1.0, in1=rsb[:, j:j + 1],
                                                           op0=ALU.mult, op1=ALU.mult).then_inc(st_ready, 1)
                        if j >= 2:
                            dve.wait_ge(msg_stored, b - 2 + (2 if j == 2 else 1))
                            for c in range(2, 4):
                                dve.wait_ge(msg_psum, 4 * (b - 2) + c + 1)
                                nc.vector.tensor_copy(msg[:, j % 2, c * 512:(c + 1) * 512],
                                                      ps[0:P, 4 + c, :]).then_inc(msg_v, 1)

                prepare(0)
                with dve.Fori(0, NCH - 1) as i:
                    own.loop(i, MID_STEPS)
                    prepare(i + 1)
                    finish(i)
                own.end(NCH - 1)
                finish(NCH - 1)

        with nc.Block() as block:
            cut = carve()
            hz = cut([NBLK * D], parts=P)
            h1c = cut([D], parts=P)
            h1T = cut([2, P])
            hzt = cut([D], parts=P)
            blk = cut([1, VMAX // 2], I32)
            rowbuf = cut([2 * T, D], parts=P)
            ind = cut([2, T, WIN], parts=P)
            dl = cut([2, T], parts=P)
            car = cut([2, WIN])
            osum = cut([2, D])
            idx = cut([2, T], I32, parts=P)
            row_in = [sem(f"messages_in{j}") for j in range(2 * PAIRS)]
            dl_ready, ind_ready, car_ready, agg_done = sem("dl_ready"), sem("ind1_ready"), sem("car1_ready"), sem("summed1")
            win_done, osum_ready = sem("window1_done"), sem("osum1_ready")
            rel_out, rel_stored, idx_ready, zeros = sem("rel_out"), sem("rel_stored"), sem("idx1_ready"), sem("zeros1_ready")
            h1c_ready, h1t_psum, h1T_ready = sem("h1_copied"), sem("h1_turned1"), sem("h1T1_ready")
            loop_psum, loop_taken, blk_ready = sem("loop_psum"), sem("loop_taken"), sem("blocks_ready")

            @block.sync
            def _(sp):
                nt = trip_count(sp)
                sp.sem_inc(rel_stored, 1)
                sp.wait_ge(zeros, 1)
                sp.dma_start(rel[0:WIN, :], osum[:, 1, :]).then_inc(rel_out, 16)
                with sp.Fori(0, nt) as i:
                    for u in range(2):
                        v = 2 * i + u
                        sp.wait_ge(osum_ready, v + 3)
                        sp.nop(nofuse=True)
                        sp.wait_ge(rel_out, 16 * (v + 1))
                        sp.nop(nofuse=True)
                        sp.sem_inc(rel_stored, 1)
                        w = sp.value_load(wof[0:1, bass.ds(v + 1, 1)], min_val=0, max_val=NWIN * WIN)
                        sp.dma_start(rel[bass.ds(w, WIN), :], osum[:, u, :]).then_inc(rel_out, 16)
                sp.wait_ge(rel_out, 32 * nt + 16)
                sp.nop(nofuse=True)

            @block.gpsimd
            def _(pool):
                nt = trip_count(pool)
                nc.gpsimd.iota(blk, pattern=[[1, VMAX // 2]], base=0, channel_multiplier=0).then_inc(blk_ready, 1)

                with pool.Fori(0, nt) as i:
                    for u in range(2):
                        v = 2 * i + u
                        pool.wait_ge(idx_ready, v + 1)
                        for t in range(T):
                            if t % 2 == 0:
                                pool.wait_ge(agg_done, 4 * v + t // 2 + 1)
                                pool.nop(nofuse=True)
                            pool.indirect_dma_start(
                                out=rowbuf[:, u * T + t, :], out_offset=None, in_=h_all,
                                in_offset=bass.IndirectOffsetOnAxis(ap=idx[:, u, t:t + 1], axis=0)
                            ).then_inc(row_in[u * PAIRS + t // 2], 16)

            @block.scalar
            def _(act):
                nt = trip_count(act)
                act.sem_inc(osum_ready, 2)
                with act.Fori(0, nt) as i:
                    act.wait_ge(h1t_psum, 2 * i + 2)
                    nc.scalar.activation(h1T, ps[:, 0, 0:2 * P].rearrange("p (k n) -> p k n", k=2),
                                         ACT.Copy).then_inc(h1T_ready, 1)
                    for u in range(2):
                        v = 2 * i + u
                        act.wait_ge(win_done, v + 1)
                        act.wait_ge(rel_stored, v + 1)
                        nc.scalar.activation(osum[:, u, :], ps[:, 6 + u, 0:D], ACT.Copy).then_inc(osum_ready, 1)

            @block.tensor
            def _(pe):
                nt = trip_count(pe)
                pe.sem_inc(agg_done, 8)
                pe.wait_ge(zeros, 1)
                with pe.Fori(0, nt) as i:
                    pe.wait_ge(h1c_ready, i + 1)
                    for k in range(2):
                        nc.tensor.transpose(ps[:, 0, k * P:k * P + P], h1c[:, k * 128:k * 128 + 128],
                                            ident[0:P, 0:P]).then_inc(h1t_psum, 1)
                    for u in range(2):
                        v = 2 * i + u
                        if u == 1:
                            pe.wait_ge(h1T_ready, i + 1)
                            pe.wait_ge(loop_taken, i + 1)
                            for k in range(2):
                                last = nc.tensor.matmul(ps[0:P, 1, 0:D], h1T[:, k, :], wloop[:, k, :],
                                                        start=(k == 0), stop=(k == 1))
                            last.then_inc(loop_psum, 1)
                        pe.wait_ge(ind_ready, v + 1)
                        pe.wait_ge(osum_ready, v + 1)
                        for t in range(T):
                            if t % 2 == 0:
                                pe.wait_ge(row_in[u * PAIRS + t // 2], 32 * i + 32)
                            last = nc.tensor.matmul(ps[:, 6 + u, 0:D], ind[:, u, t, :], rowbuf[:, u * T + t, :],
                                                    start=(t == 0), stop=False)
                            if t % 2:
                                last.then_inc(agg_done, 1)
                        pe.wait_ge(osum_ready, v + 2)
                        pe.wait_ge(car_ready, v + 1)
                        nc.tensor.matmul(ps[:, 6 + u, 0:D], car[:, u, :], osum[:, 1 - u, :], start=False, stop=True).then_inc(win_done, 1)

            @block.vector
            def _(dve):
                nt = trip_count(dve)
                own = Steps(dve, sem("edge1_dve"))

                def indices(v, u):
                    g = dve.value_load(gof[0:1, bass.ds(v, 1)], min_val=0, max_val=G - 1)
                    nc.vector.tensor_copy(idx[:, u, :], typs[:, bass.ds(g * T, T)]).then_inc(idx_ready, 1)

                indices(0, 0)
                own.did(nc.vector.memset(osum, 0.0))
                own.wait()
                dve.sem_inc(zeros, 1)
                dve.wait_ge(blk_ready, 1)
                nc.vector.tensor_scalar(blk, blk, float(NBLK - 1), None, ALU.min).then_inc(blk_ready, 1)
                dve.wait_ge(blk_ready, 2)
                dve.sem_inc(loop_taken, 1)
                with dve.Fori(0, nt) as i:
                    own.loop(i, 1)
                    b = dve.value_load(blk[0:1, 0, bass.ds(i, 1)], min_val=0, max_val=NBLK - 1)
                    dve.wait_ge(loop_taken, i + 1)
                    nc.vector.tensor_copy(h1c, hs[:, bass.ds(b * D, D)]).then_inc(h1c_ready, 1)
                    for u in range(2):
                        v = 2 * i + u
                        g = dve.value_load(gof[0:1, bass.ds(v, 1)], min_val=0, max_val=G - 1)
                        dve.wait_ge(agg_done, 4 * v + 4)
                        dve.wait_ge(osum_ready, v + 1)
                        nc.vector.tensor_scalar(dl[:, u, :], dstf[:, bass.ds(g * T, T)], wst[0:P, bass.ds(v, 1)], None,
                                                ALU.subtract).then_inc(dl_ready, 1)
                        nc.vector.tensor_scalar(car[:, u, :], iotaj[:, :], wcar[:, bass.ds(v, 1)], None,
                                                ALU.is_equal).then_inc(car_ready, 1)
                        dve.wait_ge(dl_ready, v + 1)
                        for t in range(T):
                            last = nc.vector.tensor_scalar(ind[:, u, t, :], iotaj[0:P, :], dl[:, u, t:t + 1], None, ALU.is_equal)
                        last.then_inc(ind_ready, 1)
                        dve.wait_ge(agg_done, 4 * v + 8)
                        indices(v + 1, 1 - u)
                    dve.wait_ge(loop_psum, i + 1)
                    own.did(nc.vector.tensor_tensor(hzt, ps[0:P, 1, 0:D], rowb[:, 1, :], ALU.add))
                    own.wait()
                    nc.vector.tensor_tensor(hz[:, bass.ds(b * D, D)], h1c, hzt, ALU.add).then_inc(loop_taken, 1)

        with nc.Block() as block:
            cut = carve()
            hz = cut([NBLK * D], parts=P)
            z = cut([NBLK * D], parts=P)
            zst = cut([NBLK, 6], parts=P)
            zmv = cut([NBLK, 2], parts=P)
            vv = cut([4, NBLK], parts=P)
            rel_in = [sem("first_rel_in"), sem("rel_in")]
            z_ready, g_ready, m_ready, n_ready = (sem(n) for n in ("z_ready", "gelu_ready", "moments_ready", "normed_ready"))
            s_ready, o_dve, o_pool, out_sem = (sem(n) for n in ("scaled_ready", "result_by_dve", "result_by_pool", "result_out"))
            BY_DVE = (1, 3)

            def block_of(t, i, j):
                return t[:, bass.ds((i * CH + j) * D, D)]

            @block.sync
            def _(sp):
                for n, (c, e) in enumerate(((0, CH), (CH, NBLK))):
                    sp.dma_start(z[:, c * D:e * D].rearrange("p (b d) -> p b d", d=D),
                                 rel[c * P:e * P, :].rearrange("(b p) d -> p b d", p=P)).then_inc(rel_in[n], 16)
                with sp.Fori(0, NCH) as i:
                    for j in range(CH):
                        by_dve = j in BY_DVE
                        sp.wait_ge(o_dve if by_dve else o_pool,
                                   i * (len(BY_DVE) if by_dve else CH - len(BY_DVE)) + j // 2 + 1)
                        sp.nop(nofuse=True)
                        sp.dma_start(out[bass.ds((i * CH + j) * P, P), :], block_of(z, i, j)).then_inc(out_sem, 16)
                sp.wait_ge(out_sem, 16 * NBLK)

            @block.gpsimd
            def _(pool):
                with pool.Fori(0, NCH) as i:
                    for j in range(CH):
                        if j not in BY_DVE:
                            pool.wait_ge(s_ready, i * CH + j + 1)
                            pool.nop(nofuse=True)
                            nc.gpsimd.tensor_tensor(block_of(z, i, j), block_of(z, i, j), block_of(xs, i, j),
                                                    ALU.add).then_inc(o_pool, 1)

            @block.scalar
            def _(act):
                with act.Fori(0, NCH) as i:
                    for j in range(CH):
                        act.wait_ge(z_ready, i * CH + j + 1)
                        nc.scalar.activation(block_of(z, i, j), block_of(z, i, j), ACT.Gelu).then_inc(g_ready, 1)
                act.wait_ge(m_ready, 1)
                with act.Fori(0, NCH) as i:
                    for j in range(CH):
                        b = i * CH + j
                        nc.scalar.activation(block_of(z, i, j), block_of(z, i, j), ACT.Identity,
                                             bias=vv[:, 3, bass.ds(b, 1)], scale=vv[:, 2, bass.ds(b, 1)]).then_inc(n_ready, 1)

            @block.vector
            def _(dve):
                own = Steps(dve, sem("last_dve"))

                def add(i):
                    for j in range(CH):
                        nc.vector.tensor_tensor(block_of(z, i, j), block_of(z, i, j), block_of(hz, i, j),
                                                ALU.add).then_inc(z_ready, 1)

                def stats(i):
                    for j in range(CH):
                        b = i * CH + j
                        dve.wait_ge(g_ready, b + 1)
                        dve.nop(nofuse=True)
                        own.did(nc.vector.bn_stats(zst[:, bass.ds(b, 1), :].rearrange("p o s -> p (o s)"), block_of(z, i, j)))

                dve.wait_ge(rel_in[0], 16)
                add(0)
                dve.wait_ge(rel_in[1], 16)
                with dve.Fori(0, NCH - 1) as i:
                    own.loop(i, CH)
                    add(i + 1)
                    stats(i)
                own.end(NCH - 1)
                stats(NCH - 1)
                own.wait()
                dve.nop(nofuse=True)
                for b in range(NBLK):
                    own.did(nc.vector.bn_aggr(zmv[:, b, :], zst[:, b, :]))
                own.wait()
                own.did(nc.vector.tensor_scalar(vv[:, 0, :], zmv[:, :, 1], EPS, None, ALU.add))
                own.wait()
                rsqrt(own, vv[:, 0, :], vv[:, 2, :], vv[:, 1, :])
                nc.vector.scalar_tensor_tensor(out=vv[:, 3, :], in0=zmv[:, :, 0], scalar=-1.0, in1=vv[:, 2, :],
                                               op0=ALU.mult, op1=ALU.mult).then_inc(m_ready, 1)
                with dve.Fori(0, NCH) as i:
                    for j in range(CH + 1):
                        if j < CH:
                            dve.wait_ge(n_ready, i * CH + j + 1)
                            nc.vector.tensor_tensor(block_of(z, i, j), block_of(z, i, j), rowb[:, 2, :], ALU.mult).then_inc(s_ready, 1)
                        if j - 1 in BY_DVE:
                            dve.wait_ge(s_ready, i * CH + j)
                            nc.vector.tensor_tensor(block_of(z, i, j - 1), block_of(z, i, j - 1), block_of(xs, i, j - 1),
                                                    ALU.add).then_inc(o_dve, 1)


_INS = ['x', 'src', 'dst', 'edge_type_8', 'L0_gnn_Wqkv', 'L0_gnn_bqkv', 'L0_gnn_ln_attn_g', 'L0_gnn_ln_attn_b',
        'L0_gnn_ln_res_g', 'L0_gnn_ln_res_b', 'L0_gnn_W_in', 'L0_gnn_b_in', 'L0_gnn_W_out', 'L0_gnn_b_out',
        'L1_gnn_basis', 'L1_gnn_comp', 'L1_gnn_loop_w', 'L1_gnn_h_bias', 'L1_gnn_ln_gamma', 'L1_gnn_ln_beta']


def kernel(**inputs):
    import numpy as _np
    import concourse.bacc as _bacc
    from concourse import mybir as _mybir
    from concourse.bass_utils import run_bass_kernel_spmd as _run

    nc = _bacc.Bacc("TRN2", target_bir_lowering=False, num_devices=1)
    arrays, args = {}, []
    for name in _INS:
        a = _np.ascontiguousarray(inputs[name])
        arrays[f"in_{name}"] = a
        args.append(nc.dram_tensor(f"in_{name}", a.shape, _mybir.dt.from_np(a.dtype), kind="ExternalInput").ap())
    o = nc.dram_tensor("out", (N, D), _mybir.dt.float32, kind="ExternalOutput").ap()
    program(nc, *args, o)
    r = _run(nc, [arrays], core_ids=[0])
    return r.results[0]["out"]
```
